# Optimizing a Trainium2 kernel written in Bass

```python
import numpy as np
import jax
import jax.numpy as jnp

def _softmax(x, axis=-1):
    return jax.nn.softmax(x, axis=axis)

def _gelu(x):
    return jax.nn.gelu(x, approximate=True)

def _silu(x):
    return jax.nn.silu(x)

def _sigmoid(x):
    return jax.nn.sigmoid(x)

def _layernorm(x, axis=-1, eps=1e-05):
    m = jnp.mean(x, axis=axis, keepdims=True)
    v = jnp.var(x, axis=axis, keepdims=True)
    return (x - m) / jnp.sqrt(v + eps)

def _scatter_add(tgt, idx, src, axis=0):
    return tgt.at[idx].add(src)

def _segment_sum(src, seg, n):
    return jax.ops.segment_sum(src, seg, n)
kernel_name = 'mk_decoder_preln_d2_seqx_r4_5d542e'

def setup_inputs(seed: int=0):
    np.random.seed(seed)
    _w = jnp.asarray

    def _rec_inputs():
        import jax
        import jax.numpy as jnp
        _rk = jax.random.key(seed)
        x = -0.0005146 + 1 * jax.random.normal(jax.random.fold_in(_rk, 1), (8, 112, 256), jnp.float32)
        _lenS = 112 - jax.random.randint(jax.random.fold_in(_rk, 7), (8,), 0, max(1, 112 // 4) + 1, jnp.int32)
        _lenS2 = 375 - jax.random.randint(jax.random.fold_in(_rk, 8), (8,), 0, max(1, 375 // 4) + 1, jnp.int32)
        _ctx_1024P = jax.random.normal(jax.random.fold_in(_rk, 11), (8, 16, 256), jnp.float32)
        _ctx_1024c = jax.random.dirichlet(jax.random.fold_in(_rk, 511), 0.3 * jnp.ones((16,), jnp.float32), (8, 375))
        _ctx_1024t = jnp.einsum('bsk,bkd->bsd', _ctx_1024c, _ctx_1024P)
        _ctx_1024t = _ctx_1024t * jax.lax.rsqrt(jnp.mean(jnp.square(_ctx_1024t)) + 1e-12) * 0.953939
        ctx_1024 = -0.000392918 + 0.999932 * (_ctx_1024t + 0.3 * jax.random.normal(jax.random.fold_in(_rk, 611), (8, 375, 256), jnp.float32))
        _validS = jnp.arange(112)[None, :] < _lenS[:, None]
        _validS2 = jnp.arange(375)[None, :] < _lenS2[:, None]
        _causal = jnp.tril(jnp.ones((112, 112), dtype=bool))
        mask_BxS2_bf1 = jnp.ones((8, 375), dtype=bool)
        mask_SxS2_if1 = jnp.where(jnp.ones((112, 375), dtype=bool), 1, 0).astype(jnp.int32)
        return (x, ctx_1024, mask_BxS2_bf1, mask_SxS2_if1)
    x, ctx_1024, mask_BxS2_bf1, mask_SxS2_if1 = _rec_inputs()

    def _L0_attn_setup():
        import jax, jax.numpy as jnp
        import numpy as np
        NUM_HEADS = 16
        DIM_HEAD = 64
        SCALE = DIM_HEAD ** (-0.5)
        ROPE_BASE = 10000.0

        def _rope(t):
            n, d = (t.shape[2], t.shape[3])
            inv_freq = 1.0 / ROPE_BASE ** (jnp.arange(0, d, 2, dtype=jnp.float32) / d)
            freqs = jnp.arange(n, dtype=jnp.float32)[:, None] * inv_freq[None, :]
            cos = jnp.concatenate([jnp.cos(freqs), jnp.cos(freqs)], axis=-1)
            sin = jnp.concatenate([jnp.sin(freqs), jnp.sin(freqs)], axis=-1)
            t1, t2 = jnp.split(t, 2, axis=-1)
            rot = jnp.concatenate([-t2, t1], axis=-1)
            return t * cos + rot * sin
        key = jax.random.key(seed)
        k1, k2, k3 = jax.random.split(key, 3)
        B, N, D = (2, 2049, 256)
        x = jax.random.normal(k1, (B, N, D), dtype=jnp.float32)
        ln_gamma = jnp.ones((D,), dtype=jnp.float32)
        ln_beta = jnp.zeros((D,), dtype=jnp.float32)
        w_qkv = jax.random.normal(k2, (D, 3 * NUM_HEADS * DIM_HEAD), dtype=jnp.float32) * 0.02
        w_out = jax.random.normal(k3, (NUM_HEADS * DIM_HEAD, D), dtype=jnp.float32) * 0.02
        return {'x': x, 'ln_gamma': ln_gamma, 'ln_beta': ln_beta, 'w_qkv': w_qkv, 'w_out': w_out}
    _L0_attn_all = _L0_attn_setup()
    _L0_attn_in = {k: v for k, v in _L0_attn_all.items() if k in ('ln_gamma', 'ln_beta', 'w_qkv', 'w_out')}
    del _L0_attn_all

    def _L0_xattn_setup():
        import jax, jax.numpy as jnp
        import numpy as np
        DIM = 256
        DIM_LATENT = 256
        DIM_HEAD = 64
        HEADS = 16
        INNER = HEADS * DIM_HEAD

        def layernorm(x, g, b, eps=1e-05):
            m = jnp.mean(x, axis=-1, keepdims=True)
            v = jnp.mean((x - m) ** 2, axis=-1, keepdims=True)
            return (x - m) / jnp.sqrt(v + eps) * g + b

        def rmsnorm(x, gamma, eps=1e-08):
            n = jnp.linalg.norm(x, axis=-1, keepdims=True) * x.shape[-1] ** (-0.5)
            return x / jnp.maximum(n, eps) * gamma
        key = jax.random.key(seed)
        ks = jax.random.split(key, 8)
        b, n, m = (4, 1024, 128)
        x = jax.random.normal(ks[0], (b, n, DIM), dtype=jnp.float32)
        latents = jax.random.normal(ks[1], (b, m, DIM_LATENT), dtype=jnp.float32)
        mask = jnp.ones((b, n), dtype=bool)
        s = 0.02
        return {'x': x, 'latents': latents, 'mask': mask, 'ln_x_g': jnp.ones((DIM,), jnp.float32), 'ln_x_b': jnp.zeros((DIM,), jnp.float32), 'ln_l_g': jnp.ones((DIM_LATENT,), jnp.float32), 'ln_l_b': jnp.zeros((DIM_LATENT,), jnp.float32), 'qn_g': jnp.ones((DIM_HEAD,), jnp.float32), 'kn_g': jnp.ones((DIM_HEAD,), jnp.float32), 'Wq': jax.random.normal(ks[2], (DIM_LATENT, INNER), jnp.float32) * s, 'Wkv': jax.random.normal(ks[3], (DIM, 2 * INNER), jnp.float32) * s, 'Wout': jax.random.normal(ks[4], (INNER, DIM_LATENT), jnp.float32) * s, 'bout': jnp.zeros((DIM_LATENT,), jnp.float32)}
    _L0_xattn_all = _L0_xattn_setup()
    _L0_xattn_in = {k: v for k, v in _L0_xattn_all.items() if k in ('ln_x_g', 'ln_x_b', 'ln_l_g', 'ln_l_b', 'qn_g', 'kn_g', 'Wq', 'Wkv', 'Wout', 'bout')}
    del _L0_xattn_all

    def _L0_ffn_setup():
        import jax, jax.numpy as jnp
        import numpy as np
        D_MODEL = 256
        D1, D2 = (32, 32)
        F1, F2 = (64, 64)
        E = 64
        TOP_K = 2

        def kmoe(x_flat, W_router, A, B, scale, bias, d_in1, d_in2, d_out1, d_out2, top_k):
            logits = x_flat @ W_router.T
            vals, idx = jax.lax.top_k(logits, top_k)
            probs = jax.nn.softmax(vals, axis=-1)
            xs = x_flat.reshape(-1, d_in1, d_in2)
            Ag = A[idx]
            Bg = B[idx]
            Y = jnp.einsum('nkoi,nij,nkpj->nkop', Ag, xs, Bg)
            out = jnp.einsum('nkop,nk->nop', Y, probs).reshape(-1, d_out1 * d_out2)
            return out * scale + bias
        key = jax.random.key(seed)
        ks = jax.random.split(key, 12)
        s = 0.02
        return {'x': jax.random.normal(ks[0], (4, 512, D_MODEL), dtype=jnp.float32), 'W_up': jax.random.normal(ks[1], (E, D1 * D2), dtype=jnp.float32) * s, 'A_up': jax.random.normal(ks[2], (E, F1, D1), dtype=jnp.float32) * s, 'B_up': jax.random.normal(ks[3], (E, F2, D2), dtype=jnp.float32) * s, 'scale_up': jnp.ones((1,), dtype=jnp.float32), 'bias_up': jnp.zeros((F1 * F2,), dtype=jnp.float32), 'W_down': jax.random.normal(ks[4], (E, F1 * F2), dtype=jnp.float32) * s, 'A_down': jax.random.normal(ks[5], (E, D1, F1), dtype=jnp.float32) * s, 'B_down': jax.random.normal(ks[6], (E, D2, F2), dtype=jnp.float32) * s, 'scale_down': jnp.ones((1,), dtype=jnp.float32), 'bias_down': jnp.zeros((D1 * D2,), dtype=jnp.float32)}
    _L0_ffn_all = _L0_ffn_setup()
    _L0_ffn_in = {k: v for k, v in _L0_ffn_all.items() if k in ('W_up', 'A_up', 'B_up', 'scale_up', 'bias_up', 'W_down', 'A_down', 'B_down', 'scale_down', 'bias_down')}
    del _L0_ffn_all

    def _L1_attn_setup():
        import jax, jax.numpy as jnp
        import numpy as np
        EMBED_DIM = 256
        NUM_HEADS = 16
        HEAD_DIM = EMBED_DIM // NUM_HEADS
        key = jax.random.key(seed)
        k1, k2, k3 = jax.random.split(key, 3)
        inputs = jax.random.normal(k1, (4, 512, EMBED_DIM), dtype=jnp.float32)
        rotation_params = jax.random.normal(k2, (NUM_HEADS, HEAD_DIM), dtype=jnp.float32)
        entangle_params = jax.random.normal(k3, (NUM_HEADS, HEAD_DIM), dtype=jnp.float32)
        return {'inputs': inputs, 'rotation_params': rotation_params, 'entangle_params': entangle_params}
    _L1_attn_all = _L1_attn_setup()
    _L1_attn_in = {k: v for k, v in _L1_attn_all.items() if k in ('rotation_params', 'entangle_params')}
    del _L1_attn_all

    def _L1_xattn_setup():
        import jax, jax.numpy as jnp
        import numpy as np
        import math
        B, S, D, H = (2, 512, 256, 16)
        K = D // H
        key0 = jax.random.key(seed)
        ks = jax.random.split(key0, 12)
        w = 0.02
        return {'query': jax.random.normal(ks[0], (B, S, D), jnp.float32), 'key': jax.random.normal(ks[1], (B, S, D), jnp.float32), 'value': jax.random.normal(ks[2], (B, S, D), jnp.float32), 'mask': jnp.ones((S, S), jnp.int32), 'Wq': jax.random.normal(ks[3], (H, K, D), jnp.float32) * w, 'bq': jax.random.normal(ks[4], (H, K), jnp.float32) * w, 'Wk': jax.random.normal(ks[5], (H, K, D), jnp.float32) * w, 'bk': jax.random.normal(ks[6], (H, K), jnp.float32) * w, 'Wv': jax.random.normal(ks[7], (H, K, D), jnp.float32) * w, 'bv': jax.random.normal(ks[8], (H, K), jnp.float32) * w, 'Wo': jax.random.normal(ks[9], (D, D), jnp.float32) * w, 'bo': jax.random.normal(ks[10], (D,), jnp.float32) * w}
    _L1_xattn_all = _L1_xattn_setup()
    _L1_xattn_in = {k: v for k, v in _L1_xattn_all.items() if k in ('Wq', 'bq', 'Wk', 'bk', 'Wv', 'bv', 'Wo', 'bo')}
    del _L1_xattn_all

    def _L1_ffn_setup():
        import jax, jax.numpy as jnp
        import numpy as np
        D = 256
        H = 4
        HD = D // H
        E = 8
        FF = 1024
        CAP_FACTOR = 1.0

        def _ln(x, g, b, eps=1e-05):
            mu = jnp.mean(x, -1, keepdims=True)
            v = jnp.mean((x - mu) ** 2, -1, keepdims=True)
            return (x - mu) * jax.lax.rsqrt(v + eps) * g + b

        def _mha(x, w, b, ow, ob):
            L, N, _ = x.shape
            qkv = x @ w.T + b
            q, k, v = jnp.split(qkv, 3, axis=-1)
            rh = lambda t: t.reshape(L, N, H, HD).transpose(1, 2, 0, 3)
            q, k, v = (rh(q), rh(k), rh(v))
            scores = jnp.einsum('nhld,nhmd->nhlm', q, k) / np.float32(np.sqrt(HD))
            attn = jax.nn.softmax(scores, axis=-1)
            o = jnp.einsum('nhlm,nhmd->nhld', attn, v).transpose(2, 0, 1, 3).reshape(L, N, D)
            return o @ ow.T + ob

        def _moe(x, wg, w1, b1, w2, b2):
            L, N, _ = x.shape
            S = L * N
            cap = int(CAP_FACTOR * S) // E
            xf = x.reshape(S, D)
            gates = jax.nn.softmax(xf @ wg, axis=-1)
            idx = jnp.argmax(gates, axis=-1)
            mask1 = jax.nn.one_hot(idx, E, dtype=x.dtype)
            loc = jnp.sum((jnp.cumsum(mask1, 0) - 1.0) * mask1, -1).astype(jnp.int32)
            keep = loc < cap
            gate_val = jnp.take_along_axis(gates, idx[:, None], -1)[:, 0]
            slot = jnp.where(keep, idx.astype(jnp.int32) * cap + loc, E * cap)
            disp = jnp.zeros((E * cap, D), x.dtype).at[slot].set(xf, mode='drop')
            disp = disp.reshape(E, cap, D)
            h = jnp.einsum('ecd,edf->ecf', disp, w1) + b1[:, None, :]
            y = (jnp.einsum('ecf,efd->ecd', h, w2) + b2[:, None, :]).reshape(E * cap, D)
            out = jnp.where(keep[:, None], gate_val[:, None] * y[jnp.minimum(slot, E * cap - 1)], 0.0)
            return out.reshape(L, N, D)
        key = jax.random.key(seed)
        ks = jax.random.split(key, 8)
        L, N = (256, 16)
        s = 0.02
        return {'x': jax.random.normal(ks[0], (L, N, D), jnp.float32), 'in_proj_w': jax.random.normal(ks[1], (3 * D, D), jnp.float32) * s, 'in_proj_b': jnp.zeros((3 * D,), jnp.float32), 'out_proj_w': jax.random.normal(ks[2], (D, D), jnp.float32) * s, 'out_proj_b': jnp.zeros((D,), jnp.float32), 'ln1_g': jnp.ones((D,), jnp.float32), 'ln1_b': jnp.zeros((D,), jnp.float32), 'ln2_g': jnp.ones((D,), jnp.float32), 'ln2_b': jnp.zeros((D,), jnp.float32), 'wg': jax.random.normal(ks[3], (D, E), jnp.float32) * s, 'w1': jax.random.normal(ks[4], (E, D, FF), jnp.float32) * s, 'b1': jnp.zeros((E, FF), jnp.float32), 'w2': jax.random.normal(ks[5], (E, FF, D), jnp.float32) * s, 'b2': jnp.zeros((E, D), jnp.float32)}
    _L1_ffn_all = _L1_ffn_setup()
    _L1_ffn_in = {k: v for k, v in _L1_ffn_all.items() if k in ('in_proj_w', 'in_proj_b', 'out_proj_w', 'out_proj_b', 'ln1_g', 'ln1_b', 'ln2_g', 'ln2_b', 'wg', 'w1', 'b1', 'w2', 'b2')}
    del _L1_ffn_all
    return {'x': x, 'ctx_1024': ctx_1024, 'mask_BxS2_bf1': mask_BxS2_bf1, 'mask_SxS2_if1': mask_SxS2_if1, 'L0_attn_ln_gamma': _L0_attn_in['ln_gamma'], 'L0_attn_ln_beta': _L0_attn_in['ln_beta'], 'L0_attn_w_qkv': _L0_attn_in['w_qkv'], 'L0_attn_w_out': _L0_attn_in['w_out'], 'L0_xattn_ln_x_g': _L0_xattn_in['ln_x_g'], 'L0_xattn_ln_x_b': _L0_xattn_in['ln_x_b'], 'L0_xattn_ln_l_g': _L0_xattn_in['ln_l_g'], 'L0_xattn_ln_l_b': _L0_xattn_in['ln_l_b'], 'L0_xattn_qn_g': _L0_xattn_in['qn_g'], 'L0_xattn_kn_g': _L0_xattn_in['kn_g'], 'L0_xattn_Wq': _L0_xattn_in['Wq'], 'L0_xattn_Wkv': _L0_xattn_in['Wkv'], 'L0_xattn_Wout': _L0_xattn_in['Wout'], 'L0_xattn_bout': _L0_xattn_in['bout'], 'L0_ffn_W_up': _L0_ffn_in['W_up'], 'L0_ffn_A_up': _L0_ffn_in['A_up'], 'L0_ffn_B_up': _L0_ffn_in['B_up'], 'L0_ffn_scale_up': _L0_ffn_in['scale_up'], 'L0_ffn_bias_up': _L0_ffn_in['bias_up'], 'L0_ffn_W_down': _L0_ffn_in['W_down'], 'L0_ffn_A_down': _L0_ffn_in['A_down'], 'L0_ffn_B_down': _L0_ffn_in['B_down'], 'L0_ffn_scale_down': _L0_ffn_in['scale_down'], 'L0_ffn_bias_down': _L0_ffn_in['bias_down'], 'L1_attn_rotation_params': _L1_attn_in['rotation_params'], 'L1_attn_entangle_params': _L1_attn_in['entangle_params'], 'L1_xattn_Wq': _L1_xattn_in['Wq'], 'L1_xattn_bq': _L1_xattn_in['bq'], 'L1_xattn_Wk': _L1_xattn_in['Wk'], 'L1_xattn_bk': _L1_xattn_in['bk'], 'L1_xattn_Wv': _L1_xattn_in['Wv'], 'L1_xattn_bv': _L1_xattn_in['bv'], 'L1_xattn_Wo': _L1_xattn_in['Wo'], 'L1_xattn_bo': _L1_xattn_in['bo'], 'L1_ffn_in_proj_w': _L1_ffn_in['in_proj_w'], 'L1_ffn_in_proj_b': _L1_ffn_in['in_proj_b'], 'L1_ffn_out_proj_w': _L1_ffn_in['out_proj_w'], 'L1_ffn_out_proj_b': _L1_ffn_in['out_proj_b'], 'L1_ffn_ln1_g': _L1_ffn_in['ln1_g'], 'L1_ffn_ln1_b': _L1_ffn_in['ln1_b'], 'L1_ffn_ln2_g': _L1_ffn_in['ln2_g'], 'L1_ffn_ln2_b': _L1_ffn_in['ln2_b'], 'L1_ffn_wg': _L1_ffn_in['wg'], 'L1_ffn_w1': _L1_ffn_in['w1'], 'L1_ffn_b1': _L1_ffn_in['b1'], 'L1_ffn_w2': _L1_ffn_in['w2'], 'L1_ffn_b2': _L1_ffn_in['b2']}

def reference(x, ctx_1024, mask_BxS2_bf1, mask_SxS2_if1, L0_attn_ln_gamma, L0_attn_ln_beta, L0_attn_w_qkv, L0_attn_w_out, L0_xattn_ln_x_g, L0_xattn_ln_x_b, L0_xattn_ln_l_g, L0_xattn_ln_l_b, L0_xattn_qn_g, L0_xattn_kn_g, L0_xattn_Wq, L0_xattn_Wkv, L0_xattn_Wout, L0_xattn_bout, L0_ffn_W_up, L0_ffn_A_up, L0_ffn_B_up, L0_ffn_scale_up, L0_ffn_bias_up, L0_ffn_W_down, L0_ffn_A_down, L0_ffn_B_down, L0_ffn_scale_down, L0_ffn_bias_down, L1_attn_rotation_params, L1_attn_entangle_params, L1_xattn_Wq, L1_xattn_bq, L1_xattn_Wk, L1_xattn_bk, L1_xattn_Wv, L1_xattn_bv, L1_xattn_Wo, L1_xattn_bo, L1_ffn_in_proj_w, L1_ffn_in_proj_b, L1_ffn_out_proj_w, L1_ffn_out_proj_b, L1_ffn_ln1_g, L1_ffn_ln1_b, L1_ffn_ln2_g, L1_ffn_ln2_b, L1_ffn_wg, L1_ffn_w1, L1_ffn_b1, L1_ffn_w2, L1_ffn_b2):
    import jax
    import jax.numpy as jnp

    def _L0_attn_ref(x, ln_gamma, ln_beta, w_qkv, w_out):
        import jax, jax.numpy as jnp
        import numpy as np
        NUM_HEADS = 16
        DIM_HEAD = 64
        SCALE = DIM_HEAD ** (-0.5)
        ROPE_BASE = 10000.0

        def _rope(t):
            n, d = (t.shape[2], t.shape[3])
            inv_freq = 1.0 / ROPE_BASE ** (jnp.arange(0, d, 2, dtype=jnp.float32) / d)
            freqs = jnp.arange(n, dtype=jnp.float32)[:, None] * inv_freq[None, :]
            cos = jnp.concatenate([jnp.cos(freqs), jnp.cos(freqs)], axis=-1)
            sin = jnp.concatenate([jnp.sin(freqs), jnp.sin(freqs)], axis=-1)
            t1, t2 = jnp.split(t, 2, axis=-1)
            rot = jnp.concatenate([-t2, t1], axis=-1)
            return t * cos + rot * sin
        B, N, D = x.shape
        mu = jnp.mean(x, axis=-1, keepdims=True)
        var = jnp.mean(jnp.square(x - mu), axis=-1, keepdims=True)
        xn = (x - mu) * jax.lax.rsqrt(var + 1e-05) * ln_gamma + ln_beta
        qkv = xn @ w_qkv
        q, k, v = jnp.split(qkv, 3, axis=-1)

        def to_heads(t):
            return t.reshape(B, N, NUM_HEADS, DIM_HEAD).transpose(0, 2, 1, 3)
        q, k, v = (to_heads(q), to_heads(k), to_heads(v))
        q = jnp.concatenate([q[:, :, :1, :], _rope(q[:, :, 1:, :])], axis=2)
        k = jnp.concatenate([k[:, :, :1, :], _rope(k[:, :, 1:, :])], axis=2)
        dots = jnp.einsum('bhqd,bhkd->bhqk', q, k) * SCALE
        attn = jax.nn.softmax(dots, axis=-1)
        out = jnp.einsum('bhqk,bhkd->bhqd', attn, v)
        out = out.transpose(0, 2, 1, 3).reshape(B, N, NUM_HEADS * DIM_HEAD)
        return out @ w_out

    def _L0_xattn_ref(x, latents, mask, ln_x_g, ln_x_b, ln_l_g, ln_l_b, qn_g, kn_g, Wq, Wkv, Wout, bout):
        import jax, jax.numpy as jnp
        import numpy as np
        DIM = 256
        DIM_LATENT = 256
        DIM_HEAD = 64
        HEADS = 16
        INNER = HEADS * DIM_HEAD

        def layernorm(x, g, b, eps=1e-05):
            m = jnp.mean(x, axis=-1, keepdims=True)
            v = jnp.mean((x - m) ** 2, axis=-1, keepdims=True)
            return (x - m) / jnp.sqrt(v + eps) * g + b

        def rmsnorm(x, gamma, eps=1e-08):
            n = jnp.linalg.norm(x, axis=-1, keepdims=True) * x.shape[-1] ** (-0.5)
            return x / jnp.maximum(n, eps) * gamma
        b, n, _ = x.shape
        m = latents.shape[1]
        h, d = (HEADS, DIM_HEAD)
        scale = d ** (-0.5)
        xn = layernorm(x, ln_x_g, ln_x_b)
        ln = layernorm(latents, ln_l_g, ln_l_b)
        q = (ln @ Wq).reshape(b, m, h, d).transpose(0, 2, 1, 3)
        kv = jnp.concatenate([xn @ Wkv, ln @ Wkv], axis=1)
        kv = kv.reshape(b, n + m, 2, h, d)
        k = kv[:, :, 0].transpose(0, 2, 1, 3)
        v = kv[:, :, 1].transpose(0, 2, 1, 3)
        qn = rmsnorm(q, qn_g) * scale
        kn = rmsnorm(k, kn_g)
        sim = jnp.einsum('bhid,bhjd->bhij', qn, kn)
        max_neg = -jnp.finfo(sim.dtype).max
        padded_mask = jnp.concatenate([mask, jnp.ones((b, m), bool)], axis=1)
        sim = jnp.where(padded_mask[:, None, None, :], sim, max_neg)
        attn = jax.nn.softmax(sim.astype(jnp.float32), axis=-1).astype(sim.dtype)
        out = jnp.einsum('bhij,bhjd->bhid', attn, v)
        out = out.transpose(0, 2, 1, 3).reshape(b, m, h * d)
        return out @ Wout + bout

    def _L0_ffn_ref(x, W_up, A_up, B_up, scale_up, bias_up, W_down, A_down, B_down, scale_down, bias_down):
        import jax, jax.numpy as jnp
        import numpy as np
        D_MODEL = 256
        D1, D2 = (32, 32)
        F1, F2 = (64, 64)
        E = 64
        TOP_K = 2

        def kmoe(x_flat, W_router, A, B, scale, bias, d_in1, d_in2, d_out1, d_out2, top_k):
            logits = x_flat @ W_router.T
            vals, idx = jax.lax.top_k(logits, top_k)
            probs = jax.nn.softmax(vals, axis=-1)
            xs = x_flat.reshape(-1, d_in1, d_in2)
            Ag = A[idx]
            Bg = B[idx]
            Y = jnp.einsum('nkoi,nij,nkpj->nkop', Ag, xs, Bg)
            out = jnp.einsum('nkop,nk->nop', Y, probs).reshape(-1, d_out1 * d_out2)
            return out * scale + bias
        orig_shape = x.shape
        x_flat = x.reshape(-1, D1 * D2)
        h = kmoe(x_flat, W_up, A_up, B_up, scale_up, bias_up, D1, D2, F1, F2, TOP_K)
        h = jax.nn.gelu(h, approximate=False)
        y = kmoe(h, W_down, A_down, B_down, scale_down, bias_down, F1, F2, D1, D2, TOP_K)
        return y.reshape(*orig_shape[:-1], D_MODEL)

    def _L1_attn_ref(inputs, rotation_params, entangle_params):
        import jax, jax.numpy as jnp
        import numpy as np
        EMBED_DIM = 256
        NUM_HEADS = 16
        HEAD_DIM = EMBED_DIM // NUM_HEADS
        B, T, _ = inputs.shape
        x = inputs.reshape(B, T, NUM_HEADS, HEAD_DIM).transpose(0, 2, 1, 3)
        q = x * rotation_params[None, :, None, :]
        k = x * entangle_params[None, :, None, :]
        v = x
        scale = 1.0 / np.sqrt(HEAD_DIM).astype(np.float32)
        attn_scores = jnp.einsum('bhid,bhjd->bhij', q, k) * scale
        attn_weights = jax.nn.softmax(attn_scores, axis=-1)
        out = jnp.einsum('bhij,bhjd->bhid', attn_weights, v)
        out = out.transpose(0, 2, 1, 3).reshape(B, T, EMBED_DIM)
        return out

    def _L1_xattn_ref(query, key, value, mask, Wq, bq, Wk, bk, Wv, bv, Wo, bo):
        import jax, jax.numpy as jnp
        import numpy as np
        import math
        B, S, D, H = (2, 512, 256, 16)
        K = D // H
        d_k = Wq.shape[1]
        q = jnp.einsum('bsd,hkd->bhsk', query, Wq) + bq[None, :, None, :]
        k = jnp.einsum('bsd,hkd->bhsk', key, Wk) + bk[None, :, None, :]
        v = jnp.einsum('bsd,hkd->bhsk', value, Wv) + bv[None, :, None, :]
        scores = jnp.einsum('bhsk,bhtk->bhst', q, k) / jnp.sqrt(jnp.asarray(d_k, q.dtype))
        attn = jax.nn.softmax(scores, axis=2)
        ctx = jnp.einsum('bhst,bhtk->bhsk', attn, v)
        b, h, s, dk = ctx.shape
        ctx = ctx.transpose(0, 2, 1, 3).reshape(b, s, h * dk)
        out = jnp.einsum('bsd,ed->bse', ctx, Wo) + bo
        return out

    def _L1_ffn_ref(x, in_proj_w, in_proj_b, out_proj_w, out_proj_b, ln1_g, ln1_b, ln2_g, ln2_b, wg, w1, b1, w2, b2):
        import jax, jax.numpy as jnp
        import numpy as np
        D = 256
        H = 4
        HD = D // H
        E = 8
        FF = 1024
        CAP_FACTOR = 1.0

        def _ln(x, g, b, eps=1e-05):
            mu = jnp.mean(x, -1, keepdims=True)
            v = jnp.mean((x - mu) ** 2, -1, keepdims=True)
            return (x - mu) * jax.lax.rsqrt(v + eps) * g + b

        def _mha(x, w, b, ow, ob):
            L, N, _ = x.shape
            qkv = x @ w.T + b
            q, k, v = jnp.split(qkv, 3, axis=-1)
            rh = lambda t: t.reshape(L, N, H, HD).transpose(1, 2, 0, 3)
            q, k, v = (rh(q), rh(k), rh(v))
            scores = jnp.einsum('nhld,nhmd->nhlm', q, k) / np.float32(np.sqrt(HD))
            attn = jax.nn.softmax(scores, axis=-1)
            o = jnp.einsum('nhlm,nhmd->nhld', attn, v).transpose(2, 0, 1, 3).reshape(L, N, D)
            return o @ ow.T + ob

        def _moe(x, wg, w1, b1, w2, b2):
            L, N, _ = x.shape
            S = L * N
            cap = int(CAP_FACTOR * S) // E
            xf = x.reshape(S, D)
            gates = jax.nn.softmax(xf @ wg, axis=-1)
            idx = jnp.argmax(gates, axis=-1)
            mask1 = jax.nn.one_hot(idx, E, dtype=x.dtype)
            loc = jnp.sum((jnp.cumsum(mask1, 0) - 1.0) * mask1, -1).astype(jnp.int32)
            keep = loc < cap
            gate_val = jnp.take_along_axis(gates, idx[:, None], -1)[:, 0]
            slot = jnp.where(keep, idx.astype(jnp.int32) * cap + loc, E * cap)
            disp = jnp.zeros((E * cap, D), x.dtype).at[slot].set(xf, mode='drop')
            disp = disp.reshape(E, cap, D)
            h = jnp.einsum('ecd,edf->ecf', disp, w1) + b1[:, None, :]
            y = (jnp.einsum('ecf,efd->ecd', h, w2) + b2[:, None, :]).reshape(E * cap, D)
            out = jnp.where(keep[:, None], gate_val[:, None] * y[jnp.minimum(slot, E * cap - 1)], 0.0)
            return out.reshape(L, N, D)
        y1 = _ln(x + _mha(x, in_proj_w, in_proj_b, out_proj_w, out_proj_b), ln1_g, ln1_b)
        y2 = _ln(y1 + _moe(y1, wg, w1, b1, w2, b2), ln2_g, ln2_b)
        return y2
    x = x + _L0_attn_ref(_layernorm(x, axis=-1), L0_attn_ln_gamma, L0_attn_ln_beta, L0_attn_w_qkv, L0_attn_w_out)
    x = x + _L0_xattn_ref(ctx_1024, _layernorm(x, axis=-1), mask_BxS2_bf1, L0_xattn_ln_x_g, L0_xattn_ln_x_b, L0_xattn_ln_l_g, L0_xattn_ln_l_b, L0_xattn_qn_g, L0_xattn_kn_g, L0_xattn_Wq, L0_xattn_Wkv, L0_xattn_Wout, L0_xattn_bout)
    x = x + _L0_ffn_ref(_layernorm(x, axis=-1), L0_ffn_W_up, L0_ffn_A_up, L0_ffn_B_up, L0_ffn_scale_up, L0_ffn_bias_up, L0_ffn_W_down, L0_ffn_A_down, L0_ffn_B_down, L0_ffn_scale_down, L0_ffn_bias_down)
    x = x + _L1_attn_ref(_layernorm(x, axis=-1), L1_attn_rotation_params, L1_attn_entangle_params)
    x = x + _L1_xattn_ref(_layernorm(x, axis=-1), ctx_1024, ctx_1024, mask_SxS2_if1, L1_xattn_Wq, L1_xattn_bq, L1_xattn_Wk, L1_xattn_bk, L1_xattn_Wv, L1_xattn_bv, L1_xattn_Wo, L1_xattn_bo)
    x = x + _L1_ffn_ref(_layernorm(x, axis=-1), L1_ffn_in_proj_w, L1_ffn_in_proj_b, L1_ffn_out_proj_w, L1_ffn_out_proj_b, L1_ffn_ln1_g, L1_ffn_ln1_b, L1_ffn_ln2_g, L1_ffn_ln2_b, L1_ffn_wg, L1_ffn_w1, L1_ffn_b1, L1_ffn_w2, L1_ffn_b2)
    return x

_drawn_inputs = setup_inputs


def setup_inputs(seed=0):
    import zlib

    import numpy as np

    out = dict(_drawn_inputs(seed))
    spreads = {'L0_attn_ln_gamma': (1.0, 0.6),
     'L0_attn_ln_beta': (0.0, 0.1),
     'L0_xattn_ln_x_g': (1.0, 0.546),
     'L0_xattn_ln_x_b': (0.0, 0.271),
     'L0_xattn_ln_l_g': (1.0, 0.6),
     'L0_xattn_ln_l_b': (0.0, 0.69),
     'L0_xattn_qn_g': (1.0, 0.6),
     'L0_xattn_kn_g': (1.0, 0.6),
     'L0_xattn_bout': (0.0, 0.1),
     'L0_ffn_bias_up': (0.0, 0.8),
     'L0_ffn_bias_down': (0.0, 0.1),
     'L1_ffn_in_proj_b': (0.0, 0.495),
     'L1_ffn_out_proj_b': (0.0, 0.1),
     'L1_ffn_ln1_g': (1.0, 0.2),
     'L1_ffn_ln1_b': (0.0, 0.1),
     'L1_ffn_ln2_g': (1.0, 0.2),
     'L1_ffn_ln2_b': (0.0, 0.1),
     'L1_ffn_b1': (0.0, 0.8),
     'L1_ffn_b2': (0.0, 0.8)}
    factors = {'L0_ffn_W_up': 8.0,
     'L0_ffn_A_up': 8.0,
     'L0_ffn_B_up': 8.0,
     'L0_ffn_W_down': 8.0,
     'L0_ffn_A_down': 8.0,
     'L0_ffn_B_down': 8.0,
     'L1_xattn_Wq': 5.678,
     'L1_xattn_bq': 8.0,
     'L1_xattn_Wk': 5.91,
     'L1_xattn_bk': 8.0,
     'L1_xattn_bv': 2.967,
     'L1_xattn_bo': 3.002,
     'L1_ffn_wg': 3.027,
     'L1_ffn_w1': 3.253,
     'L1_ffn_w2': 3.11}
    for name, (base, spread) in spreads.items():
        noise = np.random.default_rng([zlib.crc32(name.encode()), seed]).standard_normal(out[name].shape)
        drawn = base * np.exp(spread * noise) if base else spread * noise
        out[name] = jnp.asarray(drawn.astype(out[name].dtype))
    for name, factor in factors.items():
        out[name] = (out[name] * factor).astype(out[name].dtype)
    return out
```

```python
import numpy as np
import concourse.bass as bass
from concourse import mybir
from contextlib import ExitStack

F32 = mybir.dt.float32
U32 = mybir.dt.uint32
U8 = mybir.dt.uint8
ALU = mybir.AluOpType
ACT = mybir.ActivationFunctionType
AX = mybir.AxisListType

B, T, D = 8, 112, 256
C = 375
CT = 125
H = 16
KC = D // 128
PAIRS = B // 2
EPS = 1e-5
BANKS = 8


class Ring:

    def __init__(self, env, names):
        self.env = env
        self.names = names
        self.at = {name: i for i, name in enumerate(names)}
        assert len(self.at) == len(names)
        self.uses = [len(range(k, len(names), BANKS)) for k in range(BANKS)]
        self.base = list(env.bank_uses)

    def close(self, turns):
        for k in range(BANKS):
            self.env.bank_uses[k] += turns * self.uses[k]

    def bank(self, name):
        return self.env.psum[:, self.at[name] % BANKS, :]

    def _count(self, name, turn):
        i = self.at[name]
        return i % BANKS, turn * self.uses[i % BANKS] + (self.base[i % BANKS] + i // BANKS + 1)

    def wait_free(self, pe, name, turn):
        k, n = self._count(name, turn)
        pe.wait_ge(self.env.bank_free[k], n)
        return self.bank(name)

    def wait_full(self, eng, name, turn):
        k, n = self._count(name, turn)
        eng.wait_ge(self.env.bank_full[k], n)
        return self.bank(name)

    def wait_read(self, eng, name, turn):
        k, n = self._count(name, turn)
        eng.wait_ge(self.env.bank_free[k], n + 1)

    def full(self, name):
        return self.env.bank_full[self.at[name] % BANKS]

    def free(self, name):
        return self.env.bank_free[self.at[name] % BANKS]


COLUMNS = [("attn_gamma", KC), ("attn_beta", KC), ("xattn_x_gamma", KC), ("xattn_x_beta", KC),
           ("xattn_l_gamma", KC), ("xattn_l_beta", KC), ("q_gamma", 1), ("k_gamma", 1),
           ("rotation", KC), ("entangle", KC), ("bq", KC), ("bk", KC), ("in_proj_b", 6), ("b1", 64)]


class Env:

    def __init__(self, nc, ctx):
        self.nc = nc
        self.psum = ctx.enter_context(nc.psum_tensor("psum", [128, BANKS, 512], F32))
        self.bank_full = [ctx.enter_context(nc.semaphore(f"bank_full{k}")) for k in range(BANKS)]
        self.bank_free = [ctx.enter_context(nc.semaphore(f"bank_free{k}")) for k in range(BANKS)]
        self.bank_uses = [0] * BANKS
        self.x = ctx.enter_context(nc.sbuf_tensor("x_stream", [T, B, D], F32))
        self.y = ctx.enter_context(nc.sbuf_tensor("last_block_stream", [T, B, D], F32))
        self.ident = ctx.enter_context(nc.sbuf_tensor("ident", [128, 128], F32))
        self.columns = ctx.enter_context(nc.sbuf_tensor("columns", [128, sum(n for _, n in COLUMNS)], F32))
        self.minus_half = ctx.enter_context(nc.sbuf_tensor("minus_half", [128, 32], F32))


    def column_at(self, name):
        names = [other for other, _ in COLUMNS]
        return sum(n for _, n in COLUMNS[:names.index(name)])

    def col(self, name, k=0):
        at = self.column_at(name) + k
        return self.columns[:, at:at + 1]


def tools(nc, ctx, phase):
    def sb(name, shape, dtype=F32):
        return ctx.enter_context(nc.sbuf_tensor(f"{phase}_{name}", shape, dtype))

    def sem(name):
        return ctx.enter_context(nc.semaphore(f"{phase}_{name}"))
    return sb, sem


def heads(ap, h, d):
    return ap.rearrange("p (h d) -> p h d", h=h)


def spread(ap, n):
    p, h = ap.shape
    return ap.rearrange("p (h o) -> p h o", o=1).to_broadcast([p, h, n])


def transposes(pe, env, out, src, rows, cols, each=1):
    for k in range(each):
        last = pe.transpose(out[0:cols, k * rows:(k + 1) * rows], src[0:rows, k * cols:(k + 1) * cols],
                            env.ident[0:rows, 0:rows])
    return last


def phase_load(nc, env, x, columns):
    ctx = ExitStack()
    with ctx:
        sb, sem = tools(nc, ctx, "load")
        x_in, zeroed, ready = sem("x_in"), sem("zeroed"), sem("ready")
        block = ctx.enter_context(nc.Block())

        @block.sync
        def _(sp):
            sp.dma_start(env.x[:], x.rearrange("b s d -> s b d")).then_inc(x_in, 16)
            sp.dma_start(env.columns[:], columns).then_inc(x_in, 16)
            sp.wait_ge(x_in, 32)

        @block.tensor
        def _(pe):
            for k in range(BANKS):
                pe.sem_inc(env.bank_free[k], 1)

        @block.gpsimd
        def _(pool):
            pool.memset(env.minus_half[:], -0.5).then_inc(ready, 1)
            pool.memset(env.ident[:], 0.0).then_inc(zeroed, 1)
            pool.wait_ge(zeroed, 1)
            pool.affine_select(out=env.ident[:], in_=env.ident[:], compare_op=ALU.not_equal, fill=1.0,
                               base=0, pattern=[[-1, 128]], channel_multiplier=1).then_inc(ready, 1)
            pool.wait_ge(ready, 2)


def norm_columns(dve, mv, stats, src, n, rows, s_stats, s_var, scale, add):
    for k in range(n):
        dve.bn_stats(stats[0:rows, k, :], src(k)).then_inc(s_stats, 1)
    for k in range(n):
        dve.wait_ge(s_stats, k + 1)
        last = dve.bn_aggr(mv[0:rows, k, 0:2], stats[0:rows, k, :])
    last.then_inc(s_stats, 1)
    dve.wait_ge(s_stats, n + 1)
    dve.tensor_scalar(mv[0:rows, 0:n, 2], mv[0:rows, 0:n, 1], scale, add, ALU.mult, ALU.add).then_inc(s_var, 1)


def phase_self_attention_rope(nc, env, w_qkv, w_out, cos, sin):
    ctx = ExitStack()
    with ctx:
        sb, sem = tools(nc, ctx, "rope")
        DH, UNITS = 64, 8
        wq = sb("w_qkv", [128, KC, 3 * H * DH])
        wo = sb("w_out", [128, 8, D])
        cs = sb("cos", [T, DH])
        sn = sb("sin", [T, DH])
        stats = sb("stats", [T, B, 6])
        mv = sb("mean_var", [T, B, 4])
        xn = [sb(f"xn{i}", [T, D]) for i in range(2)]
        xT = [sb(f"xT{i}", [128, KC, T]) for i in range(2)]
        qk = [sb(f"qk{i}", [T, 2 * H * DH]) for i in range(2)]
        rot = [sb(f"rot{i}", [T, 512]) for i in range(2)]
        v = [sb(f"v{i}", [T, H, DH + 1]) for i in range(2)]
        qT = [sb(f"qT{i}", [128, 8, 2, T]) for i in range(2)]
        kT = [sb(f"kT{i}", [128, 8, T]) for i in range(2)]
        P = [sb(f"P{i}", [T, 4 * T]) for i in range(4)]
        PT = [sb(f"PT{i}", [T, 4 * T]) for i in range(2)]
        mx = sb("max", [T, UNITS, 4])
        rs = sb("recip", [T, UNITS, 4])
        o = [sb(f"o{i}", [T, H * DH]) for i in range(2)]
        oT = [sb(f"oT{i}", [128, 8, T]) for i in range(2)]

        loaded, w_loaded, wo_loaded, ones = sem("loaded"), sem("w_loaded"), sem("wo_loaded"), sem("ones")
        s_stats, s_var, s_rstd, s_xn = sem("stats"), sem("var"), sem("rstd"), sem("xn")
        s_rot, s_max, s_exp, s_sum = sem("rotated"), sem("max"), sem("exp"), sem("sum")

        def head(g, i):
            return 8 * (g // 2) + g % 2 + 2 * i

        units = [(g, par) for g in range(4) for par in range(2)]
        names = [("xT", par) for par in range(2)]
        names += [("qkv", par, j) for par in range(2) for j in range(6)]
        names += [("qkT", par, j) for par in range(2) for j in range(4)]
        for u in range(UNITS + 3):
            names += [("S", u)] * (u < UNITS) + [("PT", u - 2)] * (0 <= u - 2 < UNITS) + [("O", u - 3)] * (u >= 3)
        names += [("oT", par, j) for par in range(2) for j in range(2)]
        names += [("out", par) for par in range(2)]
        ring = Ring(env, names)
        block = ctx.enter_context(nc.Block())

        @block.sync
        def _(sp):
            sp.dma_start(cs[:], cos).then_inc(loaded, 16)
            sp.dma_start(sn[:], sin).then_inc(loaded, 16)
            sp.dma_start(wq[:], w_qkv.rearrange("(k p) n -> p k n", p=128)).then_inc(w_loaded, 16)
            sp.dma_start(wo[:], w_out.rearrange("(k p) n -> p k n", p=128)).then_inc(wo_loaded, 16)
            sp.wait_ge(w_loaded, 16)
            sp.wait_ge(wo_loaded, 16)

        @block.gpsimd
        def _(pool):
            for i in range(2):
                pool.memset(v[i][:], 1.0).then_inc(ones, 1)
                pool.memset(qT[i][:], 0.0).then_inc(ones, 1)
            pool.wait_ge(s_var, 1)
            pool.tensor_tensor(mv[:, :, 3], mv[:, :, 2], env.minus_half[0:T, 0:B], ALU.pow).then_inc(s_rstd, 1)
            with pool.Fori(0, PAIRS) as t:
                for par in range(2):
                    for j in range(4):
                        ring.wait_read(pool, ("qkv", par, j), t)
                        part = qk[par][:, j * 512:(j + 1) * 512]
                        pool.tensor_tensor(part, part, rot[j % 2][:], ALU.add).then_inc(s_rot, 1)

        @block.scalar
        def _(act):
            act.wait_ge(ones, 4)
            with act.Fori(0, PAIRS) as t:
                for par in range(2):
                    src = ring.wait_full(act, ("xT", par), t)
                    for k in range(KC):
                        last = act.activation(xT[par][:, k, :], src[:, k * T:(k + 1) * T], ACT.Identity,
                                              bias=env.col("attn_beta", k), scale=env.col("attn_gamma", k))
                    last.then_inc(ring.free(("xT", par)), 1)
                for par in range(2):
                    for j in range(4, 6):
                        src = ring.wait_full(act, ("qkv", par, j), t)
                        act.copy(v[par][:, (j - 4) * 8:(j - 3) * 8, 0:DH],
                                 heads(src[0:T, :], 8, DH)).then_inc(ring.free(("qkv", par, j)), 1)
                for par in range(2):
                    for j in range(2):
                        src = ring.wait_full(act, ("qkT", par, j), t)
                        for half in range(2):
                            rows = slice(64 * half, 64 * half + 64)
                            last = act.copy(qT[par][rows, 4 * j:4 * j + 4, half, :], heads(src[rows, 0:4 * T], 4, T))
                        last.then_inc(ring.free(("qkT", par, j)), 1)
                    for j in range(2):
                        src = ring.wait_full(act, ("qkT", par, 2 + j), t)
                        act.copy(kT[par][:, 4 * j:4 * j + 4, :].rearrange("p a b -> p (a b)"),
                                 src[:, 0:4 * T]).then_inc(ring.free(("qkT", par, 2 + j)), 1)
                for u in range(UNITS + 2):
                    if u < UNITS:
                        ring.wait_read(act, ("S", u), t)
                        act.activation(P[u % 4][:], P[u % 4][:], ACT.Exp, scale=DH ** -0.5).then_inc(s_exp, 1)
                    if u >= 2:
                        src = ring.wait_full(act, ("PT", u - 2), t)
                        act.copy(PT[u % 2][:], src[0:T, 0:4 * T]).then_inc(ring.free(("PT", u - 2)), 1)
                for par in range(2):
                    for j in range(2):
                        src = ring.wait_full(act, ("oT", par, j), t)
                        act.copy(oT[par][:, 4 * j:4 * j + 4, :].rearrange("p a b -> p (a b)"),
                                 src[:, 0:4 * T]).then_inc(ring.free(("oT", par, j)), 1)

        @block.vector
        def _(dve):
            dve.wait_ge(loaded, 32)
            norm_columns(dve, mv, stats, lambda k: env.x[:, k, :], B, T, s_stats, s_var, 1.0 + EPS, EPS * EPS)
            dve.wait_ge(s_rstd, 1)
            with dve.Fori(0, PAIRS) as t:
                for par in range(2):
                    b = t * 2 + par
                    xb = env.x[:, bass.ds(b, 1), :].rearrange("p a d -> p (a d)")
                    dve.tensor_scalar(xn[par][:], xb, mv[:, bass.ds(b, 1), 0:1].rearrange("p a o -> p (a o)"),
                                      mv[:, bass.ds(b, 1), 3:4].rearrange("p a o -> p (a o)"),
                                      ALU.subtract, ALU.mult).then_inc(s_xn, 1)
                for par in range(2):
                    for j in range(4):
                        src = ring.wait_full(dve, ("qkv", par, j), t)
                        if par * 4 + j >= 2:
                            dve.wait_ge(s_rot, t * 8 + (par * 4 + j - 1))
                        th = heads(src[0:T, :], 8, DH)
                        ch = cs[:, :].rearrange("p (o d) -> p o d", o=1).to_broadcast([T, 8, DH])
                        rh = heads(rot[j % 2][:], 8, DH)
                        HD = DH // 2
                        dve.tensor_tensor(heads(qk[par][:, j * 512:(j + 1) * 512], 8, DH), th, ch, ALU.mult)
                        for a in range(2):
                            sh = sn[:, a * HD:(a + 1) * HD].rearrange("p (o d) -> p o d", o=1)\
                                .to_broadcast([T, 8, HD])
                            last = dve.tensor_tensor(rh[:, :, a * HD:(a + 1) * HD],
                                                     th[:, :, (1 - a) * HD:(2 - a) * HD], sh, ALU.mult)
                        last.then_inc(ring.free(("qkv", par, j)), 1)
                for u in range(UNITS + 3):
                    if u < UNITS:
                        src = ring.wait_full(dve, ("S", u), t)
                        s4 = heads(src[0:T, 0:4 * T], 4, T)
                        dve.tensor_reduce(mx[:, u, :], s4, AX.X, ALU.max).then_inc(s_max, 1)
                        dve.wait_ge(s_max, t * UNITS + (u + 1))
                        dve.tensor_tensor(heads(P[u % 4][:], 4, T), s4, spread(mx[:, u, :], T),
                                          ALU.subtract).then_inc(ring.free(("S", u)), 1)
                    if u >= 3:
                        w = u - 3
                        g, par = units[w]
                        src = ring.wait_full(dve, ("O", w), t)
                        o4 = heads(src[0:T, 0:4 * (DH + 1)], 4, DH + 1)
                        dve.reciprocal(rs[:, w, :], o4[:, :, DH]).then_inc(s_sum, 1)
                        dve.wait_ge(s_sum, t * UNITS + (w + 1))
                        dve.tensor_tensor(heads(o[par][:], H, DH)[:, head(g, 0):head(g, 3) + 1:2, :], o4[:, :, 0:DH],
                                          spread(rs[:, w, :], DH), ALU.mult).then_inc(ring.free(("O", w)), 1)
                for par in range(2):
                    b = t * 2 + par
                    xb = env.x[:, bass.ds(b, 1), :].rearrange("p a d -> p (a d)")
                    src = ring.wait_full(dve, ("out", par), t)
                    dve.tensor_tensor(xb, xb, src[0:T, 0:D], ALU.add).then_inc(ring.free(("out", par)), 1)

        @block.tensor
        def _(pe):
            pe.wait_ge(w_loaded, 16)
            pe.wait_ge(wo_loaded, 16)
            with pe.Fori(0, PAIRS) as t:
                for par in range(2):
                    out = ring.wait_free(pe, ("xT", par), t)
                    pe.wait_ge(s_xn, t * 2 + (par + 1))
                    transposes(pe, env, out, xn[par], T, 128, KC).then_inc(ring.full(("xT", par)), 1)
                for par in range(2):
                    ring.wait_read(pe, ("xT", par), t)
                    for j in range(6):
                        out = ring.wait_free(pe, ("qkv", par, j), t)
                        for k in range(KC):
                            last = pe.matmul(out[0:T, :], xT[par][:, k, :], wq[:, k, j * 512:(j + 1) * 512],
                                             start=k == 0, stop=k == KC - 1)
                        last.then_inc(ring.full(("qkv", par, j)), 1)
                for par in range(2):
                    for j in range(4):
                        pe.wait_ge(s_rot, t * 8 + (par * 4 + j + 1))
                        out = ring.wait_free(pe, ("qkT", par, j), t)
                        transposes(pe, env, out, qk[par][:, j * 512:(j + 1) * 512], T, 128, 4)\
                            .then_inc(ring.full(("qkT", par, j)), 1)
                for u in range(UNITS + 3):
                    if u < UNITS:
                        g, par = units[u]
                        out = ring.wait_free(pe, ("S", u), t)
                        ring.wait_read(pe, ("qkT", par, 2 + g // 2), t)
                        for i in range(4):
                            h = head(g, i)
                            last = pe.matmul(out[0:T, i * T:(i + 1) * T], qT[par][:, h // 2, h % 2, :],
                                             kT[par][:, h // 2, :], start=True, stop=True)
                        last.then_inc(ring.full(("S", u)), 1)
                    if 0 <= u - 2 < UNITS:
                        w = u - 2
                        out = ring.wait_free(pe, ("PT", w), t)
                        pe.wait_ge(s_exp, t * UNITS + (w + 1))
                        transposes(pe, env, out, P[w % 4], T, T, 4).then_inc(ring.full(("PT", w)), 1)
                    if u >= 3:
                        w = u - 3
                        g, par = units[w]
                        out = ring.wait_free(pe, ("O", w), t)
                        ring.wait_read(pe, ("PT", w), t)
                        ring.wait_read(pe, ("qkv", par, 4 + g // 2), t)
                        for i in range(4):
                            last = pe.matmul(out[0:T, i * (DH + 1):(i + 1) * (DH + 1)],
                                             PT[w % 2][:, i * T:(i + 1) * T], v[par][:, head(g, i), :],
                                             start=True, stop=True)
                        last.then_inc(ring.full(("O", w)), 1)
                for par in range(2):
                    ring.wait_read(pe, ("O", UNITS - 2 + par), t)
                    for j in range(2):
                        out = ring.wait_free(pe, ("oT", par, j), t)
                        transposes(pe, env, out, o[par][:, j * 512:(j + 1) * 512], T, 128, 4)\
                            .then_inc(ring.full(("oT", par, j)), 1)
                for par in range(2):
                    out = ring.wait_free(pe, ("out", par), t)
                    ring.wait_read(pe, ("oT", par, 1), t)
                    for k in range(8):
                        last = pe.matmul(out[0:T, 0:D], oT[par][:, k, :], wo[:, k, :], start=k == 0, stop=k == 7)
                    last.then_inc(ring.full(("out", par)), 1)
        ring.close(PAIRS)


def phase_cross_attention_normed(nc, env, ctx_rows, mask, w_q, w_kv, w_out, b_out):
    ctx = ExitStack()
    with ctx:
        sb, sem = tools(nc, ctx, "cross")
        DH, UNITS, NT = 64, 32, C // CT
        KEYS = C + T
        BIG = float(np.finfo(np.float32).max)
        wq = sb("w_q", [128, KC, H * DH])
        wkv = sb("w_kv", [128, KC, 2 * H * DH])
        wo = sb("w_out", [128, 8, D])
        bo = sb("b_out", [T, D])
        rows_in = sb("ctx", [CT, B * NT, D])
        mask_in = sb("mask", [T, B, C], U8)
        qk_gamma = sb("qk_gamma", [128, 1])
        stats = sb("stats", [128, B * NT + B, 6])
        mv = sb("mean_var", [128, B * NT + B, 4])
        bias = [sb(f"mask_bias{i}", [T, KEYS]) for i in range(2)]
        xn = [sb(f"xn{i}", [CT, D]) for i in range(2)]
        xT = [sb(f"xT{i}", [128, KC, CT]) for i in range(2)]
        lT = [sb(f"lT{i}", [128, KC, T]) for i in range(2)]
        sq = [sb(f"squares{i}", [CT, H * DH]) for i in range(2)]
        ssq = sb("rms", [CT, 10, 2, H])
        kn = [sb(f"kn{i}", [CT, H * DH]) for i in range(2)]
        kT = [sb(f"kT{i}", [128, 8, KEYS]) for i in range(2)]
        qT = [sb(f"qT{i}", [128, 8, 2, T]) for i in range(2)]
        v = [sb(f"v{i}", [CT, NT + 1, H, DH + 1]) for i in range(2)]
        P = [sb(f"P{i}", [T, KEYS]) for i in range(4)]
        low = sb("row_min", [T, UNITS])
        PT = [sb(f"PT{i}", [CT, 4 * T]) for i in range(4)]
        rs = sb("recip", [T, UNITS // 4, 4])
        o = [sq[i][0:T, :] for i in range(2)]
        oT = [sb(f"oT{i}", [128, 8, T]) for i in range(2)]
        waited = sb("waited", [1, UNITS // 2])
        res = [sb(f"res{i}", [T, D]) for i in range(2)]

        loaded, w_loaded, wo_loaded, set_up = sem("loaded"), sem("w_loaded"), sem("wo_loaded"), sem("set_up")
        s_stats, s_var, s_lstats, s_lvar, s_rstd = sem("stats"), sem("var"), sem("lstats"), sem("lvar"), sem("rstd")
        s_xn, s_sq, s_ssum, s_mean, s_rms, s_kn = sem("xn"), sem("sq"), sem("ssum"), sem("mean"), sem("rms"), sem("kn")
        s_bias, s_exp, s_sum, s_res, s_gamma = sem("bias"), sem("exp"), sem("sum"), sem("res"), sem("gamma")
        s_low = sem("low")

        tiles = [(par, c) for par in range(2) for c in range(5)]
        TILES = len(tiles)
        height = [CT, CT, CT, T, T]

        def turned(i):
            par, c = tiles[i]
            return xT[i % 2][:, :, 0:CT] if c < 3 else lT[par][:, :, :]

        names = [("xT", 0)]
        for i in range(TILES + 1):
            names += [("xT", i + 1)] * (i + 1 < TILES and tiles[min(i + 1, TILES - 1)][1] < 4)
            if i < TILES:
                names += [("mm", i, j) for j in range(4 if tiles[i][1] < 4 else 2)]
            if i >= 1:
                names += [("kT", i - 1, j) for j in range(2)]
        STEPS = UNITS // 2
        for s in range(STEPS + 2):
            if s < STEPS:
                names += [("S", 2 * s), ("S", 2 * s + 1)]
            if 1 <= s <= STEPS:
                names += [("PT", 2 * s - 2), ("PT", 2 * s - 1)]
            if s >= 2 and s % 2 == 0:
                names += [("O", s // 2 - 1)]
        names += [("oT", par, j) for par in range(2) for j in range(2)]
        names += [("out", par) for par in range(2)]
        ring = Ring(env, names)
        block = ctx.enter_context(nc.Block())

        @block.sync
        def _(sp):
            sp.dma_start(rows_in[:], ctx_rows.rearrange("b (c p) d -> p (b c) d", p=CT)).then_inc(loaded, 16)
            sp.dma_start(mask_in[:], mask.rearrange("(o b) c -> o b c", o=1).to_broadcast([T, B, C]))\
                .then_inc(loaded, 16)
            sp.dma_start(bo[:], b_out.rearrange("(o d) -> o d", o=1).to_broadcast([T, D])).then_inc(loaded, 16)
            sp.dma_start(wkv[:], w_kv.rearrange("(k p) n -> p k n", p=128)).then_inc(w_loaded, 16)
            sp.dma_start(wq[:], w_q.rearrange("(k p) n -> p k n", p=128)).then_inc(w_loaded, 16)
            sp.dma_start(wo[:], w_out.rearrange("(k p) n -> p k n", p=128)).then_inc(wo_loaded, 16)
            sp.wait_ge(wo_loaded, 16)

        @block.gpsimd
        def _(pool):
            for i in range(2):
                pool.memset(v[i][:], 1.0).then_inc(set_up, 1)
                pool.memset(bias[i][:, C:KEYS], 0.0).then_inc(set_up, 1)
                pool.memset(qT[i][:], 0.0).then_inc(set_up, 1)
            pool.wait_ge(s_lvar, 1)
            pool.tensor_tensor(mv[0:T, B * NT:, 3], mv[0:T, B * NT:, 2], env.minus_half[0:T, 0:B], ALU.pow)\
                .then_inc(s_rstd, 1)
            pool.wait_ge(s_var, 1)
            pool.tensor_tensor(mv[0:CT, 0:B * NT, 3], mv[0:CT, 0:B * NT, 2], env.minus_half[0:CT, 0:B * NT],
                               ALU.pow).then_inc(s_rstd, 1)
            with pool.Fori(0, PAIRS) as t:
                for i in range(TILES):
                    n = height[tiles[i][1]]
                    pool.wait_ge(s_mean, t * TILES + (i + 1))
                    pool.tensor_tensor(ssq[0:n, i, 1, :], ssq[0:n, i, 0, :], env.minus_half[0:n, 0:H],
                                       ALU.pow).then_inc(s_rms, 1)

        @block.scalar
        def _(act):
            act.wait_ge(set_up, 6)
            act.wait_ge(s_gamma, 2)

            def turn_evac(i, t):
                c = tiles[i][1]
                n = height[c]
                src = ring.wait_full(act, ("xT", i), t)
                kind = "x" if c < 3 else "l"
                for k in range(KC):
                    last = act.activation(turned(i)[:, k, :], src[:, k * n:(k + 1) * n], ACT.Identity,
                                          bias=env.col(f"xattn_{kind}_beta", k),
                                          scale=env.col(f"xattn_{kind}_gamma", k))
                last.then_inc(ring.free(("xT", i)), 1)

            with act.Fori(0, PAIRS) as t:
                turn_evac(0, t)
                for i in range(TILES + 1):
                    if ("xT", i + 1) in ring.at:
                        turn_evac(i + 1, t)
                    if i < TILES:
                        par, c = tiles[i]
                        n = height[c]
                        for j in range(2):
                            src = ring.wait_full(act, ("mm", i, j), t)
                            act.activation(sq[i % 2][0:n, j * 512:(j + 1) * 512], src[0:n, :], ACT.Square)\
                                .then_inc(s_sq, 1)
                        for j in range(2 * (c < 4)):
                            src = ring.wait_full(act, ("mm", i, 2 + j), t)
                            act.copy(v[par][0:n, c, 8 * j:8 * j + 8, 0:DH], heads(src[0:n, :], 8, DH))\
                                .then_inc(ring.free(("mm", i, 2 + j)), 1)
                    if i >= 1:
                        par, c = tiles[i - 1]
                        n = height[c]
                        for j in range(2):
                            src = ring.wait_full(act, ("kT", i - 1, j), t)
                            s4 = heads(src[:, 0:4 * n], 4, n)
                            if c < 4:
                                op = act.copy(kT[par][:, 4 * j:4 * j + 4, c * CT:c * CT + n], s4)
                            else:
                                for half in range(2):
                                    rows = slice(64 * half, 64 * half + 64)
                                    op = act.mul(qT[par][rows, 4 * j:4 * j + 4, half, :], s4[rows],
                                                 qk_gamma[rows, :])
                            op.then_inc(ring.free(("kT", i - 1, j)), 1)
                for s in range(STEPS + 1):
                    if s < STEPS:
                        for u in (2 * s, 2 * s + 1):
                            ring.wait_read(act, ("S", u), t)
                            act.activation(P[u % 4][:], P[u % 4][:], ACT.Exp, bias=low[:, u:u + 1],
                                           scale=-1.0).then_inc(s_exp, 1)
                    if s >= 1:
                        u = 2 * s - 2
                        src = ring.wait_full(act, ("PT", u), t)
                        act.copy(PT[u % 4][:], src[0:CT, 0:4 * T]).then_inc(ring.free(("PT", u)), 1)
                for par in range(2):
                    for j in range(2):
                        src = ring.wait_full(act, ("oT", par, j), t)
                        act.copy(oT[par][:, 4 * j:4 * j + 4, :].rearrange("p a b -> p (a b)"),
                                 src[:, 0:4 * T]).then_inc(ring.free(("oT", par, j)), 1)

        @block.vector
        def _(dve):
            dve.tensor_scalar(qk_gamma[:], env.col("q_gamma"), env.col("k_gamma"), -(DH ** -0.5),
                              ALU.mult, ALU.mult).then_inc(s_gamma, 2)
            norm_columns(dve, mv[:, B * NT:, :], stats[:, B * NT:, :], lambda k: env.x[:, k, :], B, T,
                         s_lstats, s_lvar, 1.0 + EPS, EPS * EPS)
            dve.wait_ge(loaded, 48)
            norm_columns(dve, mv, stats[:, :, :], lambda k: rows_in[:, k, :], B * NT, CT, s_stats, s_var,
                         1.0, EPS)
            dve.wait_ge(s_rstd, 2)
            dve.wait_ge(set_up, 6)

            def normalise(i, t):
                par, c = tiles[i]
                b = t * 2 + par
                n = height[c]
                at, src = (b * NT + c, rows_in) if c < 3 else (b + B * NT, env.x)
                row = src[0:n, bass.ds(at if c < 3 else b, 1), :].rearrange("p a d -> p (a d)")
                dve.tensor_scalar(xn[i % 2][0:n, :], row,
                                  mv[0:n, bass.ds(at, 1), 0:1].rearrange("p a o -> p (a o)"),
                                  mv[0:n, bass.ds(at, 1), 3:4].rearrange("p a o -> p (a o)"),
                                  ALU.subtract, ALU.mult).then_inc(s_xn, 1)

            with dve.Fori(0, PAIRS) as t:
                for par in range(2):
                    b = t * 2 + par
                    dve.tensor_scalar(bias[par][:, 0:C], mask_in[:, bass.ds(b, 1), :].rearrange("p a c -> p (a c)"),
                                      -BIG, BIG, ALU.mult, ALU.add).then_inc(s_bias, 1)
                normalise(0, t)
                for i in range(TILES):
                    if i + 1 < TILES and tiles[i + 1][1] < 4:
                        if i >= 1:
                            ring.wait_full(dve, ("xT", i - 1 if tiles[i - 1][1] < 4 else i - 2), t)
                        normalise(i + 1, t)
                    n = height[tiles[i][1]]
                    dve.wait_ge(s_sq, t * 2 * TILES + 2 * (i + 1))
                    dve.tensor_reduce(ssq[0:n, i, 0, :], heads(sq[i % 2][0:n, :], H, DH), AX.X, ALU.add)\
                        .then_inc(s_ssum, 1)
                    dve.wait_ge(s_ssum, t * TILES + (i + 1))
                    dve.tensor_scalar(ssq[0:n, i, 0, :], ssq[0:n, i, 0, :], 1.0 / DH, 1e-16, ALU.mult, ALU.max)\
                        .then_inc(s_mean, 1)
                    dve.wait_ge(s_rms, t * TILES + (i + 1))
                    for j in range(2):
                        src = ring.wait_full(dve, ("mm", i, j), t)
                        dve.tensor_tensor(heads(kn[i % 2][0:n, j * 512:(j + 1) * 512], 8, DH),
                                          heads(src[0:n, :], 8, DH), spread(ssq[0:n, i, 1, 8 * j:8 * j + 8], DH),
                                          ALU.mult).then_inc(ring.free(("mm", i, j)), 1)
                for s in range(STEPS + 3):
                    if s < STEPS:
                        if s == 0:
                            dve.wait_ge(s_bias, t * 2 + 2)
                        for u in (2 * s, 2 * s + 1):
                            src = ring.wait_full(dve, ("S", u), t)
                        dve.tensor_copy(waited[:, s:s + 1], src[0:1, 0:1])
                        for u in (2 * s, 2 * s + 1):
                            src = ring.bank(("S", u))
                            dve.tensor_tensor_reduce(out=P[u % 4][:], in0=src[0:T, 0:KEYS], in1=bias[u // H][:],
                                                     scale=1.0, scalar=BIG, op0=ALU.add, op1=ALU.min,
                                                     accum_out=low[:, u:u + 1]).then_inc(ring.free(("S", u)), 1)
                    if s >= 4 and s % 2 == 0:
                        w = s // 2 - 2
                        src = ring.wait_full(dve, ("O", w), t)
                        o4 = heads(src[0:T, 0:4 * (DH + 1)], 4, DH + 1)
                        dve.reciprocal(rs[:, w, :], o4[:, :, DH]).then_inc(s_sum, 1)
                        dve.wait_ge(s_sum, t * (UNITS // 4) + (w + 1))
                        dve.tensor_tensor(heads(o[w // 4][:, (w % 4) * 4 * DH:(w % 4 + 1) * 4 * DH], 4, DH),
                                          o4[:, :, 0:DH], spread(rs[:, w, :], DH), ALU.mult)\
                            .then_inc(ring.free(("O", w)), 1)
                    if 1 <= s <= STEPS:
                        u = 2 * s - 1
                        src = ring.wait_full(dve, ("PT", u), t)
                        dve.tensor_copy(PT[u % 4][:], src[0:CT, 0:4 * T]).then_inc(ring.free(("PT", u)), 1)
                for par in range(2):
                    b = t * 2 + par
                    xb = env.x[:, bass.ds(b, 1), :].rearrange("p a d -> p (a d)")
                    src = ring.wait_full(dve, ("out", par), t)
                    dve.tensor_tensor(res[par][:], bo[:], src[0:T, 0:D], ALU.add).then_inc(ring.free(("out", par)), 1)
                    ring.wait_read(dve, ("out", par), t)
                    dve.tensor_tensor(xb, xb, res[par][:], ALU.add).then_inc(s_res, 1)

        @block.tensor
        def _(pe):
            pe.wait_ge(w_loaded, 32)
            pe.wait_ge(wo_loaded, 16)
            turned_rows = [i for i in range(TILES) if tiles[i][1] < 4]

            def turn(i, t):
                out = ring.wait_free(pe, ("xT", i), t)
                pe.wait_ge(s_xn, t * len(turned_rows) + (turned_rows.index(i) + 1))
                n = height[tiles[i][1]]
                transposes(pe, env, out, xn[i % 2], n, 128, KC).then_inc(ring.full(("xT", i)), 1)

            with pe.Fori(0, PAIRS) as t:
                turn(0, t)
                for i in range(TILES + 1):
                    if ("xT", i + 1) in ring.at:
                        turn(i + 1, t)
                    if i < TILES:
                        par, c = tiles[i]
                        n = height[c]
                        if c < 4:
                            ring.wait_read(pe, ("xT", i), t)
                        for j in range(4 if c < 4 else 2):
                            out = ring.wait_free(pe, ("mm", i, j), t)
                            w = wkv if c < 4 else wq
                            for k in range(KC):
                                last = pe.matmul(out[0:n, :], turned(i)[:, k, :] if c < 4 else lT[par][:, k, :],
                                                 w[:, k, j * 512:(j + 1) * 512], start=k == 0, stop=k == KC - 1)
                            last.then_inc(ring.full(("mm", i, j)), 1)
                    if i >= 1:
                        n = height[tiles[i - 1][1]]
                        for j in range(2):
                            out = ring.wait_free(pe, ("kT", i - 1, j), t)
                            ring.wait_read(pe, ("mm", i - 1, j), t)
                            transposes(pe, env, out, kn[(i - 1) % 2][:, j * 512:(j + 1) * 512], n, 128, 4)\
                                .then_inc(ring.full(("kT", i - 1, j)), 1)
                for s in range(STEPS + 2):
                    if s < STEPS:
                        for u in (2 * s, 2 * s + 1):
                            par, h = divmod(u, H)
                            out = ring.wait_free(pe, ("S", u), t)
                            if s == 0:
                                ring.wait_read(pe, ("kT", TILES - 1, 1), t)
                            pe.matmul(out[0:T, 0:KEYS], qT[par][:, h // 2, h % 2, :], kT[par][:, h // 2, :],
                                      start=True, stop=True).then_inc(ring.full(("S", u)), 1)
                    if 1 <= s <= STEPS:
                        for u in (2 * s - 2, 2 * s - 1):
                            out = ring.wait_free(pe, ("PT", u), t)
                            pe.wait_ge(s_exp, t * UNITS + (u + 1))
                            for c in range(4):
                                n = height[c]
                                last = pe.transpose(out[0:n, c * T:(c + 1) * T], P[u % 4][:, c * CT:c * CT + n],
                                                    env.ident[0:T, 0:T])
                            last.then_inc(ring.full(("PT", u)), 1)
                    if s >= 2:
                        for u in (2 * s - 4, 2 * s - 3):
                            par, h = divmod(u, H)
                            out = ring.wait_free(pe, ("O", u // 4), t) if u % 4 == 0 else ring.bank(("O", u // 4))
                            ring.wait_read(pe, ("PT", u), t)
                            for c in range(4):
                                n = height[c]
                                last = pe.matmul(out[0:T, (u % 4) * (DH + 1):(u % 4 + 1) * (DH + 1)],
                                                 PT[u % 4][0:n, c * T:(c + 1) * T], v[par][0:n, c, h, :],
                                                 start=c == 0, stop=c == 3)
                            if u % 4 == 3:
                                last.then_inc(ring.full(("O", u // 4)), 1)
                for par in range(2):
                    ring.wait_read(pe, ("O", 4 * par + 3), t)
                    for j in range(2):
                        out = ring.wait_free(pe, ("oT", par, j), t)
                        transposes(pe, env, out, o[par][:, j * 512:(j + 1) * 512], T, 128, 4)\
                            .then_inc(ring.full(("oT", par, j)), 1)
                for par in range(2):
                    out = ring.wait_free(pe, ("out", par), t)
                    ring.wait_read(pe, ("oT", par, 1), t)
                    for k in range(8):
                        last = pe.matmul(out[0:T, 0:D], oT[par][:, k, :], wo[:, k, :], start=k == 0, stop=k == 7)
                    last.then_inc(ring.full(("out", par)), 1)
        ring.close(PAIRS)


def phase_kronecker_experts(nc, env, w_up, a_up, b_up, w_down, a_down, b_down, bias_up, bias_down, scales):
    ctx = ExitStack()
    with ctx:
        sb, sem = tools(nc, ctx, "kron")
        E, D1, F1 = 64, 32, 64
        N = 2 * T // 4
        NB = T // 4
        router_up = sb("router_up", [128, 8, E])
        router_down = sb("router_down", [128, F1, E])
        first_up = sb("b_up", [128, E, F1])
        second_up = sb("a_up", [128, E, F1])
        first_down = sb("b_down", [128, E, D1])
        second_down = sb("a_down", [128, E, D1])
        bias_u = sb("bias_up", [F1, F1])
        bias_d = sb("bias_down", [D1, D1])
        scale = sb("scales", [F1, 2])
        ones = sb("ones", [N, 128])
        stats = sb("stats", [T, B, 6])
        mv = sb("mean_var", [T, B, 4])
        xn = [sb(f"xn{i}", [T, D]) for i in range(2)]
        xT = sb("xT", [128, KC, 2 * T])
        X = sb("X", [128, N, D1])
        W = [sb(f"W{i}", [128, 8, F1]) for i in range(4)]
        pre = [sb(f"pre{i}", [F1, 512]) for i in range(2)]
        h = sb("h", [128, N, F1])
        W2 = [sb(f"W2_{i}", [128, 16, D1]) for i in range(4)]
        y = sb("y", [D1, N, D1])
        yT = sb("yT", [128, KC, 2 * T])
        logits = [sb(f"logits{i}", [N, E]) for i in range(2)]
        top = [sb(f"top{i}", [N, 8]) for i in range(2)]
        which = [sb(f"which{i}", [N, 8], U32) for i in range(2)]
        which8 = [sb(f"which8_{i}", [N, 2], U8) for i in range(2)]
        prob = [sb(f"prob{i}", [N, 8]) for i in range(2)]
        diag = [sb(f"diag{i}", [N, N, 2]) for i in range(2)]
        pb = [sb(f"prob_rows{i}", [F1, 2 * N]) for i in range(2)]
        row = [sb(f"index_row{i}", [1, 2 * N], U8) for i in range(2)]
        waited = sb("waited", [1, 8])

        loaded, tables, zeroed, oned = sem("loaded"), sem("tables"), sem("zeroed"), sem("oned")
        s_stats, s_var, s_rstd, s_xn = sem("stats"), sem("var"), sem("rstd"), sem("xn")
        s_X, s_h, s_pre, s_yT = sem("X"), sem("h"), sem("pre"), sem("yT")
        s_top, s_which, s_which8, s_diff, s_exp = sem("top"), sem("which"), sem("which8"), sem("diff"), sem("exp")
        s_den, s_p0, s_p1, s_diag = sem("den"), sem("p0"), sem("p1"), sem("diag")
        s_index = [sem("index_up"), sem("index_down")]

        UP_W, UP_H, DN_W = N // 4, N // 8, N // 8
        names = [("xT", 0), ("xT", 1), ("logits", 0), ("probs", 0)]
        for w in range(UP_W + 1):
            names += [("W", w)] * (w < UP_W) + [("h", (w - 1) // 2)] * (w >= 1 and (w - 1) % 2 == 0)
        names += [("logits", 1), ("probs", 1)]
        for w in range(DN_W + 1):
            names += [("W2", w)] * (w < DN_W) + [("y", w - 1)] * (w >= 1)
        names += [("back", 0), ("back", 1)]
        ring = Ring(env, names)
        block = ctx.enter_context(nc.Block())

        @block.sync
        def _(sp):
            sp.dma_start(router_up[:], w_up).then_inc(loaded, 16)
            sp.dma_start(bias_u[:], bias_up).then_inc(loaded, 16)
            sp.dma_start(bias_d[:], bias_down).then_inc(loaded, 16)
            sp.dma_start(scale[:], scales.rearrange("(o d) -> o d", o=1).to_broadcast([F1, 2])).then_inc(loaded, 16)
            sp.wait_ge(zeroed, 15)
            sp.dma_start(router_down[0:F1], w_down).then_inc(tables, 16)
            sp.dma_start(first_up[0:D1], b_up).then_inc(tables, 16)
            sp.dma_start(second_up[0:D1], a_up).then_inc(tables, 16)
            sp.dma_start(first_down[0:F1], b_down).then_inc(tables, 16)
            sp.dma_start(second_down[0:F1], a_down).then_inc(tables, 16)
            with sp.Fori(0, PAIRS) as t:
                for layer in range(2):
                    sp.wait_ge(s_which8, t * 2 + (layer + 1))
                    sp.dma_start(row[layer][:].rearrange("o (n k) -> o n k", k=2),
                                 which8[layer][:]).then_inc(s_index[layer], 16)

        @block.gpsimd
        def _(pool):
            for z in [router_down, first_up, second_up, first_down, second_down, X, *W, h, *W2]:
                pool.memset(z[:], 0.0).then_inc(zeroed, 1)
            pool.memset(ones[:], 1.0).then_inc(oned, 1)
            pool.wait_ge(s_var, 1)
            pool.tensor_tensor(mv[:, :, 3], mv[:, :, 2], env.minus_half[0:T, 0:B], ALU.pow).then_inc(s_rstd, 1)

        @block.scalar
        def _(act):
            act.wait_ge(loaded, 64)
            act.wait_ge(zeroed, 15)
            with act.Fori(0, PAIRS) as t:
                for par in range(2):
                    src = ring.wait_full(act, ("xT", par), t)
                    act.copy(xT[:, :, par * T:(par + 1) * T],
                             src[:, 0:KC * T].rearrange("p (k n) -> p k n", k=KC)).then_inc(ring.free(("xT", par)), 1)
                ring.wait_read(act, ("xT", 1), t)
                for ci in range(8):
                    k, q = divmod(ci, 4)
                    last = act.copy(X[0:D1].rearrange("p n (r c) -> p (n r) c", c=8)[:, :, ci],
                                    xT[32 * q:32 * q + 32, k, :])
                last.then_inc(s_X, 1)
                for layer in range(2):
                    act.wait_ge(s_diff, t * 2 + (layer + 1))
                    act.activation(prob[layer][:, 1:2], prob[layer][:, 0:1], ACT.Exp).then_inc(s_exp, 1)
                    if layer == 0:
                        for w in range(UP_H):
                            ring.wait_read(act, ("h", w), t)
                            act.activation(h[0:F1, 8 * w:8 * w + 8, :].rearrange("p n o -> p (n o)"),
                                           pre[w % 2][:], ACT.Gelu).then_inc(s_h, 1)
                ring.wait_read(act, ("y", DN_W - 1), t)
                for ci in range(8):
                    k, q = divmod(ci, 4)
                    last = act.copy(yT[32 * q:32 * q + 32, k, :],
                                    y[:].rearrange("p n (r c) -> p (n r) c", c=8)[:, :, ci])
                last.then_inc(s_yT, 1)

        @block.vector
        def _(dve):
            norm_columns(dve, mv, stats, lambda k: env.x[:, k, :], B, T, s_stats, s_var, 1.0, EPS)
            dve.wait_ge(s_rstd, 1)
            dve.wait_ge(loaded, 64)
            dve.wait_ge(zeroed, 15)

            def route(layer, t):
                n = t * 2 + (layer + 1)
                p = prob[layer]
                src = ring.wait_full(dve, ("logits", layer), t)
                dve.tensor_copy(logits[layer][:], src[0:N, 0:E]).then_inc(ring.free(("logits", layer)), 1)
                ring.wait_read(dve, ("logits", layer), t)
                dve.tensor_copy(waited[:, 4 * layer:4 * layer + 1], logits[layer][0:1, 0:1])
                dve.max(top[layer][:], logits[layer][:]).then_inc(s_top, 1)
                dve.wait_ge(s_top, n)
                dve.tensor_tensor(p[:, 0:1], top[layer][:, 1:2], top[layer][:, 0:1], ALU.subtract)\
                    .then_inc(s_diff, 1)
                dve.max_index(which[layer][:], top[layer][:], logits[layer][:]).then_inc(s_which, 1)
                dve.wait_ge(s_which, n)
                dve.tensor_copy(which8[layer][:], which[layer][:, 0:2]).then_inc(s_which8, 1)
                dve.wait_ge(s_exp, n)
                dve.tensor_scalar(p[:, 2:3], p[:, 1:2], 1.0, None, ALU.add).then_inc(s_den, 1)
                dve.wait_ge(s_den, n)
                dve.reciprocal(p[:, 3:4], p[:, 2:3]).then_inc(s_p0, 1)
                dve.wait_ge(s_p0, n)
                dve.tensor_tensor(p[:, 4:5], p[:, 1:2], p[:, 3:4], ALU.mult).then_inc(s_p1, 1)
                dve.wait_ge(s_p1, n)
                dve.tensor_tensor(diag[layer][:], spread(env.ident[0:N, 0:N], 2),
                                  p[:, 3:5].rearrange("p (o k) -> p o k", o=1).to_broadcast([N, N, 2]),
                                  ALU.mult).then_inc(s_diag, 1)
                src = ring.wait_full(dve, ("probs", layer), t)
                dve.tensor_copy(pb[layer][:], src[0:F1, 0:2 * N]).then_inc(ring.free(("probs", layer)), 1)
                ring.wait_read(dve, ("probs", layer), t)

            with dve.Fori(0, PAIRS) as t:
                for par in range(2):
                    b = t * 2 + par
                    xb = env.x[:, bass.ds(b, 1), :].rearrange("p a d -> p (a d)")
                    dve.tensor_scalar(xn[par][:], xb, mv[:, bass.ds(b, 1), 0:1].rearrange("p a o -> p (a o)"),
                                      mv[:, bass.ds(b, 1), 3:4].rearrange("p a o -> p (a o)"),
                                      ALU.subtract, ALU.mult).then_inc(s_xn, 1)
                route(0, t)
                for w in range(UP_W + 1):
                    if w < UP_W:
                        src = ring.wait_full(dve, ("W", w), t)
                        dve.tensor_tensor(W[w % 4][0:D1], src[0:D1, :].rearrange("p (n f) -> p n f", n=8),
                                          spread(pb[0][0:D1, 8 * w:8 * w + 8], F1), ALU.mult)\
                            .then_inc(ring.free(("W", w)), 1)
                    if w >= 2 and w % 2 == 0:
                        m = w // 2 - 1
                        if m >= 2:
                            dve.wait_ge(s_h, t * UP_H + (m - 1))
                        src = ring.wait_full(dve, ("h", m), t)
                        dve.scalar_tensor_tensor(pre[m % 2][:].rearrange("p (n o) -> p n o", n=8),
                                                 src[0:F1, :].rearrange("p (n o) -> p n o", n=8), scale[:, 0:1],
                                                 bias_u[:].rearrange("p (a o) -> p a o", a=1)
                                                 .to_broadcast([F1, 8, F1]), ALU.mult, ALU.add)\
                            .then_inc(ring.free(("h", m)), 1)
                route(1, t)
                for w in range(DN_W + 1):
                    if w < DN_W:
                        src = ring.wait_full(dve, ("W2", w), t)
                        dve.tensor_tensor(W2[w % 4][0:F1], src[0:F1, :].rearrange("p (n f) -> p n f", n=16),
                                          spread(pb[1][:, 16 * w:16 * w + 16], D1), ALU.mult)\
                            .then_inc(ring.free(("W2", w)), 1)
                    if w >= 1:
                        u = w - 1
                        src = ring.wait_full(dve, ("y", u), t)
                        dve.scalar_tensor_tensor(y[:, 8 * u:8 * u + 8, :],
                                                 src[0:D1, 0:8 * D1].rearrange("p (n o) -> p n o", n=8),
                                                 scale[0:D1, 1:2],
                                                 bias_d[:].rearrange("p (a o) -> p a o", a=1)
                                                 .to_broadcast([D1, 8, D1]), ALU.mult, ALU.add)\
                            .then_inc(ring.free(("y", u)), 1)
                for par in range(2):
                    b = t * 2 + par
                    xb = env.x[:, bass.ds(b, 1), :].rearrange("p a d -> p (a d)")
                    src = ring.wait_full(dve, ("back", par), t)
                    dve.tensor_tensor(xb, xb, src[0:T, 0:D], ALU.add).then_inc(ring.free(("back", par)), 1)

        @block.tensor
        def _(pe):
            pe.wait_ge(tables, 80)
            pe.wait_ge(loaded, 64)
            pe.wait_ge(zeroed, 15)
            pe.wait_ge(oned, 1)

            def picked(layer, first, count):
                _, got = nc.values_load_multi_w_load_instructions(
                    row[layer][0:1, first:first + count], engines=[mybir.EngineType.PE],
                    min_val=0, max_val=E - 1,
                    skip_runtime_bounds_check_because="max_index over E logits yields 0 .. E - 1")
                return got

            def probs(layer, t):
                out = ring.wait_free(pe, ("probs", layer), t)
                pe.wait_ge(s_index[layer], t * 16 + 16)
                if layer == 0:
                    pe.wait_ge(s_X, t + 1)
                pe.wait_ge(s_diag, t * 2 + (layer + 1))
                pe.matmul(out[:, 0:2 * N], ones[:], diag[layer][:].rearrange("p n k -> p (n k)"),
                          start=True, stop=True).then_inc(ring.full(("probs", layer)), 1)

            with pe.Fori(0, PAIRS) as t:
                for par in range(2):
                    out = ring.wait_free(pe, ("xT", par), t)
                    pe.wait_ge(s_xn, t * 2 + (par + 1))
                    transposes(pe, env, out, xn[par], T, 128, KC).then_inc(ring.full(("xT", par)), 1)
                out = ring.wait_free(pe, ("logits", 0), t)
                ring.wait_read(pe, ("xT", 1), t)
                for r in range(4):
                    for k in range(KC):
                        last = pe.matmul(out[0:N, 0:E], xT[:, k, r::4], router_up[:, KC * r + k, :],
                                         start=r + k == 0, stop=r == 3 and k == KC - 1)
                last.then_inc(ring.full(("logits", 0)), 1)
                probs(0, t)
                for w in range(UP_W + 1):
                    if w < UP_W:
                        experts = picked(0, 8 * w, 8)
                        out = ring.wait_free(pe, ("W", w), t)
                        for m in range(8):
                            last = pe.matmul(out[0:D1, m * F1:(m + 1) * F1], X[:, 4 * w + m // 2, :],
                                             first_up[:, bass.ds(experts[m], 1), :].rearrange("p a f -> p (a f)"),
                                             start=True, stop=True)
                        last.then_inc(ring.full(("W", w)), 1)
                    if w >= 1:
                        u = w - 1
                        experts = picked(0, 8 * u, 8)
                        out = ring.wait_free(pe, ("h", u // 2), t) if u % 2 == 0 else ring.bank(("h", u // 2))
                        ring.wait_read(pe, ("W", u), t)
                        for m in range(8):
                            at = (u % 2) * 4 + m // 2
                            last = pe.matmul(out[0:F1, at * F1:(at + 1) * F1], W[u % 4][:, m, :],
                                             second_up[:, bass.ds(experts[m], 1), :].rearrange("p a f -> p (a f)"),
                                             start=m % 2 == 0, stop=m % 2 == 1)
                        if u % 2 == 1:
                            last.then_inc(ring.full(("h", u // 2)), 1)
                out = ring.wait_free(pe, ("logits", 1), t)
                pe.wait_ge(s_h, t * UP_H + UP_H)
                for i in range(F1):
                    last = pe.matmul(out[0:N, 0:E], h[:, :, i], router_down[:, i, :],
                                     start=i == 0, stop=i == F1 - 1)
                last.then_inc(ring.full(("logits", 1)), 1)
                probs(1, t)
                for w in range(DN_W + 1):
                    if w < DN_W:
                        experts = picked(1, 16 * w, 16)
                        out = ring.wait_free(pe, ("W2", w), t)
                        for m in range(16):
                            last = pe.matmul(out[0:F1, m * D1:(m + 1) * D1], h[:, 8 * w + m // 2, :],
                                             first_down[:, bass.ds(experts[m], 1), :].rearrange("p a f -> p (a f)"),
                                             start=True, stop=True)
                        last.then_inc(ring.full(("W2", w)), 1)
                    if w >= 1:
                        u = w - 1
                        experts = picked(1, 16 * u, 16)
                        out = ring.wait_free(pe, ("y", u), t)
                        ring.wait_read(pe, ("W2", u), t)
                        for m in range(16):
                            at = m // 2
                            last = pe.matmul(out[0:D1, at * D1:(at + 1) * D1], W2[u % 4][:, m, :],
                                             second_down[:, bass.ds(experts[m], 1), :].rearrange("p a f -> p (a f)"),
                                             start=m % 2 == 0, stop=m % 2 == 1)
                        last.then_inc(ring.full(("y", u)), 1)
                pe.wait_ge(s_yT, t + 1)
                for par in range(2):
                    out = ring.wait_free(pe, ("back", par), t)
                    for k in range(KC):
                        last = pe.transpose(out[0:T, k * 128:(k + 1) * 128], yT[:, k, par * T:(par + 1) * T],
                                            env.ident[:])
                    last.then_inc(ring.full(("back", par)), 1)
        ring.close(PAIRS)


def phase_self_attention_scaled(nc, env, head_mask):
    ctx = ExitStack()
    with ctx:
        sb, sem = tools(nc, ctx, "scaled")
        DH, UNITS = 16, 8
        own = sb("own_features", [128, 8])
        scaled = sb("scaled_features", [128, KC, 8])
        stats = sb("stats", [T, B, 6])
        mv = sb("mean_var", [T, B, 4])
        xn = [sb(f"xn{i}", [T, D]) for i in range(2)]
        v = [sb(f"v{i}", [T, H, DH + 1]) for i in range(2)]
        xT = [sb(f"xT{i}", [128, KC, T]) for i in range(2)]
        km = [sb(f"km{i}", [128, H, T]) for i in range(2)]
        P = [sb(f"P{i}", [T, 4 * T]) for i in range(4)]
        PT = [sb(f"PT{i}", [T, 4 * T]) for i in range(2)]
        mx = sb("max", [T, UNITS, 4])
        rs = sb("recip", [T, UNITS, 4])
        o = [sb(f"o{i}", [T, D]) for i in range(2)]

        loaded, ones = sem("loaded"), sem("ones")
        s_stats, s_var, s_rstd, s_xn, s_own = sem("stats"), sem("var"), sem("rstd"), sem("xn"), sem("own")
        s_v, s_km, s_max, s_exp, s_sum, s_res = sem("v"), sem("km"), sem("max"), sem("exp"), sem("sum"), sem("res")

        units = [(g, par) for g in range(4) for par in range(2)]
        names = [("xT", par) for par in range(2)]
        for u in range(UNITS + 3):
            names += [("S", u)] * (u < UNITS) + [("PT", u - 2)] * (0 <= u - 2 < UNITS) + [("O", u - 3)] * (u >= 3)
        ring = Ring(env, names)
        block = ctx.enter_context(nc.Block())

        @block.sync
        def _(sp):
            sp.dma_start(own[:], head_mask).then_inc(loaded, 16)
            sp.wait_ge(loaded, 16)

        @block.gpsimd
        def _(pool):
            for i in range(2):
                pool.memset(v[i][:], 1.0).then_inc(ones, 1)
            pool.wait_ge(s_var, 1)
            pool.tensor_tensor(mv[:, :, 3], mv[:, :, 2], env.minus_half[0:T, 0:B], ALU.pow).then_inc(s_rstd, 1)

        @block.scalar
        def _(act):
            act.wait_ge(ones, 2)
            with act.Fori(0, PAIRS) as t:
                for par in range(2):
                    src = ring.wait_full(act, ("xT", par), t)
                    act.copy(xT[par][:].rearrange("p k n -> p (k n)"), src[:, 0:KC * T])\
                        .then_inc(ring.free(("xT", par)), 1)
                    act.wait_ge(s_xn, t * 2 + (par + 1))
                    act.copy(v[par][:, :, 0:DH], heads(xn[par][:], H, DH)).then_inc(s_v, 1)
                for u in range(UNITS + 2):
                    if u < UNITS:
                        ring.wait_read(act, ("S", u), t)
                        act.activation(P[u % 4][:], P[u % 4][:], ACT.Exp).then_inc(s_exp, 1)
                    if u >= 2:
                        src = ring.wait_full(act, ("PT", u - 2), t)
                        act.copy(PT[u % 2][:], src[0:T, 0:4 * T]).then_inc(ring.free(("PT", u - 2)), 1)

        @block.vector
        def _(dve):
            dve.wait_ge(loaded, 16)
            for k in range(KC):
                dve.tensor_scalar(scaled[:, k, :], own[:], env.col("rotation", k), env.col("entangle", k),
                                  ALU.mult, ALU.mult).then_inc(s_own, 1)
            norm_columns(dve, mv, stats, lambda k: env.x[:, k, :], B, T, s_stats, s_var, 1.0, EPS)
            dve.wait_ge(s_rstd, 1)
            dve.wait_ge(s_own, 2)
            with dve.Fori(0, PAIRS) as t:
                for par in range(2):
                    b = t * 2 + par
                    xb = env.x[:, bass.ds(b, 1), :].rearrange("p a d -> p (a d)")
                    dve.tensor_scalar(xn[par][:], xb, mv[:, bass.ds(b, 1), 0:1].rearrange("p a o -> p (a o)"),
                                      mv[:, bass.ds(b, 1), 3:4].rearrange("p a o -> p (a o)"),
                                      ALU.subtract, ALU.mult).then_inc(s_xn, 1)
                for par in range(2):
                    ring.wait_read(dve, ("xT", par), t)
                    for k in range(KC):
                        dve.tensor_tensor(km[par][:, 8 * k:8 * k + 8, :],
                                          xT[par][:, k, :].rearrange("p (a n) -> p a n", a=1)
                                          .to_broadcast([128, 8, T]), spread(scaled[:, k, :], T), ALU.mult)\
                            .then_inc(s_km, 1)
                for u in range(UNITS + 3):
                    if u < UNITS:
                        src = ring.wait_full(dve, ("S", u), t)
                        s4 = heads(src[0:T, 0:4 * T], 4, T)
                        dve.tensor_reduce(mx[:, u, :], s4, AX.X, ALU.max).then_inc(s_max, 1)
                        dve.wait_ge(s_max, t * UNITS + (u + 1))
                        dve.tensor_tensor(heads(P[u % 4][:], 4, T), s4, spread(mx[:, u, :], T),
                                          ALU.subtract).then_inc(ring.free(("S", u)), 1)
                    if u >= 3:
                        w = u - 3
                        g, par = units[w]
                        src = ring.wait_full(dve, ("O", w), t)
                        o4 = heads(src[0:T, 0:4 * (DH + 1)], 4, DH + 1)
                        dve.reciprocal(rs[:, w, :], o4[:, :, DH]).then_inc(s_sum, 1)
                        dve.wait_ge(s_sum, t * UNITS + (w + 1))
                        dve.tensor_tensor(heads(o[par][:, g * 4 * DH:(g + 1) * 4 * DH], 4, DH), o4[:, :, 0:DH],
                                          spread(rs[:, w, :], DH), ALU.mult).then_inc(ring.free(("O", w)), 1)
                for par in range(2):
                    b = t * 2 + par
                    xb = env.x[:, bass.ds(b, 1), :].rearrange("p a d -> p (a d)")
                    ring.wait_read(dve, ("O", UNITS - 2 + par), t)
                    dve.tensor_tensor(xb, xb, o[par][:], ALU.add).then_inc(s_res, 1)

        @block.tensor
        def _(pe):
            with pe.Fori(0, PAIRS) as t:
                for par in range(2):
                    out = ring.wait_free(pe, ("xT", par), t)
                    pe.wait_ge(s_xn, t * 2 + (par + 1))
                    transposes(pe, env, out, xn[par], T, 128, KC).then_inc(ring.full(("xT", par)), 1)
                for u in range(UNITS + 3):
                    if u < UNITS:
                        g, par = units[u]
                        out = ring.wait_free(pe, ("S", u), t)
                        pe.wait_ge(s_km, t * 4 + (2 * par + g // 2 + 1))
                        pe.matmul(out[0:T, 0:4 * T], xT[par][:, g // 2, :],
                                  km[par][:, 4 * g:4 * g + 4, :].rearrange("p a b -> p (a b)"),
                                  start=True, stop=True).then_inc(ring.full(("S", u)), 1)
                    if 0 <= u - 2 < UNITS:
                        w = u - 2
                        out = ring.wait_free(pe, ("PT", w), t)
                        pe.wait_ge(s_exp, t * UNITS + (w + 1))
                        transposes(pe, env, out, P[w % 4], T, T, 4).then_inc(ring.full(("PT", w)), 1)
                    if u >= 3:
                        w = u - 3
                        g, par = units[w]
                        out = ring.wait_free(pe, ("O", w), t)
                        ring.wait_read(pe, ("PT", w), t)
                        pe.wait_ge(s_v, t * 2 + (par + 1))
                        for i in range(4):
                            last = pe.matmul(out[0:T, i * (DH + 1):(i + 1) * (DH + 1)],
                                             PT[w % 2][:, i * T:(i + 1) * T], v[par][:, 4 * g + i, :],
                                             start=True, stop=True)
                        last.then_inc(ring.full(("O", w)), 1)
        ring.close(PAIRS)


def phase_cross_attention_queries(nc, env, ctx_rows, head_mask, w_q, w_k, w_v, w_o, b_v, b_o):
    ctx = ExitStack()
    with ctx:
        sb, sem = tools(nc, ctx, "over")
        DH, UNITS, NT = 16, 8, C // CT
        wq, wk, wv, wo = (sb(n, [128, KC, D]) for n in ("w_q", "w_k", "w_v", "w_o"))
        bv = sb("b_v", [CT, D])
        bo = sb("b_o", [T, D])
        own = sb("own_features", [128, 8])
        rows_in = sb("ctx", [CT, B * NT, D])
        rows_now = [sb(f"ctx_now{i}", [CT, NT, D]) for i in range(2)]
        stats = sb("stats", [T, B, 6])
        mv = sb("mean_var", [T, B, 4])
        xn = [sb(f"xn{i}", [T, D]) for i in range(2)]
        xT = [sb(f"xT{i}", [128, KC, T]) for i in range(2)]
        qT = [sb(f"qT{i}", [128, KC, T]) for i in range(2)]
        qm = [sb(f"qm{i}", [128, H, T]) for i in range(2)]
        cT = [sb(f"cT{i}", [128, KC, C]) for i in range(2)]
        kT = [sb(f"kT{i}", [128, KC, C]) for i in range(2)]
        v = [sb(f"v{i}", [CT, NT, D]) for i in range(2)]
        P = [sb(f"P{i}", [CT, 4 * T]) for i in range(6)]
        V = [sb(f"V{i}", [CT, 4 * DH]) for i in range(6)]
        SUB = UNITS * NT
        mx = sb("max", [CT, SUB, 4])
        rs = sb("recip", [CT, SUB, 8])
        o = [sb(f"o{i}", [T, D]) for i in range(2)]
        oT = [sb(f"oT{i}", [128, KC, T]) for i in range(2)]
        res = [sb(f"res{i}", [T, D]) for i in range(2)]

        loaded = sem("loaded")
        s_stats, s_var, s_rstd, s_xn = sem("stats"), sem("var"), sem("rstd"), sem("xn")
        s_rows = sem("rows")
        s_qm, s_max, s_exp, s_den, s_rec, s_V, s_res = (sem(n) for n in ("qm", "max", "exp", "den", "rec", "V", "res"))

        units = [(g, par) for g in range(4) for par in range(2)]
        names = [("xT", 0), ("xT", 1)]
        names += [("cT", par, c) for par in range(2) for c in range(NT)]
        names += [("qT", 0), ("qT", 1)]
        names += [("kT", par, m) for par in range(2) for m in range(KC)]
        names += [("v", par, c) for par in range(2) for c in range(NT)]
        for u in range(SUB + 3):
            names += [("S", u)] * (u < SUB) + [("O", u // 3 - 1)] * (u >= 3 and u % 3 == 2)
        names += [("oT", 0), ("oT", 1), ("out", 0), ("out", 1)]
        ring = Ring(env, names)
        block = ctx.enter_context(nc.Block())

        @block.sync
        def _(sp):
            sp.dma_start(own[:], head_mask).then_inc(loaded, 16)
            for w, src in ((wq, w_q), (wk, w_k), (wv, w_v), (wo, w_o)):
                sp.dma_start(w[:], src.rearrange("(k p) n -> p k n", p=128)).then_inc(loaded, 16)
            sp.dma_start(bv[:], b_v.rearrange("(o d) -> o d", o=1).to_broadcast([CT, D])).then_inc(loaded, 16)
            sp.dma_start(bo[:], b_o.rearrange("(o d) -> o d", o=1).to_broadcast([T, D])).then_inc(loaded, 16)
            sp.dma_start(rows_in[:], ctx_rows.rearrange("b (c p) d -> p (b c) d", p=CT)).then_inc(loaded, 16)
            sp.wait_ge(loaded, 128)

        @block.gpsimd
        def _(pool):
            pool.wait_ge(s_var, 1)
            pool.tensor_tensor(mv[:, :, 3], mv[:, :, 2], env.minus_half[0:T, 0:B], ALU.pow).then_inc(s_rstd, 1)

        @block.scalar
        def _(act):
            with act.Fori(0, PAIRS) as t:
                for par in range(2):
                    src = ring.wait_full(act, ("xT", par), t)
                    act.copy(xT[par][:].rearrange("p k n -> p (k n)"), src[:, 0:KC * T])\
                        .then_inc(ring.free(("xT", par)), 1)
                for par in range(2):
                    for c in range(NT):
                        src = ring.wait_full(act, ("cT", par, c), t)
                        act.copy(cT[par][:, :, c * CT:(c + 1) * CT],
                                 src[:, 0:KC * CT].rearrange("p (k n) -> p k n", k=KC))\
                            .then_inc(ring.free(("cT", par, c)), 1)
                for par in range(2):
                    src = ring.wait_full(act, ("qT", par), t)
                    for m in range(KC):
                        last = act.activation(qT[par][:, m, :], src[:, m * T:(m + 1) * T], ACT.Identity,
                                              bias=env.col("bq", m))
                    last.then_inc(ring.free(("qT", par)), 1)
                for par in range(2):
                    for m in range(KC):
                        src = ring.wait_full(act, ("kT", par, m), t)
                        act.activation(kT[par][:, m, :], src[:, 0:C], ACT.Identity, bias=env.col("bk", m))\
                            .then_inc(ring.free(("kT", par, m)), 1)
                for u in range(SUB + 4):
                    if u < SUB:
                        ring.wait_read(act, ("S", u), t)
                        act.activation(P[u % 6][:], P[u % 6][:], ACT.Exp, scale=DH ** -0.5).then_inc(s_exp, 1)
                    if u >= 5 and u % 3 == 2:
                        w = u // 3 - 1
                        g, par = units[w]
                        src = ring.wait_full(act, ("O", w), t)
                        act.copy(o[par][:, g * 4 * DH:(g + 1) * 4 * DH], src[0:T, 0:4 * DH])\
                            .then_inc(ring.free(("O", w)), 1)
                for par in range(2):
                    src = ring.wait_full(act, ("oT", par), t)
                    act.copy(oT[par][:].rearrange("p k n -> p (k n)"), src[:, 0:KC * T])\
                        .then_inc(ring.free(("oT", par)), 1)

        @block.vector
        def _(dve):
            norm_columns(dve, mv, stats, lambda k: env.x[:, k, :], B, T, s_stats, s_var, 1.0, EPS)
            dve.wait_ge(s_rstd, 1)
            dve.wait_ge(loaded, 128)
            with dve.Fori(0, PAIRS) as t:
                for par in range(2):
                    b = t * 2 + par
                    xb = env.x[:, bass.ds(b, 1), :].rearrange("p a d -> p (a d)")
                    dve.tensor_scalar(xn[par][:], xb, mv[:, bass.ds(b, 1), 0:1].rearrange("p a o -> p (a o)"),
                                      mv[:, bass.ds(b, 1), 3:4].rearrange("p a o -> p (a o)"),
                                      ALU.subtract, ALU.mult).then_inc(s_xn, 1)
                for par in range(2):
                    for c in range(NT):
                        row = rows_in[:, bass.ds((t * 2 + par) * NT + c, 1), :].rearrange("p a d -> p (a d)")
                        dve.tensor_copy(rows_now[par][:, c, :], row).then_inc(s_rows, 1)
                for par in range(2):
                    ring.wait_read(dve, ("qT", par), t)
                    for k in range(KC):
                        dve.tensor_tensor(qm[par][:, 8 * k:8 * k + 8, :],
                                          qT[par][:, k, :].rearrange("p (a n) -> p a n", a=1)
                                          .to_broadcast([128, 8, T]), spread(own[:], T), ALU.mult)\
                            .then_inc(s_qm, 1)
                for par in range(2):
                    for c in range(NT):
                        src = ring.wait_full(dve, ("v", par, c), t)
                        dve.tensor_tensor(v[par][:, c, :], src[0:CT, 0:D], bv[:], ALU.add)\
                            .then_inc(ring.free(("v", par, c)), 1)
                for u in range(SUB + 1):
                    if u < SUB:
                        if u >= 6:
                            ring.wait_full(dve, ("O", u // 3 - 2), t)
                        src = ring.wait_full(dve, ("S", u), t)
                        s4 = heads(src[0:CT, 0:4 * T], 4, T)
                        dve.tensor_reduce(mx[:, u, :], s4, AX.X, ALU.max).then_inc(s_max, 1)
                        dve.wait_ge(s_max, t * SUB + (u + 1))
                        dve.tensor_tensor(heads(P[u % 6][:], 4, T), s4, spread(mx[:, u, :], T),
                                          ALU.subtract).then_inc(ring.free(("S", u)), 1)
                    if u >= 1:
                        w = u - 1
                        g, par = units[w // 3]
                        n = t * SUB + (w + 1)
                        dve.wait_ge(s_exp, n)
                        dve.tensor_reduce(rs[:, w, 0:4], heads(P[w % 6][:], 4, T), AX.X, ALU.add).then_inc(s_den, 1)
                        dve.wait_ge(s_den, n)
                        dve.reciprocal(rs[:, w, 4:8], rs[:, w, 0:4]).then_inc(s_rec, 1)
                        dve.wait_ge(s_rec, n)
                        if w == 0:
                            ring.wait_read(dve, ("v", 1, NT - 1), t)
                        dve.tensor_tensor(heads(V[w % 6][:], 4, DH),
                                          heads(v[par][:, w % 3, g * 4 * DH:(g + 1) * 4 * DH], 4, DH),
                                          spread(rs[:, w, 4:8], DH), ALU.mult).then_inc(s_V, 1)
                for par in range(2):
                    b = t * 2 + par
                    xb = env.x[:, bass.ds(b, 1), :].rearrange("p a d -> p (a d)")
                    src = ring.wait_full(dve, ("out", par), t)
                    dve.tensor_tensor(res[par][:], bo[:], src[0:T, 0:D], ALU.add).then_inc(ring.free(("out", par)), 1)
                    ring.wait_read(dve, ("out", par), t)
                    dve.tensor_tensor(xb, xb, res[par][:], ALU.add).then_inc(s_res, 1)

        @block.tensor
        def _(pe):
            pe.wait_ge(loaded, 128)
            with pe.Fori(0, PAIRS) as t:
                for par in range(2):
                    out = ring.wait_free(pe, ("xT", par), t)
                    pe.wait_ge(s_xn, t * 2 + (par + 1))
                    transposes(pe, env, out, xn[par], T, 128, KC).then_inc(ring.full(("xT", par)), 1)
                for par in range(2):
                    for c in range(NT):
                        out = ring.wait_free(pe, ("cT", par, c), t)
                        pe.wait_ge(s_rows, t * 2 * NT + (par * NT + c + 1))
                        transposes(pe, env, out, rows_now[par][:, c, :], CT, 128, KC)\
                            .then_inc(ring.full(("cT", par, c)), 1)
                for par in range(2):
                    out = ring.wait_free(pe, ("qT", par), t)
                    ring.wait_read(pe, ("xT", par), t)
                    for m in range(KC):
                        for k in range(KC):
                            last = pe.matmul(out[:, m * T:(m + 1) * T], wq[:, k, m * 128:(m + 1) * 128],
                                             xT[par][:, k, :], start=k == 0, stop=k == KC - 1)
                    last.then_inc(ring.full(("qT", par)), 1)
                for par in range(2):
                    for m in range(KC):
                        out = ring.wait_free(pe, ("kT", par, m), t)
                        ring.wait_read(pe, ("cT", par, NT - 1), t)
                        for k in range(KC):
                            last = pe.matmul(out[:, 0:C], wk[:, k, m * 128:(m + 1) * 128], cT[par][:, k, :],
                                             start=k == 0, stop=k == KC - 1)
                        last.then_inc(ring.full(("kT", par, m)), 1)
                for par in range(2):
                    for c in range(NT):
                        out = ring.wait_free(pe, ("v", par, c), t)
                        for k in range(KC):
                            last = pe.matmul(out[0:CT, 0:D], cT[par][:, k, c * CT:(c + 1) * CT], wv[:, k, :],
                                             start=k == 0, stop=k == KC - 1)
                        last.then_inc(ring.full(("v", par, c)), 1)
                for u in range(SUB + 3):
                    if u < SUB:
                        g, par = units[u // 3]
                        c = u % 3
                        out = ring.wait_free(pe, ("S", u), t)
                        if c == 0:
                            pe.wait_ge(s_qm, t * 4 + (2 * par + g // 2 + 1))
                            ring.wait_read(pe, ("kT", par, g // 2), t)
                        pe.matmul(out[0:CT, 0:4 * T], kT[par][:, g // 2, c * CT:(c + 1) * CT],
                                  qm[par][:, 4 * g:4 * g + 4, :].rearrange("p a b -> p (a b)"),
                                  start=True, stop=True).then_inc(ring.full(("S", u)), 1)
                    if u >= 3 and u % 3 == 2:
                        w = u // 3 - 1
                        out = ring.wait_free(pe, ("O", w), t)
                        pe.wait_ge(s_V, t * SUB + (3 * w + 3))
                        for i in range(4):
                            for c in range(NT):
                                n = (3 * w + c) % 6
                                last = pe.matmul(out[0:T, i * DH:(i + 1) * DH], P[n][:, i * T:(i + 1) * T],
                                                 V[n][:, i * DH:(i + 1) * DH], start=c == 0, stop=c == NT - 1)
                        last.then_inc(ring.full(("O", w)), 1)
                for par in range(2):
                    out = ring.wait_free(pe, ("oT", par), t)
                    ring.wait_read(pe, ("O", UNITS - 2 + par), t)
                    transposes(pe, env, out, o[par], T, 128, KC).then_inc(ring.full(("oT", par)), 1)
                for par in range(2):
                    out = ring.wait_free(pe, ("out", par), t)
                    ring.wait_read(pe, ("oT", par), t)
                    for k in range(KC):
                        last = pe.matmul(out[0:T, 0:D], oT[par][:, k, :], wo[:, k, :], start=k == 0, stop=k == KC - 1)
                    last.then_inc(ring.full(("out", par)), 1)
        ring.close(PAIRS)


def phase_attention_over_sequences(nc, env, w_in, w_out, b_v, b_out, ln_g, ln_b, block_bias):
    ctx = ExitStack()
    with ctx:
        sb, sem = tools(nc, ctx, "mha")
        NH, DH, BL = 4, 64, T * B // 128
        win = sb("w_in", [128, KC, 3 * D])
        wo = sb("w_out", [128, KC, D])
        bv = sb("b_v", [128, D])
        bo = sb("b_out", [T, D])
        g1 = sb("ln_gamma", [T, D])
        b1 = sb("ln_beta", [T, D])
        own = sb("block_bias", [128, 128])
        xT = sb("xT", [128, KC, T, B])
        qkT = sb("qkT", [128, 4, T * B])
        v = sb("v", [128, BL, NH, DH + 1])
        P = [sb(f"P{i}", [128, NH * 128]) for i in range(4)]
        PT = [sb(f"PT{i}", [128, NH * 128]) for i in range(2)]
        mx = sb("max", [128, BL, NH])
        rs = sb("recip", [128, BL, NH])
        o = [sb(f"o{i}", [128, D]) for i in range(2)]
        oT = sb("oT", [128, KC, B, T])
        res = [sb(f"res{i}", [T, D]) for i in range(2)]
        stats = sb("stats", [T, B, 6])
        mv = sb("mean_var", [T, B, 4])
        stats0 = sb("stats_in", [T, B, 6])
        mv0 = sb("mean_var_in", [T, B, 4])
        z = [sb(f"z{i}", [T, D]) for i in range(2)]

        loaded, ones = sem("loaded"), sem("ones")
        s_add, s_max, s_sub, s_exp, s_sum = (sem(n) for n in ("add", "max", "sub", "exp", "sum"))
        s_stats0, s_var0, s_rstd0, s_in = (sem(n) for n in ("stats_in", "var_in", "rstd_in", "normed_in"))
        s_res, s_stats, s_var, s_rstd, s_z, s_g, s_y = (sem(n) for n in ("res", "stats", "var", "rstd", "z", "g", "y"))

        names = [("xT", b) for b in range(B)]
        names += [("qkT", m, n) for n in range(2) for m in range(4)]
        names += [("v", u) for u in range(BL)]
        for u in range(BL + 4):
            names += [("S", u, 0), ("S", u, 1)] * (u < BL) + [("PT", u - 2)] * (0 <= u - 2 < BL)
            names += [("O", u - 3)] * (0 <= u - 3 < BL) + [("oT", u - 4)] * (u >= 4)
        names += [("out", b) for b in range(B)]
        ring = Ring(env, names)
        block = ctx.enter_context(nc.Block())

        def rows(ap, n):
            return ap.rearrange("(o d) -> o d", o=1).to_broadcast([n, D])

        @block.sync
        def _(sp):
            sp.dma_start(win[:], w_in.rearrange("(k p) n -> p k n", p=128)).then_inc(loaded, 16)
            sp.dma_start(wo[:], w_out.rearrange("(k p) n -> p k n", p=128)).then_inc(loaded, 16)
            sp.dma_start(own[:], block_bias).then_inc(loaded, 16)
            sp.dma_start(bv[:], rows(b_v, 128)).then_inc(loaded, 16)
            for dst, src in ((bo, b_out), (g1, ln_g), (b1, ln_b)):
                sp.dma_start(dst[:], rows(src, T)).then_inc(loaded, 16)
            sp.wait_ge(loaded, 112)

        @block.gpsimd
        def _(pool):
            pool.memset(v[:], 1.0).then_inc(ones, 1)
            pool.wait_ge(s_var0, 1)
            pool.tensor_tensor(mv0[:, :, 3], mv0[:, :, 2], env.minus_half[0:T, 0:B], ALU.pow).then_inc(s_rstd0, 1)
            pool.wait_ge(s_var, 1)
            pool.tensor_tensor(mv[:, :, 3], mv[:, :, 2], env.minus_half[0:T, 0:B], ALU.pow).then_inc(s_rstd, 1)

        @block.scalar
        def _(act):
            for b in range(B):
                src = ring.wait_full(act, ("xT", b), 0)
                act.copy(xT[:, :, :, b], src[:, 0:KC * T].rearrange("p (k n) -> p k n", k=KC))\
                    .then_inc(ring.free(("xT", b)), 1)
            for n in range(2):
                for m in range(4):
                    src = ring.wait_full(act, ("qkT", m, n), 0)
                    act.activation(qkT[:, m, n * 448:(n + 1) * 448], src[:, 0:448], ACT.Identity,
                                   bias=env.col("in_proj_b", m)).then_inc(ring.free(("qkT", m, n)), 1)
            for u in range(BL + 4):
                if u < BL:
                    act.wait_ge(s_sub, u + 1)
                    act.activation(P[u % 4][:], P[u % 4][:], ACT.Exp, scale=DH ** -0.5).then_inc(s_exp, 1)
                if 0 <= u - 2 < BL:
                    src = ring.wait_full(act, ("PT", u - 2), 0)
                    act.copy(PT[u % 2][:], src[:, :]).then_inc(ring.free(("PT", u - 2)), 1)
                if u >= 4:
                    w = u - 4
                    src = ring.wait_full(act, ("oT", w), 0)
                    for k in range(KC):
                        last = act.copy(oT[:, k, :, 16 * w:16 * w + 16].rearrange("p l n -> p n l"),
                                        src[:, k * 128:(k + 1) * 128].rearrange("p (n l) -> p n l", l=B))
                    last.then_inc(ring.free(("oT", w)), 1)

        @block.vector
        def _(dve):
            norm_columns(dve, mv0, stats0, lambda k: env.x[:, k, :], B, T, s_stats0, s_var0, 1.0, EPS)
            dve.wait_ge(s_rstd0, 1)
            for b in range(B):
                dve.tensor_scalar(env.y[:, b, :], env.x[:, b, :], mv0[:, b, 0:1], mv0[:, b, 3:4],
                                  ALU.subtract, ALU.mult).then_inc(s_in, 1)
            dve.wait_ge(loaded, 112)
            dve.wait_ge(ones, 1)
            for u in range(BL):
                src = ring.wait_full(dve, ("v", u), 0)
                dve.tensor_tensor(v[:, u, :, 0:DH], heads(src[:, 0:D], NH, DH), heads(bv[:], NH, DH), ALU.add)\
                    .then_inc(ring.free(("v", u)), 1)
            for u in range(BL + 3):
                if u < BL:
                    p4 = heads(P[u % 4][:], NH, 128)
                    for a in range(2):
                        src = ring.wait_full(dve, ("S", u, a), 0)
                        dve.tensor_tensor(p4[:, 2 * a:2 * a + 2, :], heads(src[:, 0:256], 2, 128),
                                          own[:].rearrange("p (a n) -> p a n", a=1).to_broadcast([128, 2, 128]),
                                          ALU.add).then_inc(ring.free(("S", u, a)), 1)
                        ring.wait_read(dve, ("S", u, a), 0)
                    dve.tensor_reduce(mx[:, u, :], p4, AX.X, ALU.max).then_inc(s_max, 1)
                    dve.wait_ge(s_max, u + 1)
                    dve.tensor_tensor(p4, p4, spread(mx[:, u, :], 128), ALU.subtract).then_inc(s_sub, 1)
                if u >= 3:
                    w = u - 3
                    src = ring.wait_full(dve, ("O", w), 0)
                    o4 = heads(src[:, 0:NH * (DH + 1)], NH, DH + 1)
                    dve.reciprocal(rs[:, w, :], o4[:, :, DH]).then_inc(s_sum, 1)
                    dve.wait_ge(s_sum, w + 1)
                    dve.tensor_tensor(heads(o[w % 2][:], NH, DH), o4[:, :, 0:DH], spread(rs[:, w, :], DH),
                                      ALU.mult).then_inc(ring.free(("O", w)), 1)
            for b in range(B):
                src = ring.wait_full(dve, ("out", b), 0)
                if b >= 2:
                    dve.wait_ge(s_res, b - 1)
                dve.tensor_tensor(res[b % 2][:], bo[:], src[0:T, 0:D], ALU.add).then_inc(ring.free(("out", b)), 1)
                ring.wait_read(dve, ("out", b), 0)
                dve.tensor_tensor(env.y[:, b, :], env.y[:, b, :], res[b % 2][:], ALU.add).then_inc(s_res, 1)
            dve.wait_ge(s_res, B)
            norm_columns(dve, mv, stats, lambda k: env.y[:, k, :], B, T, s_stats, s_var, 1.0, EPS)
            dve.wait_ge(s_rstd, 1)
            normalise_rows(dve, env, mv, z, g1, b1, s_z, s_g, s_y)

        @block.tensor
        def _(pe):
            pe.wait_ge(loaded, 112)
            for b in range(B):
                out = ring.wait_free(pe, ("xT", b), 0)
                pe.wait_ge(s_in, b + 1)
                transposes(pe, env, out, env.y[:, b, :], T, 128, KC).then_inc(ring.full(("xT", b)), 1)
            for b in range(B):
                ring.wait_read(pe, ("xT", b), 0)
            cols = xT[:].rearrange("p k n l -> p k (n l)")
            for n in range(2):
                for m in range(4):
                    out = ring.wait_free(pe, ("qkT", m, n), 0)
                    for k in range(KC):
                        last = pe.matmul(out[:, 0:448], win[:, k, m * 128:(m + 1) * 128],
                                         cols[:, k, n * 448:(n + 1) * 448], start=k == 0, stop=k == KC - 1)
                    last.then_inc(ring.full(("qkT", m, n)), 1)
            for u in range(BL):
                out = ring.wait_free(pe, ("v", u), 0)
                for k in range(KC):
                    last = pe.matmul(out[:, 0:D], cols[:, k, u * 128:(u + 1) * 128], win[:, k, 2 * D:3 * D],
                                     start=k == 0, stop=k == KC - 1)
                last.then_inc(ring.full(("v", u)), 1)
            for n in range(2):
                for m in range(4):
                    ring.wait_read(pe, ("qkT", m, n), 0)
            for u in range(BL + 4):
                if u < BL:
                    for a in range(2):
                        out = ring.wait_free(pe, ("S", u, a), 0)
                        rows_a = slice(64 * a, 64 * a + 64)
                        for j in range(2):
                            last = pe.matmul(out[:, j * 128:(j + 1) * 128],
                                             qkT[rows_a, j, u * 128:(u + 1) * 128],
                                             qkT[rows_a, 2 + j, u * 128:(u + 1) * 128], start=True, stop=True)
                        last.then_inc(ring.full(("S", u, a)), 1)
                if 0 <= u - 2 < BL:
                    w = u - 2
                    out = ring.wait_free(pe, ("PT", w), 0)
                    pe.wait_ge(s_exp, w + 1)
                    transposes(pe, env, out, P[w % 4], 128, 128, NH).then_inc(ring.full(("PT", w)), 1)
                if 0 <= u - 3 < BL:
                    w = u - 3
                    out = ring.wait_free(pe, ("O", w), 0)
                    ring.wait_read(pe, ("PT", w), 0)
                    ring.wait_read(pe, ("v", w), 0)
                    for h in range(NH):
                        i = (h % 2) * 2 + h // 2
                        last = pe.matmul(out[:, h * (DH + 1):(h + 1) * (DH + 1)],
                                         PT[w % 2][:, i * 128:(i + 1) * 128], v[:, w, h, :], start=True, stop=True)
                    last.then_inc(ring.full(("O", w)), 1)
                if u >= 4:
                    w = u - 4
                    out = ring.wait_free(pe, ("oT", w), 0)
                    ring.wait_read(pe, ("O", w), 0)
                    transposes(pe, env, out, o[w % 2], 128, 128, KC).then_inc(ring.full(("oT", w)), 1)
            ring.wait_read(pe, ("oT", BL - 1), 0)
            for b in range(B):
                out = ring.wait_free(pe, ("out", b), 0)
                for k in range(KC):
                    last = pe.matmul(out[0:T, 0:D], oT[:, k, b, :], wo[:, k, :], start=k == 0, stop=k == KC - 1)
                last.then_inc(ring.full(("out", b)), 1)
        ring.close(1)


def normalise_rows(dve, env, mv, z, gamma, beta, s_z, s_g, s_y):
    for b in range(B):
        if b >= 2:
            dve.wait_ge(s_y, b - 1)
        dve.tensor_scalar(z[b % 2][:], env.y[:, b, :], mv[:, b, 0:1], mv[:, b, 3:4],
                          ALU.subtract, ALU.mult).then_inc(s_z, 1)
        dve.wait_ge(s_z, b + 1)
        dve.tensor_tensor(z[b % 2][:], z[b % 2][:], gamma[:], ALU.mult).then_inc(s_g, 1)
        dve.wait_ge(s_g, b + 1)
        dve.tensor_tensor(env.y[:, b, :], z[b % 2][:], beta[:], ALU.add).then_inc(s_y, 1)


def phase_capacity_experts(nc, env, out, w_gate, w1, w2, b2, ln_g, ln_b, slots, slot_ids, iota8, before):
    ctx = ExitStack()
    with ctx:
        sb, sem = tools(nc, ctx, "moe")
        E, CAP, FF, WB = 8, B * T // 8, 1024, 4
        FC = FF // 128
        wg = sb("w_gate", [128, KC, E])
        w1_sb = [sb(f"w1_{i}", [128, KC, FF]) for i in range(WB)]
        w2_sb = [sb(f"w2_{i}", [128, FC, D]) for i in range(WB)]
        b2_sb = sb("b2", [CAP, E, D])
        g2 = sb("ln_gamma", [T, D])
        be2 = sb("ln_beta", [T, D])
        slot_row = sb("slot_row", [T, E * CAP])
        slot_id = sb("slot_id", [CAP, E])
        io = sb("iota8", [T, E])
        earlier = sb("earlier", [T, T])
        ones = sb("ones", [T, T])
        yT = sb("yT", [128, KC, B, T])
        logits = sb("logits", [T, B, E])
        mx = sb("max", [T, B])
        eq = sb("eq", [T, B, E])
        cand = sb("cand", [T, B, E])
        best = sb("best", [T, B])
        hot = sb("one_hot", [T, B, E])
        ex = sb("exp", [T, B, E])
        gate = sb("gate", [T, B, 2])
        loc = sb("loc", [T, B])
        lochot = sb("lochot", [T, B, E])
        over = sb("over", [T, B])
        slot = sb("slot", [T, B])
        Pm = sb("into_slots", [T, B, E * CAP])
        diag = [sb(f"diag{i}", [T, T]) for i in range(B)]
        srow = sb("slot_of_token", [CAP, B * T])
        R = sb("from_slots", [CAP, E, B * T])
        dT = sb("dispatched", [128, KC, E * CAP])
        hT = [sb(f"hT{i}", [128, FC, CAP]) for i in range(2)]
        ys = sb("expert_out", [CAP, E, D])
        stats = sb("stats", [T, B, 6])
        mv = sb("mean_var", [T, B, 4])
        z = [sb(f"z{i}", [T, D]) for i in range(2)]

        loaded, s_ones, stored, s_end = sem("loaded"), sem("ones"), sem("stored"), sem("end")
        w_in = [sem(f"w_in{i}") for i in range(WB)]
        chain = sem("routing_step")
        s_sub, s_exp, s_hot, s_slot, s_P, s_diag, s_R = (sem(n) for n in ("sub", "exp", "hot", "slot", "P", "diag", "R"))
        s_res, s_stats, s_var, s_rstd, s_z, s_g, s_y = (sem(n) for n in ("res", "stats", "var", "rstd", "z", "g", "y"))
        HALF = E * CAP // 2

        names = [("yT", b) for b in range(B)] + [("logits", 0), ("loc", 0), ("row", 0), ("row", 1)]
        names += [("d", n, k) for n in range(2) for k in range(KC)]
        ring = Ring(env, names)
        ring.close(1)
        TURNS = E // WB
        names = [("h", 0, 0), ("h", 0, 1)]
        for i in range(WB):
            names += [("h", i + 1, 0), ("h", i + 1, 1)] * (i + 1 < WB) + [("y", i)]
        work = Ring(env, names)
        work.close(TURNS)
        back = Ring(env, [("x", b) for b in range(B)])
        back.close(1)
        block = ctx.enter_context(nc.Block())

        @block.sync
        def _(sp):
            for dst, src in ((wg, w_gate.rearrange("(k p) n -> p k n", p=128)),
                             (b2_sb, b2.rearrange("(o e) d -> o e d", o=1).to_broadcast([CAP, E, D])),
                             (g2, ln_g.rearrange("(o d) -> o d", o=1).to_broadcast([T, D])),
                             (be2, ln_b.rearrange("(o d) -> o d", o=1).to_broadcast([T, D])),
                             (slot_row, slots.rearrange("(o d) -> o d", o=1).to_broadcast([T, E * CAP])),
                             (slot_id, slot_ids),
                             (io, iota8.rearrange("(o d) -> o d", o=1).to_broadcast([T, E])),
                             (earlier, before)):
                sp.dma_start(dst[:], src).then_inc(loaded, 16)
            for e in range(WB):
                sp.dma_start(w1_sb[e][:], w1[e].rearrange("(k p) n -> p k n", p=128)).then_inc(w_in[e], 16)
                sp.dma_start(w2_sb[e][:], w2[e].rearrange("(k p) n -> p k n", p=128)).then_inc(w_in[e], 16)
            for e in range(WB, E):
                work.wait_full(sp, ("y", e - WB), 0)
                sp.dma_start(w1_sb[e - WB][:], w1[e].rearrange("(k p) n -> p k n", p=128)).then_inc(w_in[e - WB], 16)
                sp.dma_start(w2_sb[e - WB][:], w2[e].rearrange("(k p) n -> p k n", p=128)).then_inc(w_in[e - WB], 16)
            for b in range(B):
                sp.wait_ge(s_end, b + 1)
                sp.dma_start(out[b], env.x[:, b, :]).then_inc(stored, 16)
            sp.wait_ge(stored, 16 * B)

        @block.gpsimd
        def _(pool):
            pool.memset(ones[:], 1.0).then_inc(s_ones, 1)
            pool.wait_ge(s_var, 1)
            pool.tensor_tensor(mv[:, :, 3], mv[:, :, 2], env.minus_half[0:T, 0:B], ALU.pow).then_inc(s_rstd, 1)

        @block.scalar
        def _(act):
            for b in range(B):
                src = ring.wait_full(act, ("yT", b), 0)
                act.copy(yT[:, :, b, :], src[:, 0:KC * T].rearrange("p (k n) -> p k n", k=KC))\
                    .then_inc(ring.free(("yT", b)), 1)
            act.wait_ge(s_sub, 1)
            act.activation(ex[:], ex[:], ACT.Exp).then_inc(s_exp, 1)
            for n in range(2):
                src = ring.wait_full(act, ("row", n), 0)
                act.copy(srow[:, n * HALF:(n + 1) * HALF], src[0:CAP, 0:HALF]).then_inc(ring.free(("row", n)), 1)
            for n in range(2):
                for k in range(KC):
                    src = ring.wait_full(act, ("d", n, k), 0)
                    act.copy(dT[:, k, n * HALF:(n + 1) * HALF], src[:, 0:HALF]).then_inc(ring.free(("d", n, k)), 1)

        @block.vector
        def _(dve):
            steps = [0]

            def step(op):
                steps[0] += 1
                op.then_inc(chain, 1)
                dve.wait_ge(chain, steps[0])

            dve.wait_ge(loaded, 128)
            per_expert = io[:].rearrange("p (b e) -> p b e", b=1).to_broadcast([T, B, E])
            src = ring.wait_full(dve, ("logits", 0), 0)
            dve.tensor_copy(logits[:], src[0:T, 0:B * E].rearrange("p (b e) -> p b e", b=B))\
                .then_inc(ring.free(("logits", 0)), 1)
            ring.wait_read(dve, ("logits", 0), 0)
            step(dve.tensor_reduce(mx[:], logits[:], AX.X, ALU.max))
            dve.tensor_tensor(ex[:], logits[:], spread(mx[:], E), ALU.subtract).then_inc(s_sub, 1)
            step(dve.tensor_tensor(eq[:], logits[:], spread(mx[:], E), ALU.is_equal))
            step(dve.scalar_tensor_tensor(cand[:], eq[:], -float(E), per_expert, ALU.mult, ALU.add))
            step(dve.tensor_reduce(best[:], cand[:], AX.X, ALU.min))
            step(dve.tensor_scalar(best[:], best[:], float(E), None, ALU.add))
            dve.tensor_tensor(hot[:], per_expert, spread(best[:], E), ALU.is_equal).then_inc(s_hot, 1)
            dve.wait_ge(s_hot, 1)
            dve.wait_ge(s_exp, 1)
            step(dve.tensor_reduce(gate[:, :, 0], ex[:], AX.X, ALU.add))
            step(dve.reciprocal(gate[:, :, 1], gate[:, :, 0]))
            src = ring.wait_full(dve, ("loc", 0), 0)
            dve.tensor_tensor(lochot[:], src[0:T, 0:B * E].rearrange("p (b e) -> p b e", b=B), hot[:], ALU.mult)\
                .then_inc(ring.free(("loc", 0)), 1)
            ring.wait_read(dve, ("loc", 0), 0)
            step(dve.tensor_reduce(loc[:], lochot[:], AX.X, ALU.add))
            step(dve.tensor_scalar(over[:], loc[:], float(CAP), float(4 * E * CAP), ALU.is_ge, ALU.mult))
            step(dve.scalar_tensor_tensor(slot[:], best[:], float(CAP), loc[:], ALU.mult, ALU.add))
            step(dve.tensor_tensor(slot[:], slot[:], over[:], ALU.add))
            for b in range(B):
                dve.tensor_scalar(diag[b][:], env.ident[0:T, 0:T], slot[:, b:b + 1], None, ALU.mult)\
                    .then_inc(s_diag, 1)
            for b in range(B):
                dve.tensor_scalar(Pm[:, b, :], slot_row[:], slot[:, b:b + 1], None, ALU.is_equal).then_inc(s_P, 1)
            ring.wait_read(dve, ("row", 0), 0)
            ring.wait_read(dve, ("row", 1), 0)
            for e in range(E):
                dve.tensor_scalar(R[:, e, :], srow[:], slot_id[:, e:e + 1], None, ALU.is_equal).then_inc(s_R, 1)

            b1_at = env.column_at("b1")
            with dve.Fori(0, TURNS) as t:
                for i in range(WB + 1):
                    if i < WB:
                        e = t * WB + i
                        for a in range(2):
                            src = work.wait_full(dve, ("h", i, a), t)
                            b1 = env.columns[:, bass.ds(e * FC + (b1_at + 4 * a), 4)]
                            dve.tensor_tensor(hT[i % 2][:, 4 * a:4 * a + 4, :], heads(src[:, 0:4 * CAP], 4, CAP),
                                              spread(b1, CAP), ALU.add).then_inc(work.free(("h", i, a)), 1)
                    if i >= 1:
                        e = t * WB + (i - 1)
                        src = work.wait_full(dve, ("y", i - 1), t)
                        dve.tensor_tensor(ys[:, bass.ds(e, 1), :].rearrange("p a d -> p (a d)"), src[0:CAP, 0:D],
                                          b2_sb[:, bass.ds(e, 1), :].rearrange("p a d -> p (a d)"), ALU.add)\
                            .then_inc(work.free(("y", i - 1)), 1)
            for b in range(B):
                src = back.wait_full(dve, ("x", b), 0)
                dve.scalar_tensor_tensor(env.y[:, b, :], src[0:T, 0:D], gate[:, b, 1:2], env.y[:, b, :],
                                         ALU.mult, ALU.add).then_inc(back.free(("x", b)), 1)
            back.wait_read(dve, ("x", B - 1), 0)
            norm_columns(dve, mv, stats, lambda k: env.y[:, k, :], B, T, s_stats, s_var, 1.0, EPS)
            dve.wait_ge(s_rstd, 1)
            normalise_rows(dve, env, mv, z, g2, be2, s_z, s_g, s_y)
            for b in range(B):
                dve.wait_ge(s_y, b + 1)
                dve.tensor_tensor(env.x[:, b, :], env.x[:, b, :], env.y[:, b, :], ALU.add).then_inc(s_end, 1)

        @block.tensor
        def _(pe):
            pe.wait_ge(loaded, 128)
            pe.wait_ge(s_ones, 1)
            for b in range(B):
                out_ = ring.wait_free(pe, ("yT", b), 0)
                transposes(pe, env, out_, env.y[:, b, :], T, 128, KC).then_inc(ring.full(("yT", b)), 1)
            acc = ring.wait_free(pe, ("logits", 0), 0)
            for b in range(B):
                ring.wait_read(pe, ("yT", b), 0)
                for k in range(KC):
                    last = pe.matmul(acc[0:T, b * E:(b + 1) * E], yT[:, k, b, :], wg[:, k, :],
                                     start=k == 0, stop=k == KC - 1)
            last.then_inc(ring.full(("logits", 0)), 1)
            acc = ring.wait_free(pe, ("loc", 0), 0)
            pe.wait_ge(s_hot, 1)
            pe.matmul(acc[0:T, 0:B * E], earlier[:], hot[:].rearrange("p b e -> p (b e)"), start=True, stop=False)
            for d in range(1, B):
                last = pe.matmul(acc[0:T, d * E:B * E], ones[:], hot[:, 0:B - d, :].rearrange("p b e -> p (b e)"),
                                 start=False, stop=d == B - 1)
            last.then_inc(ring.full(("loc", 0)), 1)
            for n in range(2):
                acc = ring.wait_free(pe, ("row", n), 0)
                for i in range(4):
                    b = 4 * n + i
                    pe.wait_ge(s_diag, b + 1)
                    last = pe.matmul(acc[0:CAP, i * T:(i + 1) * T], ones[:, 0:CAP], diag[b][:], start=True, stop=True)
                last.then_inc(ring.full(("row", n)), 1)
            for n in range(2):
                for k in range(KC):
                    acc = ring.wait_free(pe, ("d", n, k), 0)
                    for b in range(B):
                        if n + k == 0:
                            pe.wait_ge(s_P, b + 1)
                        last = pe.matmul(acc[:, 0:HALF], env.y[:, b, k * 128:(k + 1) * 128],
                                         Pm[:, b, n * HALF:(n + 1) * HALF], start=b == 0, stop=b == B - 1)
                    last.then_inc(ring.full(("d", n, k)), 1)
            for n in range(2):
                for k in range(KC):
                    ring.wait_read(pe, ("d", n, k), 0)

            def hidden(i, t):
                pe.wait_ge(w_in[i], t * 32 + 32)
                for a in range(2):
                    acc = work.wait_free(pe, ("h", i, a), t)
                    for f in range(4):
                        for k in range(KC):
                            last = pe.matmul(acc[:, f * CAP:(f + 1) * CAP],
                                             w1_sb[i][:, k, (4 * a + f) * 128:(4 * a + f + 1) * 128],
                                             dT[:, k, bass.ds((t * WB + i) * CAP, CAP)],
                                             start=k == 0, stop=k == KC - 1)
                    last.then_inc(work.full(("h", i, a)), 1)

            with pe.Fori(0, TURNS) as t:
                hidden(0, t)
                for i in range(WB):
                    if i + 1 < WB:
                        hidden(i + 1, t)
                    acc = work.wait_free(pe, ("y", i), t)
                    work.wait_read(pe, ("h", i, 0), t)
                    work.wait_read(pe, ("h", i, 1), t)
                    for f in range(FC):
                        last = pe.matmul(acc[0:CAP, 0:D], hT[i % 2][:, f, :], w2_sb[i][:, f, :],
                                         start=f == 0, stop=f == FC - 1)
                    last.then_inc(work.full(("y", i)), 1)
            work.wait_read(pe, ("y", WB - 1), TURNS - 1)
            pe.wait_ge(s_R, E)
            for b in range(B):
                acc = back.wait_free(pe, ("x", b), 0)
                for e in range(E):
                    last = pe.matmul(acc[0:T, 0:D], R[:, e, b * T:(b + 1) * T], ys[:, e, :],
                                     start=e == 0, stop=e == E - 1)
                last.then_inc(back.full(("x", b)), 1)


def program(nc, a, out):
    ctx = ExitStack()
    with ctx:
        env = Env(nc, ctx)
        phase_load(nc, env, a["x"], a["columns"])
        phase_self_attention_rope(nc, env, a["L0_attn_w_qkv"], a["L0_attn_w_out"],
                                  a["rope_cos"], a["rope_sin"])
        phase_cross_attention_normed(nc, env, a["ctx"], a["mask"], a["L0_xattn_Wq"], a["L0_xattn_Wkv"],
                                     a["L0_xattn_Wout"], a["L0_xattn_bout"])
        phase_kronecker_experts(nc, env, a["router_up"], a["A_up"], a["B_up"], a["router_down"], a["A_down"],
                                a["B_down"], a["bias_up"], a["bias_down"], a["kron_scales"])
        phase_self_attention_scaled(nc, env, a["head_mask_scaled"])
        phase_cross_attention_queries(nc, env, a["ctx"], a["head_mask"], a["L1_xattn_Wq"], a["L1_xattn_Wk"],
                                      a["L1_xattn_Wv"], a["L1_xattn_Wo"], a["L1_xattn_bv"], a["L1_xattn_bo"])
        phase_attention_over_sequences(nc, env, a["in_proj_w"], a["out_proj_w"], a["in_proj_b_v"],
                                       a["out_proj_b"], a["ln1_g"], a["ln1_b"], a["block_bias"])
        phase_capacity_experts(nc, env, out, a["wg"], a["w1"], a["w2"], a["b2"], a["ln2_g"], a["ln2_b"],
                               a["slots"], a["slot_ids"], a["iota8"], a["earlier"])


def rotary_tables():
    dim = 64
    inv = (1.0 / np.float32(10000.0) ** (np.arange(0, dim, 2, dtype=np.float32) / np.float32(dim))).astype(np.float32)
    f = np.arange(T - 1, dtype=np.float32)[:, None] * inv[None, :]
    cos = np.concatenate([np.ones((1, dim // 2), np.float32), np.cos(f)])
    sin = np.concatenate([np.zeros((1, dim // 2), np.float32), np.sin(f)])
    return np.concatenate([cos, cos], 1), np.concatenate([-sin, sin], 1)


def columns(inputs):
    def by_feature(name):
        return inputs[name].reshape(-1, 128).T

    def twice(name):
        return np.concatenate([inputs[name], inputs[name]]).reshape(128, 1)
    got = {"attn_gamma": by_feature("L0_attn_ln_gamma"), "attn_beta": by_feature("L0_attn_ln_beta"),
           "xattn_x_gamma": by_feature("L0_xattn_ln_x_g"), "xattn_x_beta": by_feature("L0_xattn_ln_x_b"),
           "xattn_l_gamma": by_feature("L0_xattn_ln_l_g"), "xattn_l_beta": by_feature("L0_xattn_ln_l_b"),
           "q_gamma": twice("L0_xattn_qn_g"), "k_gamma": twice("L0_xattn_kn_g"),
           "rotation": by_feature("L1_attn_rotation_params"), "entangle": by_feature("L1_attn_entangle_params"),
           "bq": by_feature("L1_xattn_bq"), "bk": by_feature("L1_xattn_bk"),
           "in_proj_b": by_feature("L1_ffn_in_proj_b"), "b1": by_feature("L1_ffn_b1")}
    return np.ascontiguousarray(np.concatenate([got[name] for name, _ in COLUMNS], axis=1))


def layout(inputs):
    a = {}
    c = np.ascontiguousarray
    a["x"] = c(inputs["x"])
    a["L0_attn_w_qkv"] = c(inputs["L0_attn_w_qkv"])
    a["L0_attn_w_out"] = c(inputs["L0_attn_w_out"])
    a["ctx"] = c(inputs["ctx_1024"])
    a["mask"] = c(inputs["mask_BxS2_bf1"]).view(np.uint8)
    for name in ("L0_xattn_Wq", "L0_xattn_Wkv", "L0_xattn_Wout", "L0_xattn_bout"):
        a[name] = c(inputs[name])
    E = 64
    a["router_up"] = c(inputs["L0_ffn_W_up"].T.reshape(8, 128, E).transpose(1, 0, 2))
    a["router_down"] = c(inputs["L0_ffn_W_down"].reshape(E, 64, 64).transpose(2, 1, 0))
    for name in ("A_up", "B_up", "A_down", "B_down"):
        a[name] = c(inputs[f"L0_ffn_{name}"].transpose(2, 0, 1))
    a["bias_up"] = c(inputs["L0_ffn_bias_up"].reshape(64, 64).T)
    a["bias_down"] = c(inputs["L0_ffn_bias_down"].reshape(32, 32).T)
    a["kron_scales"] = np.concatenate([inputs["L0_ffn_scale_up"], inputs["L0_ffn_scale_down"]])
    a["head_mask"] = (np.arange(128)[:, None] // 16 == np.arange(8)[None, :]).astype(np.float32)
    a["head_mask_scaled"] = np.where(np.arange(128)[:, None] // 16 == np.arange(8)[None, :], 0.25, 0.0)\
        .astype(np.float32)
    for name in ("Wq", "Wk", "Wv"):
        a[f"L1_xattn_{name}"] = c(inputs[f"L1_xattn_{name}"].reshape(D, D).T)
    a["L1_xattn_Wo"] = c(inputs["L1_xattn_Wo"].T)
    a["L1_xattn_bv"] = c(inputs["L1_xattn_bv"].reshape(D))
    a["L1_xattn_bo"] = c(inputs["L1_xattn_bo"])
    a["in_proj_w"] = c(inputs["L1_ffn_in_proj_w"].T)
    a["out_proj_w"] = c(inputs["L1_ffn_out_proj_w"].T)
    a["in_proj_b_v"] = c(inputs["L1_ffn_in_proj_b"][2 * D:])
    for name in ("out_proj_b", "ln1_g", "ln1_b", "ln2_g", "ln2_b", "wg", "w1", "w2", "b2"):
        a[name] = c(inputs[f"L1_ffn_{name}"])
    position = np.arange(128) // B
    a["block_bias"] = np.where(position[:, None] == position[None, :], 0.0, -1e30).astype(np.float32)
    a["slots"] = np.arange(B * T, dtype=np.float32)
    a["slot_ids"] = c(a["slots"].reshape(8, T).T)
    a["iota8"] = np.arange(8, dtype=np.float32)
    a["earlier"] = (np.arange(T)[:, None] < np.arange(T)[None, :]).astype(np.float32)
    a["columns"] = columns(inputs)
    a["rope_cos"], a["rope_sin"] = rotary_tables()
    return a


def kernel(**inputs):
    import concourse.bacc as bacc
    from concourse.bass_utils import run_bass_kernel_spmd

    nc = bacc.Bacc("TRN2", target_bir_lowering=False, num_devices=1)
    arrays = {f"in_{name}": array for name, array in layout(inputs).items()}
    aps = {name[3:]: nc.dram_tensor(name, array.shape, mybir.dt.from_np(array.dtype), kind="ExternalInput").ap()
           for name, array in arrays.items()}
    out = nc.dram_tensor("out_x", (B, T, D), F32, kind="ExternalOutput").ap()
    program(nc, aps, out)
    return run_bass_kernel_spmd(nc, [arrays], core_ids=[0]).results[0]["out_x"]
```

```python
import numpy as np
import concourse.bass as bass
from concourse import mybir
from contextlib import ExitStack

F32 = mybir.dt.float32
U32 = mybir.dt.uint32
U8 = mybir.dt.uint8
ALU = mybir.AluOpType
ACT = mybir.ActivationFunctionType
AX = mybir.AxisListType

B, T, D = 8, 112, 256
C = 375
CT = 125
H = 16
KC = D // 128
PAIRS = B // 2
EPS = 1e-5
BANKS = 8


class Ring:

    def __init__(self, env, names):
        self.env = env
        self.names = names
        self.at = {name: i for i, name in enumerate(names)}
        assert len(self.at) == len(names)
        self.uses = [len(range(k, len(names), BANKS)) for k in range(BANKS)]
        self.base = list(env.bank_uses)

    def close(self, turns):
        for k in range(BANKS):
            self.env.bank_uses[k] += turns * self.uses[k]

    def bank(self, name):
        return self.env.psum[:, self.at[name] % BANKS, :]

    def _count(self, name, turn):
        i = self.at[name]
        return i % BANKS, turn * self.uses[i % BANKS] + (self.base[i % BANKS] + i // BANKS + 1)

    def wait_free(self, pe, name, turn):
        k, n = self._count(name, turn)
        pe.wait_ge(self.env.bank_free[k], n)
        return self.bank(name)

    def wait_full(self, eng, name, turn):
        k, n = self._count(name, turn)
        eng.wait_ge(self.env.bank_full[k], n)
        return self.bank(name)

    def wait_read(self, eng, name, turn):
        k, n = self._count(name, turn)
        eng.wait_ge(self.env.bank_free[k], n + 1)

    def full(self, name):
        return self.env.bank_full[self.at[name] % BANKS]

    def free(self, name):
        return self.env.bank_free[self.at[name] % BANKS]


COLUMNS = [("attn_gamma", KC), ("attn_beta", KC), ("xattn_x_gamma", KC), ("xattn_x_beta", KC),
           ("xattn_l_gamma", KC), ("xattn_l_beta", KC), ("q_gamma", 1), ("k_gamma", 1),
           ("rotation", KC), ("entangle", KC), ("bq", KC), ("bk", KC), ("in_proj_b", 6), ("b1", 64)]


class Env:

    def __init__(self, nc, ctx):
        self.nc = nc
        self.psum = ctx.enter_context(nc.psum_tensor("psum", [128, BANKS, 512], F32))
        self.bank_full = [ctx.enter_context(nc.semaphore(f"bank_full{k}")) for k in range(BANKS)]
        self.bank_free = [ctx.enter_context(nc.semaphore(f"bank_free{k}")) for k in range(BANKS)]
        self.bank_uses = [0] * BANKS
        self.x = ctx.enter_context(nc.sbuf_tensor("x_stream", [T, B, D], F32))
        self.y = ctx.enter_context(nc.sbuf_tensor("last_block_stream", [T, B, D], F32))
        self.ident = ctx.enter_context(nc.sbuf_tensor("ident", [128, 128], F32))
        self.columns = ctx.enter_context(nc.sbuf_tensor("columns", [128, sum(n for _, n in COLUMNS)], F32))
        self.minus_half = ctx.enter_context(nc.sbuf_tensor("minus_half", [128, 32], F32))


    def column_at(self, name):
        names = [other for other, _ in COLUMNS]
        return sum(n for _, n in COLUMNS[:names.index(name)])

    def col(self, name, k=0):
        at = self.column_at(name) + k
        return self.columns[:, at:at + 1]


def tools(nc, ctx, phase):
    def sb(name, shape, dtype=F32):
        return ctx.enter_context(nc.sbuf_tensor(f"{phase}_{name}", shape, dtype))

    def sem(name):
        return ctx.enter_context(nc.semaphore(f"{phase}_{name}"))
    return sb, sem


def heads(ap, h, d):
    return ap.rearrange("p (h d) -> p h d", h=h)


def spread(ap, n):
    p, h = ap.shape
    return ap.rearrange("p (h o) -> p h o", o=1).to_broadcast([p, h, n])


def transposes(pe, env, out, src, rows, cols, each=1):
    for k in range(each):
        last = pe.transpose(out[0:cols, k * rows:(k + 1) * rows], src[0:rows, k * cols:(k + 1) * cols],
                            env.ident[0:rows, 0:rows])
    return last


def phase_load(nc, env, x, columns):
    ctx = ExitStack()
    with ctx:
        sb, sem = tools(nc, ctx, "load")
        x_in, zeroed, ready = sem("x_in"), sem("zeroed"), sem("ready")
        block = ctx.enter_context(nc.Block())

        @block.sync
        def _(sp):
            sp.dma_start(env.x[:], x.rearrange("b s d -> s b d")).then_inc(x_in, 16)
            sp.dma_start(env.columns[:], columns).then_inc(x_in, 16)
            sp.wait_ge(x_in, 32)

        @block.tensor
        def _(pe):
            for k in range(BANKS):
                pe.sem_inc(env.bank_free[k], 1)

        @block.gpsimd
        def _(pool):
            pool.memset(env.minus_half[:], -0.5).then_inc(ready, 1)
            pool.memset(env.ident[:], 0.0).then_inc(zeroed, 1)
            pool.wait_ge(zeroed, 1)
            pool.affine_select(out=env.ident[:], in_=env.ident[:], compare_op=ALU.not_equal, fill=1.0,
                               base=0, pattern=[[-1, 128]], channel_multiplier=1).then_inc(ready, 1)
            pool.wait_ge(ready, 2)


def norm_columns(dve, mv, stats, src, n, rows, s_stats, s_var, scale, add):
    for k in range(n):
        dve.bn_stats(stats[0:rows, k, :], src(k)).then_inc(s_stats, 1)
    for k in range(n):
        dve.wait_ge(s_stats, k + 1)
        last = dve.bn_aggr(mv[0:rows, k, 0:2], stats[0:rows, k, :])
    last.then_inc(s_stats, 1)
    dve.wait_ge(s_stats, n + 1)
    dve.tensor_scalar(mv[0:rows, 0:n, 2], mv[0:rows, 0:n, 1], scale, add, ALU.mult, ALU.add).then_inc(s_var, 1)


def phase_self_attention_rope(nc, env, w_qkv, w_out, cos, sin):
    ctx = ExitStack()
    with ctx:
        sb, sem = tools(nc, ctx, "rope")
        DH, UNITS = 64, 8
        wq = sb("w_qkv", [128, KC, 3 * H * DH])
        wo = sb("w_out", [128, 8, D])
        cs = sb("cos", [T, DH])
        sn = sb("sin", [T, DH])
        stats = sb("stats", [T, B, 6])
        mv = sb("mean_var", [T, B, 4])
        xn = [sb(f"xn{i}", [T, D]) for i in range(2)]
        xT = [sb(f"xT{i}", [128, KC, T]) for i in range(2)]
        qk = [sb(f"qk{i}", [T, 2 * H * DH]) for i in range(2)]
        rot = [sb(f"rot{i}", [T, 512]) for i in range(2)]
        v = [sb(f"v{i}", [T, H, DH + 1]) for i in range(2)]
        qT = [sb(f"qT{i}", [128, 8, 2, T]) for i in range(2)]
        kT = [sb(f"kT{i}", [128, 8, T]) for i in range(2)]
        P = [sb(f"P{i}", [T, 4 * T]) for i in range(4)]
        PT = [sb(f"PT{i}", [T, 4 * T]) for i in range(2)]
        mx = sb("max", [T, UNITS, 4])
        rs = sb("recip", [T, UNITS, 4])
        o = [sb(f"o{i}", [T, H * DH]) for i in range(2)]
        oT = [sb(f"oT{i}", [128, 8, T]) for i in range(2)]

        loaded, w_loaded, wo_loaded, ones = sem("loaded"), sem("w_loaded"), sem("wo_loaded"), sem("ones")
        s_stats, s_var, s_rstd, s_xn = sem("stats"), sem("var"), sem("rstd"), sem("xn")
        s_rot, s_max, s_exp, s_sum = sem("rotated"), sem("max"), sem("exp"), sem("sum")

        def head(g, i):
            return 8 * (g // 2) + g % 2 + 2 * i

        units = [(g, par) for g in range(4) for par in range(2)]
        names = [("xT", par) for par in range(2)]
        names += [("qkv", par, j) for par in range(2) for j in range(6)]
        names += [("qkT", par, j) for par in range(2) for j in range(4)]
        for u in range(UNITS + 3):
            names += [("S", u)] * (u < UNITS) + [("PT", u - 2)] * (0 <= u - 2 < UNITS) + [("O", u - 3)] * (u >= 3)
        names += [("oT", par, j) for par in range(2) for j in range(2)]
        names += [("out", par) for par in range(2)]
        ring = Ring(env, names)
        block = ctx.enter_context(nc.Block())

        @block.sync
        def _(sp):
            sp.dma_start(cs[:], cos).then_inc(loaded, 16)
            sp.dma_start(sn[:], sin).then_inc(loaded, 16)
            sp.dma_start(wq[:], w_qkv.rearrange("(k p) n -> p k n", p=128)).then_inc(w_loaded, 16)
            sp.dma_start(wo[:], w_out.rearrange("(k p) n -> p k n", p=128)).then_inc(wo_loaded, 16)
            sp.wait_ge(w_loaded, 16)
            sp.wait_ge(wo_loaded, 16)

        @block.gpsimd
        def _(pool):
            for i in range(2):
                pool.memset(v[i][:], 1.0).then_inc(ones, 1)
                pool.memset(qT[i][:], 0.0).then_inc(ones, 1)
            pool.wait_ge(s_var, 1)
            pool.tensor_tensor(mv[:, :, 3], mv[:, :, 2], env.minus_half[0:T, 0:B], ALU.pow).then_inc(s_rstd, 1)
            with pool.Fori(0, PAIRS) as t:
                for par in range(2):
                    for j in range(4):
                        ring.wait_read(pool, ("qkv", par, j), t)
                        part = qk[par][:, j * 512:(j + 1) * 512]
                        pool.tensor_tensor(part, part, rot[j % 2][:], ALU.add).then_inc(s_rot, 1)

        @block.scalar
        def _(act):
            act.wait_ge(ones, 4)
            with act.Fori(0, PAIRS) as t:
                for par in range(2):
                    src = ring.wait_full(act, ("xT", par), t)
                    for k in range(KC):
                        last = act.activation(xT[par][:, k, :], src[:, k * T:(k + 1) * T], ACT.Identity,
                                              bias=env.col("attn_beta", k), scale=env.col("attn_gamma", k))
                    last.then_inc(ring.free(("xT", par)), 1)
                for par in range(2):
                    for j in range(4, 6):
                        src = ring.wait_full(act, ("qkv", par, j), t)
                        act.copy(v[par][:, (j - 4) * 8:(j - 3) * 8, 0:DH],
                                 heads(src[0:T, :], 8, DH)).then_inc(ring.free(("qkv", par, j)), 1)
                for par in range(2):
                    for j in range(2):
                        src = ring.wait_full(act, ("qkT", par, j), t)
                        for half in range(2):
                            rows = slice(64 * half, 64 * half + 64)
                            last = act.copy(qT[par][rows, 4 * j:4 * j + 4, half, :], heads(src[rows, 0:4 * T], 4, T))
                        last.then_inc(ring.free(("qkT", par, j)), 1)
                    for j in range(2):
                        src = ring.wait_full(act, ("qkT", par, 2 + j), t)
                        act.copy(kT[par][:, 4 * j:4 * j + 4, :].rearrange("p a b -> p (a b)"),
                                 src[:, 0:4 * T]).then_inc(ring.free(("qkT", par, 2 + j)), 1)
                for u in range(UNITS + 2):
                    if u < UNITS:
                        ring.wait_read(act, ("S", u), t)
                        act.activation(P[u % 4][:], P[u % 4][:], ACT.Exp, scale=DH ** -0.5).then_inc(s_exp, 1)
                    if u >= 2:
                        src = ring.wait_full(act, ("PT", u - 2), t)
                        act.copy(PT[u % 2][:], src[0:T, 0:4 * T]).then_inc(ring.free(("PT", u - 2)), 1)
                for par in range(2):
                    for j in range(2):
                        src = ring.wait_full(act, ("oT", par, j), t)
                        act.copy(oT[par][:, 4 * j:4 * j + 4, :].rearrange("p a b -> p (a b)"),
                                 src[:, 0:4 * T]).then_inc(ring.free(("oT", par, j)), 1)

        @block.vector
        def _(dve):
            dve.wait_ge(loaded, 32)
            norm_columns(dve, mv, stats, lambda k: env.x[:, k, :], B, T, s_stats, s_var, 1.0 + EPS, EPS * EPS)
            dve.wait_ge(s_rstd, 1)
            with dve.Fori(0, PAIRS) as t:
                for par in range(2):
                    b = t * 2 + par
                    xb = env.x[:, bass.ds(b, 1), :].rearrange("p a d -> p (a d)")
                    dve.tensor_scalar(xn[par][:], xb, mv[:, bass.ds(b, 1), 0:1].rearrange("p a o -> p (a o)"),
                                      mv[:, bass.ds(b, 1), 3:4].rearrange("p a o -> p (a o)"),
                                      ALU.subtract, ALU.mult).then_inc(s_xn, 1)
                for par in range(2):
                    for j in range(4):
                        src = ring.wait_full(dve, ("qkv", par, j), t)
                        if par * 4 + j >= 2:
                            dve.wait_ge(s_rot, t * 8 + (par * 4 + j - 1))
                        th = heads(src[0:T, :], 8, DH)
                        ch = cs[:, :].rearrange("p (o d) -> p o d", o=1).to_broadcast([T, 8, DH])
                        rh = heads(rot[j % 2][:], 8, DH)
                        HD = DH // 2
                        dve.tensor_tensor(heads(qk[par][:, j * 512:(j + 1) * 512], 8, DH), th, ch, ALU.mult)
                        for a in range(2):
                            sh = sn[:, a * HD:(a + 1) * HD].rearrange("p (o d) -> p o d", o=1)\
                                .to_broadcast([T, 8, HD])
                            last = dve.tensor_tensor(rh[:, :, a * HD:(a + 1) * HD],
                                                     th[:, :, (1 - a) * HD:(2 - a) * HD], sh, ALU.mult)
                        last.then_inc(ring.free(("qkv", par, j)), 1)
                for u in range(UNITS + 3):
                    if u < UNITS:
                        src = ring.wait_full(dve, ("S", u), t)
                        s4 = heads(src[0:T, 0:4 * T], 4, T)
                        dve.tensor_reduce(mx[:, u, :], s4, AX.X, ALU.max).then_inc(s_max, 1)
                        dve.wait_ge(s_max, t * UNITS + (u + 1))
                        dve.tensor_tensor(heads(P[u % 4][:], 4, T), s4, spread(mx[:, u, :], T),
                                          ALU.subtract).then_inc(ring.free(("S", u)), 1)
                    if u >= 3:
                        w = u - 3
                        g, par = units[w]
                        src = ring.wait_full(dve, ("O", w), t)
                        o4 = heads(src[0:T, 0:4 * (DH + 1)], 4, DH + 1)
                        dve.reciprocal(rs[:, w, :], o4[:, :, DH]).then_inc(s_sum, 1)
                        dve.wait_ge(s_sum, t * UNITS + (w + 1))
                        dve.tensor_tensor(heads(o[par][:], H, DH)[:, head(g, 0):head(g, 3) + 1:2, :], o4[:, :, 0:DH],
                                          spread(rs[:, w, :], DH), ALU.mult).then_inc(ring.free(("O", w)), 1)
                for par in range(2):
                    b = t * 2 + par
                    xb = env.x[:, bass.ds(b, 1), :].rearrange("p a d -> p (a d)")
                    src = ring.wait_full(dve, ("out", par), t)
                    dve.tensor_tensor(xb, xb, src[0:T, 0:D], ALU.add).then_inc(ring.free(("out", par)), 1)

        @block.tensor
        def _(pe):
            pe.wait_ge(w_loaded, 16)
            pe.wait_ge(wo_loaded, 16)
            with pe.Fori(0, PAIRS) as t:
                for par in range(2):
                    out = ring.wait_free(pe, ("xT", par), t)
                    pe.wait_ge(s_xn, t * 2 + (par + 1))
                    transposes(pe, env, out, xn[par], T, 128, KC).then_inc(ring.full(("xT", par)), 1)
                for par in range(2):
                    ring.wait_read(pe, ("xT", par), t)
                    for j in range(6):
                        out = ring.wait_free(pe, ("qkv", par, j), t)
                        for k in range(KC):
                            last = pe.matmul(out[0:T, :], xT[par][:, k, :], wq[:, k, j * 512:(j + 1) * 512],
                                             start=k == 0, stop=k == KC - 1)
                        last.then_inc(ring.full(("qkv", par, j)), 1)
                for par in range(2):
                    for j in range(4):
                        pe.wait_ge(s_rot, t * 8 + (par * 4 + j + 1))
                        out = ring.wait_free(pe, ("qkT", par, j), t)
                        transposes(pe, env, out, qk[par][:, j * 512:(j + 1) * 512], T, 128, 4)\
                            .then_inc(ring.full(("qkT", par, j)), 1)
                for u in range(UNITS + 3):
                    if u < UNITS:
                        g, par = units[u]
                        out = ring.wait_free(pe, ("S", u), t)
                        ring.wait_read(pe, ("qkT", par, 2 + g // 2), t)
                        for i in range(4):
                            h = head(g, i)
                            last = pe.matmul(out[0:T, i * T:(i + 1) * T], qT[par][:, h // 2, h % 2, :],
                                             kT[par][:, h // 2, :], start=True, stop=True)
                        last.then_inc(ring.full(("S", u)), 1)
                    if 0 <= u - 2 < UNITS:
                        w = u - 2
                        out = ring.wait_free(pe, ("PT", w), t)
                        pe.wait_ge(s_exp, t * UNITS + (w + 1))
                        transposes(pe, env, out, P[w % 4], T, T, 4).then_inc(ring.full(("PT", w)), 1)
                    if u >= 3:
                        w = u - 3
                        g, par = units[w]
                        out = ring.wait_free(pe, ("O", w), t)
                        ring.wait_read(pe, ("PT", w), t)
                        ring.wait_read(pe, ("qkv", par, 4 + g // 2), t)
                        for i in range(4):
                            last = pe.matmul(out[0:T, i * (DH + 1):(i + 1) * (DH + 1)],
                                             PT[w % 2][:, i * T:(i + 1) * T], v[par][:, head(g, i), :],
                                             start=True, stop=True)
                        last.then_inc(ring.full(("O", w)), 1)
                for par in range(2):
                    ring.wait_read(pe, ("O", UNITS - 2 + par), t)
                    for j in range(2):
                        out = ring.wait_free(pe, ("oT", par, j), t)
                        transposes(pe, env, out, o[par][:, j * 512:(j + 1) * 512], T, 128, 4)\
                            .then_inc(ring.full(("oT", par, j)), 1)
                for par in range(2):
                    out = ring.wait_free(pe, ("out", par), t)
                    ring.wait_read(pe, ("oT", par, 1), t)
                    for k in range(8):
                        last = pe.matmul(out[0:T, 0:D], oT[par][:, k, :], wo[:, k, :], start=k == 0, stop=k == 7)
                    last.then_inc(ring.full(("out", par)), 1)
        ring.close(PAIRS)


def phase_cross_attention_normed(nc, env, ctx_rows, mask, w_q, w_kv, w_out, b_out):
    ctx = ExitStack()
    with ctx:
        sb, sem = tools(nc, ctx, "cross")
        DH, NT = 64, C // CT
        KEYS = C + T
        STEPS = H // 2
        BIG = float(np.finfo(np.float32).max)
        wq = sb("w_q", [128, KC, H * DH])
        wkv = sb("w_kv", [128, KC, 2 * H * DH])
        wo = sb("w_out", [128, 8, D])
        bo = sb("b_out", [T, D])
        rows_in = sb("ctx", [CT, B * NT, D])
        mask_in = sb("mask", [T, B, C], U8)
        qk_gamma = sb("qk_gamma", [128, 1])
        stats = sb("stats", [128, B * NT + B, 6])
        mv = sb("mean_var", [128, B * NT + B, 4])
        bias = [sb(f"mask_bias{i}", [T, KEYS]) for i in range(2)]
        xn = [sb(f"xn{i}", [CT, D]) for i in range(2)]
        xT = [sb(f"xT{i}", [128, KC, CT]) for i in range(2)]
        lT = [sb(f"lT{i}", [128, KC, T]) for i in range(2)]
        sq = [sb(f"squares{i}", [CT, H * DH]) for i in range(2)]
        ssq = sb("rms", [CT, 5, 2, H])
        kn = [sb(f"kn{i}", [CT, H * DH]) for i in range(2)]
        kT = [sb(f"kT{i}", [128, 8, KEYS]) for i in range(2)]
        qT = [sb(f"qT{i}", [128, 8, 2, T]) for i in range(2)]
        v = [sb(f"v{i}", [CT, NT + 1, H, DH + 1]) for i in range(2)]
        P = [sb(f"P{i}", [T, KEYS]) for i in range(4)]
        low = sb("row_min", [T, H])
        PT = [sb(f"PT{i}", [CT, 4 * T]) for i in range(4)]
        rs = sb("recip", [T, H // 4, 4])
        o = sb("o", [T, H * DH])
        oT = sb("oT", [128, 8, T])
        waited, whole = sb("waited", [1, STEPS]), sb("whole", [1, 1])
        res = sb("res", [T, D])

        loaded, w_loaded, wo_loaded, set_up = sem("loaded"), sem("w_loaded"), sem("wo_loaded"), sem("set_up")
        s_stats, s_var, s_lstats, s_lvar, s_rstd = sem("stats"), sem("var"), sem("lstats"), sem("lvar"), sem("rstd")
        s_xn, s_sq, s_ssum, s_mean, s_rms, s_kn = sem("xn"), sem("sq"), sem("ssum"), sem("mean"), sem("rms"), sem("kn")
        s_bias, s_exp, s_sum, s_res, s_gamma = sem("bias"), sem("exp"), sem("sum"), sem("res"), sem("gamma")
        s_divided = sem("divided")

        TILES = 5
        height = [T, T, CT, CT, CT]
        chunk = [NT, None, 0, 1, 2]
        TURNED = [0, 2, 3, 4]
        TURN = {0: [0, 2], 3: [3], 6: [4]}
        BACK = {2: 0, 4: 1, 5: 2, 7: 3, 9: 4}
        KEY = {0: 0, 2: 1, 3: 2, 5: 3, 7: 4}
        VALUE = {1: 0, 4: 2, 6: 3, 8: 4}
        ALL = STEPS + 2

        def step_tiles(i, s, heads_too, build, tail):
            names = []
            if heads_too:
                names += [("S", i, 2 * s), ("S", i, 2 * s + 1)] * (s < STEPS)
            if build:
                names += [("xT", i, c) for c in TURN.get(s, [])]
            if tail:
                names += [("oT", i, 0), ("oT", i, 1)] * (s == 0) + [("out", i)] * (s == 1)
            back = [("kT", i, BACK[s], j) for j in range(2) if build and s in BACK]
            names += back * (s < ALL - 1)
            if heads_too:
                names += [("O", i, (s - 3) // 2)] * (s >= 3 and s % 2 == 1)
            names += back * (s == ALL - 1)
            if heads_too:
                names += [("PT", i, 2 * s - 2), ("PT", i, 2 * s - 1)] * (1 <= s <= STEPS)
            if build:
                names += [("mm", i, KEY[s], j) for j in range(2) if s in KEY]
                names += [("mm", i, VALUE[s], j) for j in range(2, 4) if s in VALUE]
            return names

        def ring_of(sections, turns):
            ring = Ring(env, [name for i, what in enumerate(sections) for s in range(ALL)
                              for name in step_tiles(i, s, *what)])
            ring.close(turns)
            return ring

        FIRST, SECTION_0, MIDDLE, SECTION_7 = (False, True, False), (True, True, False), (True, True, True), \
            (True, False, True)
        rings = [ring_of([FIRST], 1), ring_of([SECTION_0], 1), ring_of([MIDDLE, MIDDLE], PAIRS - 1),
                 ring_of([SECTION_7], 1), ring_of([(False, False, True)], 1)]

        def count(seq, each, k):
            t, offset = seq
            return t * (2 * each) + (offset * each + k + 1)

        def after(seq, k):
            return seq[0], seq[1] + k

        def program_of(eng, section):
            section(rings[0], 0, 0, (0, -1), *FIRST)
            section(rings[1], 0, 0, (0, 0), *SECTION_0)
            with eng.Fori(0, PAIRS - 1) as t:
                section(rings[2], t, 0, (t, 1), *MIDDLE)
                section(rings[2], t, 1, (t, 2), *MIDDLE)
            section(rings[3], 0, 0, (PAIRS - 1, 1), *SECTION_7)
            section(rings[4], 0, 0, (PAIRS, 0), False, False, True)

        block = ctx.enter_context(nc.Block())

        @block.sync
        def _(sp):
            sp.dma_start(rows_in[:], ctx_rows.rearrange("b (c p) d -> p (b c) d", p=CT)).then_inc(loaded, 16)
            sp.dma_start(mask_in[:], mask.rearrange("(o b) c -> o b c", o=1).to_broadcast([T, B, C]))\
                .then_inc(loaded, 16)
            sp.dma_start(bo[:], b_out.rearrange("(o d) -> o d", o=1).to_broadcast([T, D])).then_inc(loaded, 16)
            sp.dma_start(wkv[:], w_kv.rearrange("(k p) n -> p k n", p=128)).then_inc(w_loaded, 16)
            sp.dma_start(wq[:], w_q.rearrange("(k p) n -> p k n", p=128)).then_inc(w_loaded, 16)
            sp.dma_start(wo[:], w_out.rearrange("(k p) n -> p k n", p=128)).then_inc(wo_loaded, 16)
            sp.wait_ge(wo_loaded, 16)

        @block.gpsimd
        def _(pool):
            for i in range(2):
                pool.memset(v[i][:], 1.0).then_inc(set_up, 1)
                pool.memset(bias[i][:, C:KEYS], 0.0).then_inc(set_up, 1)
                pool.memset(qT[i][:], 0.0).then_inc(set_up, 1)
            pool.wait_ge(s_lvar, 1)
            pool.tensor_tensor(mv[0:T, B * NT:, 3], mv[0:T, B * NT:, 2], env.minus_half[0:T, 0:B], ALU.pow)\
                .then_inc(s_rstd, 1)
            pool.wait_ge(s_var, 1)
            pool.tensor_tensor(mv[0:CT, 0:B * NT, 3], mv[0:CT, 0:B * NT, 2], env.minus_half[0:CT, 0:B * NT],
                               ALU.pow).then_inc(s_rstd, 1)

            def section(ring, turn, i, seq, heads_too, build, tail):
                for m in range(TILES * build):
                    n = height[m]
                    pool.wait_ge(s_mean, count(after(seq, 1), TILES, m))
                    pool.tensor_tensor(ssq[0:n, m, 1, :], ssq[0:n, m, 0, :], env.minus_half[0:n, 0:H],
                                       ALU.pow).then_inc(s_rms, 1)

            program_of(pool, section)

        def turned(m, seq):
            return lT[seq[1] % 2] if m < 2 else xT[TURNED.index(m) % 2]

        @block.scalar
        def _(act):
            act.wait_ge(set_up, 6)
            act.wait_ge(s_gamma, 2)

            def section(ring, turn, i, seq, heads_too, build, tail):
                par, nxt = seq[1] % 2, (seq[1] + 1) % 2
                for s in range(ALL):
                    for m in TURN.get(s, []) * build:
                        n = height[m]
                        src = ring.wait_full(act, ("xT", i, m), turn)
                        kind = "x" if m >= 2 else "l"
                        for k in range(KC):
                            last = act.activation(turned(m, after(seq, 1))[:, k, 0:n], src[:, k * n:(k + 1) * n],
                                                  ACT.Identity, bias=env.col(f"xattn_{kind}_beta", k),
                                                  scale=env.col(f"xattn_{kind}_gamma", k))
                        last.then_inc(ring.free(("xT", i, m)), 1)
                    if heads_too and s < STEPS:
                        for u in (2 * s, 2 * s + 1):
                            ring.wait_read(act, ("S", i, u), turn)
                            act.activation(P[u % 4][:], P[u % 4][:], ACT.Exp, bias=low[:, u:u + 1],
                                           scale=-1.0).then_inc(s_exp, 1)
                    for j in range(2 * (tail and s == 0)):
                        src = ring.wait_full(act, ("oT", i, j), turn)
                        act.copy(oT[:, 4 * j:4 * j + 4, :].rearrange("p a b -> p (a b)"),
                                 src[:, 0:4 * T]).then_inc(ring.free(("oT", i, j)), 1)
                    if build and s in BACK:
                        m = BACK[s]
                        n = height[m]
                        for j in range(2):
                            src = ring.wait_full(act, ("kT", i, m, j), turn)
                            s4 = heads(src[:, 0:4 * n], 4, n)
                            if m != 1:
                                at = chunk[m] * CT
                                op = act.copy(kT[nxt][:, 4 * j:4 * j + 4, at:at + n], s4)
                            else:
                                for half in range(2):
                                    rows = slice(64 * half, 64 * half + 64)
                                    op = act.mul(qT[nxt][rows, 4 * j:4 * j + 4, half, :], s4[rows],
                                                 qk_gamma[rows, :])
                            op.then_inc(ring.free(("kT", i, m, j)), 1)
                    if heads_too and 1 <= s <= STEPS:
                        u = 2 * s - 2
                        src = ring.wait_full(act, ("PT", i, u), turn)
                        act.copy(PT[u % 4][:], src[0:CT, 0:4 * T]).then_inc(ring.free(("PT", i, u)), 1)
                    if build and s in KEY:
                        m = KEY[s]
                        n = height[m]
                        for j in range(2):
                            src = ring.wait_full(act, ("mm", i, m, j), turn)
                            act.activation(sq[m % 2][0:n, j * 512:(j + 1) * 512], src[0:n, :], ACT.Square)\
                                .then_inc(s_sq, 1)
                    if build and s in VALUE:
                        m = VALUE[s]
                        n = height[m]
                        for j in range(2):
                            src = ring.wait_full(act, ("mm", i, m, 2 + j), turn)
                            act.copy(v[nxt][0:n, chunk[m], 8 * j:8 * j + 8, 0:DH], heads(src[0:n, :], 8, DH))\
                                .then_inc(ring.free(("mm", i, m, 2 + j)), 1)

            program_of(act, section)

        @block.vector
        def _(dve):
            dve.tensor_scalar(qk_gamma[:], env.col("q_gamma"), env.col("k_gamma"), -(DH ** -0.5),
                              ALU.mult, ALU.mult).then_inc(s_gamma, 2)
            norm_columns(dve, mv[:, B * NT:, :], stats[:, B * NT:, :], lambda k: env.x[:, k, :], B, T,
                         s_lstats, s_lvar, 1.0 + EPS, EPS * EPS)
            dve.wait_ge(loaded, 48)
            norm_columns(dve, mv, stats[:, :, :], lambda k: rows_in[:, k, :], B * NT, CT, s_stats, s_var,
                         1.0, EPS)
            dve.wait_ge(s_rstd, 2)
            dve.wait_ge(set_up, 6)

            def normalise(m, seq):
                b = seq[0] * 2 + seq[1]
                n = height[m]
                at, row = (b * NT + chunk[m], b * NT + chunk[m]) if m >= 2 else (b + B * NT, b)
                src = (rows_in if m >= 2 else env.x)[0:n, bass.ds(row, 1), :].rearrange("p a d -> p (a d)")
                dve.tensor_scalar(xn[TURNED.index(m) % 2][0:n, :], src,
                                  mv[0:n, bass.ds(at, 1), 0:1].rearrange("p a o -> p (a o)"),
                                  mv[0:n, bass.ds(at, 1), 3:4].rearrange("p a o -> p (a o)"),
                                  ALU.subtract, ALU.mult).then_inc(s_xn, 1)

            def divide(ring, turn, i, seq, w):
                src = ring.wait_full(dve, ("O", i, w), turn)
                o4 = heads(src[0:T, 0:4 * (DH + 1)], 4, DH + 1)
                dve.reciprocal(rs[:, w, :], o4[:, :, DH]).then_inc(s_sum, 1)
                dve.wait_ge(s_sum, count(seq, H // 4, w))
                op = dve.tensor_tensor(heads(o[:, w * 4 * DH:(w + 1) * 4 * DH], 4, DH), o4[:, :, 0:DH],
                                       spread(rs[:, w, :], DH), ALU.mult)
                if w < H // 4 - 1:
                    op.then_inc(ring.free(("O", i, w)), 1)
                else:
                    op.then_inc(s_divided, 1)
                    dve.wait_ge(s_divided, count(seq, 1, 0))
                    dve.tensor_copy(whole[:], o4[0:1, 0, 0:1]).then_inc(ring.free(("O", i, w)), 1)

            def section(ring, turn, i, seq, heads_too, build, tail):
                par, nxt = seq[1] % 2, (seq[1] + 1) % 2
                following = after(seq, 1)
                if build:
                    for m in TURN[0]:
                        normalise(m, following)
                for s in range(ALL):
                    if heads_too and s < STEPS:
                        if s == 0:
                            dve.wait_ge(s_bias, count(seq, 1, 0))
                        for u in (2 * s, 2 * s + 1):
                            src = ring.wait_full(dve, ("S", i, u), turn)
                        dve.tensor_copy(waited[:, s:s + 1], src[0:1, 0:1])
                        for u in (2 * s, 2 * s + 1):
                            src = ring.bank(("S", i, u))
                            dve.tensor_tensor_reduce(out=P[u % 4][:], in0=src[0:T, 0:KEYS], in1=bias[par][:],
                                                     scale=1.0, scalar=BIG, op0=ALU.add, op1=ALU.min,
                                                     accum_out=low[:, u:u + 1])\
                                .then_inc(ring.free(("S", i, u)), 1)
                    for m in TURN.get(s + 1, []) * build:
                        ring.wait_full(dve, ("xT", i, TURNED[TURNED.index(m) - 2]), turn)
                        normalise(m, following)
                    if build and s - 1 in KEY:
                        m = KEY[s - 1]
                        n = height[m]
                        dve.wait_ge(s_rms, count(following, TILES, m))
                        for j in range(2):
                            ring.wait_read(dve, ("mm", i, m, j), turn)
                            part = heads(kn[m % 2][0:n, j * 512:(j + 1) * 512], 8, DH)
                            dve.tensor_tensor(part, part, spread(ssq[0:n, m, 1, 8 * j:8 * j + 8], DH),
                                              ALU.mult).then_inc(s_kn, 1)
                    if build and s == 4:
                        b = following[0] * 2 + following[1]
                        dve.tensor_scalar(bias[nxt][:, 0:C],
                                          mask_in[:, bass.ds(b, 1), :].rearrange("p a c -> p (a c)"),
                                          -BIG, BIG, ALU.mult, ALU.add).then_inc(s_bias, 1)
                    if heads_too and 1 <= s <= STEPS:
                        u = 2 * s - 1
                        src = ring.wait_full(dve, ("PT", i, u), turn)
                        dve.tensor_copy(PT[u % 4][:], src[0:CT, 0:4 * T]).then_inc(ring.free(("PT", i, u)), 1)
                    if heads_too and s >= 3 and s % 2 == 1:
                        divide(ring, turn, i, seq, (s - 3) // 2)
                    if build and s in KEY:
                        m = KEY[s]
                        n = height[m]
                        for j in range(2):
                            dve.wait_ge(s_sq, count(following, 2 * TILES, 2 * m + j))
                            dve.tensor_copy(kn[m % 2][0:n, j * 512:(j + 1) * 512],
                                            ring.bank(("mm", i, m, j))[0:n, :])\
                                .then_inc(ring.free(("mm", i, m, j)), 1)
                        dve.tensor_reduce(ssq[0:n, m, 0, :], heads(sq[m % 2][0:n, :], H, DH), AX.X, ALU.add)\
                            .then_inc(s_ssum, 1)
                        dve.wait_ge(s_ssum, count(following, TILES, m))
                        dve.tensor_scalar(ssq[0:n, m, 0, :], ssq[0:n, m, 0, :], 1.0 / DH, 1e-16, ALU.mult, ALU.max)\
                            .then_inc(s_mean, 1)
                    if tail and s == 1:
                        b = seq[0] * 2 + (seq[1] - 1)
                        xb = env.x[:, bass.ds(b, 1), :].rearrange("p a d -> p (a d)")
                        src = ring.wait_full(dve, ("out", i), turn)
                        dve.tensor_tensor(res[:], bo[:], src[0:T, 0:D], ALU.add).then_inc(ring.free(("out", i)), 1)
                        ring.wait_read(dve, ("out", i), turn)
                        dve.tensor_tensor(xb, xb, res[:], ALU.add).then_inc(s_res, 1)

            program_of(dve, section)

        @block.tensor
        def _(pe):
            pe.wait_ge(w_loaded, 32)
            pe.wait_ge(wo_loaded, 16)

            def multiply(ring, turn, i, seq, m, columns):
                n = height[m]
                w = wq if m == 1 else wkv
                for j in columns:
                    out = ring.wait_free(pe, ("mm", i, m, j), turn)
                    for k in range(KC):
                        last = pe.matmul(out[0:n, :], turned(m, seq)[:, k, 0:n], w[:, k, j * 512:(j + 1) * 512],
                                         start=k == 0, stop=k == KC - 1)
                    last.then_inc(ring.full(("mm", i, m, j)), 1)

            def turn_back(ring, turn, i, seq, m):
                for j in range(2):
                    out = ring.wait_free(pe, ("kT", i, m, j), turn)
                    pe.wait_ge(s_kn, count(seq, 2 * TILES, 2 * m + j))
                    transposes(pe, env, out, kn[m % 2][:, j * 512:(j + 1) * 512], height[m], 128, 4)\
                        .then_inc(ring.full(("kT", i, m, j)), 1)

            def section(ring, turn, i, seq, heads_too, build, tail):
                par = seq[1] % 2
                following = after(seq, 1)
                for s in range(ALL):
                    if heads_too and s < STEPS:
                        for u in (2 * s, 2 * s + 1):
                            out = ring.wait_free(pe, ("S", i, u), turn)
                            pe.matmul(out[0:T, 0:KEYS], qT[par][:, u // 2, u % 2, :], kT[par][:, u // 2, :],
                                      start=True, stop=True).then_inc(ring.full(("S", i, u)), 1)
                    for m in TURN.get(s, []) * build:
                        out = ring.wait_free(pe, ("xT", i, m), turn)
                        pe.wait_ge(s_xn, count(following, len(TURNED), TURNED.index(m)))
                        transposes(pe, env, out, xn[TURNED.index(m) % 2], height[m], 128, KC)\
                            .then_inc(ring.full(("xT", i, m)), 1)
                    if tail and s == 0:
                        pe.wait_ge(s_divided, count(after(seq, -1), 1, 0))
                        for j in range(2):
                            out = ring.wait_free(pe, ("oT", i, j), turn)
                            transposes(pe, env, out, o[:, j * 512:(j + 1) * 512], T, 128, 4)\
                                .then_inc(ring.full(("oT", i, j)), 1)
                    if tail and s == 1:
                        out = ring.wait_free(pe, ("out", i), turn)
                        ring.wait_read(pe, ("oT", i, 1), turn)
                        for k in range(8):
                            last = pe.matmul(out[0:T, 0:D], oT[:, k, :], wo[:, k, :], start=k == 0, stop=k == 7)
                        last.then_inc(ring.full(("out", i)), 1)
                    if build and s in BACK and s < ALL - 1:
                        turn_back(ring, turn, i, following, BACK[s])
                    if heads_too and s >= 3 and s % 2 == 1:
                        w = (s - 3) // 2
                        out = ring.wait_free(pe, ("O", i, w), turn)
                        for u in range(4 * w, 4 * w + 4):
                            if build and s == ALL - 1 and u == H - 1:
                                turn_back(ring, turn, i, following, BACK[s])
                            ring.wait_read(pe, ("PT", i, u), turn)
                            for c in range(NT + 1):
                                n = CT if c < NT else T
                                last = pe.matmul(out[0:T, (u % 4) * (DH + 1):(u % 4 + 1) * (DH + 1)],
                                                 PT[u % 4][0:n, c * T:(c + 1) * T], v[par][0:n, c, u, :],
                                                 start=c == 0, stop=c == NT)
                        last.then_inc(ring.full(("O", i, w)), 1)
                    if heads_too and 1 <= s <= STEPS:
                        for u in (2 * s - 2, 2 * s - 1):
                            out = ring.wait_free(pe, ("PT", i, u), turn)
                            pe.wait_ge(s_exp, count(seq, H, u))
                            for c in range(NT + 1):
                                n = CT if c < NT else T
                                last = pe.transpose(out[0:n, c * T:(c + 1) * T], P[u % 4][:, c * CT:c * CT + n],
                                                    env.ident[0:T, 0:T])
                            last.then_inc(ring.full(("PT", i, u)), 1)
                    if build and s in KEY:
                        m = KEY[s]
                        if m != 1:
                            ring.wait_read(pe, ("xT", i, m), turn)
                        multiply(ring, turn, i, following, m, (0, 1))
                    if build and s in VALUE:
                        multiply(ring, turn, i, following, VALUE[s], (2, 3))
                if build and not heads_too:
                    turn_back(ring, turn, i, following, TILES - 1)
                if build:
                    ring.wait_read(pe, ("kT", i, TILES - 1, 1), turn)

            program_of(pe, section)


def phase_kronecker_experts(nc, env, w_up, a_up, b_up, w_down, a_down, b_down, bias_up, bias_down, scales):
    ctx = ExitStack()
    with ctx:
        sb, sem = tools(nc, ctx, "kron")
        E, D1, F1 = 64, 32, 64
        N = 2 * T // 4
        NB = T // 4
        router_up = sb("router_up", [128, 8, E])
        router_down = sb("router_down", [128, F1, E])
        first_up = sb("b_up", [128, E, F1])
        second_up = sb("a_up", [128, E, F1])
        first_down = sb("b_down", [128, E, D1])
        second_down = sb("a_down", [128, E, D1])
        bias_u = sb("bias_up", [F1, F1])
        bias_d = sb("bias_down", [D1, D1])
        scale = sb("scales", [F1, 2])
        ones = sb("ones", [N, 128])
        stats = sb("stats", [T, B, 6])
        mv = sb("mean_var", [T, B, 4])
        xn = [sb(f"xn{i}", [T, D]) for i in range(2)]
        xT = sb("xT", [128, KC, 2 * T])
        X = sb("X", [128, N, D1])
        W = [sb(f"W{i}", [128, 8, F1]) for i in range(4)]
        pre = [sb(f"pre{i}", [F1, 512]) for i in range(2)]
        h = sb("h", [128, N, F1])
        W2 = [sb(f"W2_{i}", [128, 16, D1]) for i in range(4)]
        y = sb("y", [D1, N, D1])
        yT = sb("yT", [128, KC, 2 * T])
        logits = [sb(f"logits{i}", [N, E]) for i in range(2)]
        top = [sb(f"top{i}", [N, 8]) for i in range(2)]
        which = [sb(f"which{i}", [N, 8], U32) for i in range(2)]
        which8 = [sb(f"which8_{i}", [N, 2], U8) for i in range(2)]
        prob = [sb(f"prob{i}", [N, 8]) for i in range(2)]
        diag = [sb(f"diag{i}", [N, N, 2]) for i in range(2)]
        pb = [sb(f"prob_rows{i}", [F1, 2 * N]) for i in range(2)]
        row = [sb(f"index_row{i}", [1, 2 * N], U8) for i in range(2)]
        waited = sb("waited", [1, 8])

        loaded, tables, zeroed, oned = sem("loaded"), sem("tables"), sem("zeroed"), sem("oned")
        s_stats, s_var, s_rstd, s_xn = sem("stats"), sem("var"), sem("rstd"), sem("xn")
        s_X, s_h, s_pre, s_yT = sem("X"), sem("h"), sem("pre"), sem("yT")
        s_top, s_which, s_which8, s_diff, s_exp = sem("top"), sem("which"), sem("which8"), sem("diff"), sem("exp")
        s_den, s_p0, s_p1, s_diag = sem("den"), sem("p0"), sem("p1"), sem("diag")
        s_index = [sem("index_up"), sem("index_down")]

        UP_W, UP_H, DN_W = N // 4, N // 8, N // 8
        names = [("xT", 0), ("xT", 1), ("logits", 0), ("probs", 0)]
        for w in range(UP_W + 1):
            names += [("W", w)] * (w < UP_W) + [("h", (w - 1) // 2)] * (w >= 1 and (w - 1) % 2 == 0)
        names += [("logits", 1), ("probs", 1)]
        for w in range(DN_W + 1):
            names += [("W2", w)] * (w < DN_W) + [("y", w - 1)] * (w >= 1)
        names += [("back", 0), ("back", 1)]
        ring = Ring(env, names)
        block = ctx.enter_context(nc.Block())

        @block.sync
        def _(sp):
            sp.dma_start(router_up[:], w_up).then_inc(loaded, 16)
            sp.dma_start(bias_u[:], bias_up).then_inc(loaded, 16)
            sp.dma_start(bias_d[:], bias_down).then_inc(loaded, 16)
            sp.dma_start(scale[:], scales.rearrange("(o d) -> o d", o=1).to_broadcast([F1, 2])).then_inc(loaded, 16)
            sp.wait_ge(zeroed, 15)
            sp.dma_start(router_down[0:F1], w_down).then_inc(tables, 16)
            sp.dma_start(first_up[0:D1], b_up).then_inc(tables, 16)
            sp.dma_start(second_up[0:D1], a_up).then_inc(tables, 16)
            sp.dma_start(first_down[0:F1], b_down).then_inc(tables, 16)
            sp.dma_start(second_down[0:F1], a_down).then_inc(tables, 16)
            with sp.Fori(0, PAIRS) as t:
                for layer in range(2):
                    sp.wait_ge(s_which8, t * 2 + (layer + 1))
                    sp.dma_start(row[layer][:].rearrange("o (n k) -> o n k", k=2),
                                 which8[layer][:]).then_inc(s_index[layer], 16)

        @block.gpsimd
        def _(pool):
            for z in [router_down, first_up, second_up, first_down, second_down, X, *W, h, *W2]:
                pool.memset(z[:], 0.0).then_inc(zeroed, 1)
            pool.memset(ones[:], 1.0).then_inc(oned, 1)
            pool.wait_ge(s_var, 1)
            pool.tensor_tensor(mv[:, :, 3], mv[:, :, 2], env.minus_half[0:T, 0:B], ALU.pow).then_inc(s_rstd, 1)

        @block.scalar
        def _(act):
            act.wait_ge(loaded, 64)
            act.wait_ge(zeroed, 15)
            with act.Fori(0, PAIRS) as t:
                for par in range(2):
                    src = ring.wait_full(act, ("xT", par), t)
                    act.copy(xT[:, :, par * T:(par + 1) * T],
                             src[:, 0:KC * T].rearrange("p (k n) -> p k n", k=KC)).then_inc(ring.free(("xT", par)), 1)
                ring.wait_read(act, ("xT", 1), t)
                for ci in range(8):
                    k, q = divmod(ci, 4)
                    last = act.copy(X[0:D1].rearrange("p n (r c) -> p (n r) c", c=8)[:, :, ci],
                                    xT[32 * q:32 * q + 32, k, :])
                last.then_inc(s_X, 1)
                for layer in range(2):
                    act.wait_ge(s_diff, t * 2 + (layer + 1))
                    act.activation(prob[layer][:, 1:2], prob[layer][:, 0:1], ACT.Exp).then_inc(s_exp, 1)
                    if layer == 0:
                        for w in range(UP_H):
                            ring.wait_read(act, ("h", w), t)
                            act.activation(h[0:F1, 8 * w:8 * w + 8, :].rearrange("p n o -> p (n o)"),
                                           pre[w % 2][:], ACT.Gelu).then_inc(s_h, 1)
                ring.wait_read(act, ("y", DN_W - 1), t)
                for ci in range(8):
                    k, q = divmod(ci, 4)
                    last = act.copy(yT[32 * q:32 * q + 32, k, :],
                                    y[:].rearrange("p n (r c) -> p (n r) c", c=8)[:, :, ci])
                last.then_inc(s_yT, 1)

        @block.vector
        def _(dve):
            norm_columns(dve, mv, stats, lambda k: env.x[:, k, :], B, T, s_stats, s_var, 1.0, EPS)
            dve.wait_ge(s_rstd, 1)
            dve.wait_ge(loaded, 64)
            dve.wait_ge(zeroed, 15)

            def route(layer, t):
                n = t * 2 + (layer + 1)
                p = prob[layer]
                src = ring.wait_full(dve, ("logits", layer), t)
                dve.tensor_copy(logits[layer][:], src[0:N, 0:E]).then_inc(ring.free(("logits", layer)), 1)
                ring.wait_read(dve, ("logits", layer), t)
                dve.tensor_copy(waited[:, 4 * layer:4 * layer + 1], logits[layer][0:1, 0:1])
                dve.max(top[layer][:], logits[layer][:]).then_inc(s_top, 1)
                dve.wait_ge(s_top, n)
                dve.tensor_tensor(p[:, 0:1], top[layer][:, 1:2], top[layer][:, 0:1], ALU.subtract)\
                    .then_inc(s_diff, 1)
                dve.max_index(which[layer][:], top[layer][:], logits[layer][:]).then_inc(s_which, 1)
                dve.wait_ge(s_which, n)
                dve.tensor_copy(which8[layer][:], which[layer][:, 0:2]).then_inc(s_which8, 1)
                dve.wait_ge(s_exp, n)
                dve.tensor_scalar(p[:, 2:3], p[:, 1:2], 1.0, None, ALU.add).then_inc(s_den, 1)
                dve.wait_ge(s_den, n)
                dve.reciprocal(p[:, 3:4], p[:, 2:3]).then_inc(s_p0, 1)
                dve.wait_ge(s_p0, n)
                dve.tensor_tensor(p[:, 4:5], p[:, 1:2], p[:, 3:4], ALU.mult).then_inc(s_p1, 1)
                dve.wait_ge(s_p1, n)
                dve.tensor_tensor(diag[layer][:], spread(env.ident[0:N, 0:N], 2),
                                  p[:, 3:5].rearrange("p (o k) -> p o k", o=1).to_broadcast([N, N, 2]),
                                  ALU.mult).then_inc(s_diag, 1)
                src = ring.wait_full(dve, ("probs", layer), t)
                dve.tensor_copy(pb[layer][:], src[0:F1, 0:2 * N]).then_inc(ring.free(("probs", layer)), 1)
                ring.wait_read(dve, ("probs", layer), t)

            with dve.Fori(0, PAIRS) as t:
                for par in range(2):
                    b = t * 2 + par
                    xb = env.x[:, bass.ds(b, 1), :].rearrange("p a d -> p (a d)")
                    dve.tensor_scalar(xn[par][:], xb, mv[:, bass.ds(b, 1), 0:1].rearrange("p a o -> p (a o)"),
                                      mv[:, bass.ds(b, 1), 3:4].rearrange("p a o -> p (a o)"),
                                      ALU.subtract, ALU.mult).then_inc(s_xn, 1)
                route(0, t)
                for w in range(UP_W + 1):
                    if w < UP_W:
                        src = ring.wait_full(dve, ("W", w), t)
                        dve.tensor_tensor(W[w % 4][0:D1], src[0:D1, :].rearrange("p (n f) -> p n f", n=8),
                                          spread(pb[0][0:D1, 8 * w:8 * w + 8], F1), ALU.mult)\
                            .then_inc(ring.free(("W", w)), 1)
                    if w >= 2 and w % 2 == 0:
                        m = w // 2 - 1
                        if m >= 2:
                            dve.wait_ge(s_h, t * UP_H + (m - 1))
                        src = ring.wait_full(dve, ("h", m), t)
                        dve.scalar_tensor_tensor(pre[m % 2][:].rearrange("p (n o) -> p n o", n=8),
                                                 src[0:F1, :].rearrange("p (n o) -> p n o", n=8), scale[:, 0:1],
                                                 bias_u[:].rearrange("p (a o) -> p a o", a=1)
                                                 .to_broadcast([F1, 8, F1]), ALU.mult, ALU.add)\
                            .then_inc(ring.free(("h", m)), 1)
                route(1, t)
                for w in range(DN_W + 1):
                    if w < DN_W:
                        src = ring.wait_full(dve, ("W2", w), t)
                        dve.tensor_tensor(W2[w % 4][0:F1], src[0:F1, :].rearrange("p (n f) -> p n f", n=16),
                                          spread(pb[1][:, 16 * w:16 * w + 16], D1), ALU.mult)\
                            .then_inc(ring.free(("W2", w)), 1)
                    if w >= 1:
                        u = w - 1
                        src = ring.wait_full(dve, ("y", u), t)
                        dve.scalar_tensor_tensor(y[:, 8 * u:8 * u + 8, :],
                                                 src[0:D1, 0:8 * D1].rearrange("p (n o) -> p n o", n=8),
                                                 scale[0:D1, 1:2],
                                                 bias_d[:].rearrange("p (a o) -> p a o", a=1)
                                                 .to_broadcast([D1, 8, D1]), ALU.mult, ALU.add)\
                            .then_inc(ring.free(("y", u)), 1)
                for par in range(2):
                    b = t * 2 + par
                    xb = env.x[:, bass.ds(b, 1), :].rearrange("p a d -> p (a d)")
                    src = ring.wait_full(dve, ("back", par), t)
                    dve.tensor_tensor(xb, xb, src[0:T, 0:D], ALU.add).then_inc(ring.free(("back", par)), 1)

        @block.tensor
        def _(pe):
            pe.wait_ge(tables, 80)
            pe.wait_ge(loaded, 64)
            pe.wait_ge(zeroed, 15)
            pe.wait_ge(oned, 1)

            def picked(layer, first, count):
                _, got = nc.values_load_multi_w_load_instructions(
                    row[layer][0:1, first:first + count], engines=[mybir.EngineType.PE],
                    min_val=0, max_val=E - 1,
                    skip_runtime_bounds_check_because="max_index over E logits yields 0 .. E - 1")
                return got

            def probs(layer, t):
                out = ring.wait_free(pe, ("probs", layer), t)
                pe.wait_ge(s_index[layer], t * 16 + 16)
                if layer == 0:
                    pe.wait_ge(s_X, t + 1)
                pe.wait_ge(s_diag, t * 2 + (layer + 1))
                pe.matmul(out[:, 0:2 * N], ones[:], diag[layer][:].rearrange("p n k -> p (n k)"),
                          start=True, stop=True).then_inc(ring.full(("probs", layer)), 1)

            with pe.Fori(0, PAIRS) as t:
                for par in range(2):
                    out = ring.wait_free(pe, ("xT", par), t)
                    pe.wait_ge(s_xn, t * 2 + (par + 1))
                    transposes(pe, env, out, xn[par], T, 128, KC).then_inc(ring.full(("xT", par)), 1)
                out = ring.wait_free(pe, ("logits", 0), t)
                ring.wait_read(pe, ("xT", 1), t)
                for r in range(4):
                    for k in range(KC):
                        last = pe.matmul(out[0:N, 0:E], xT[:, k, r::4], router_up[:, KC * r + k, :],
                                         start=r + k == 0, stop=r == 3 and k == KC - 1)
                last.then_inc(ring.full(("logits", 0)), 1)
                probs(0, t)
                for w in range(UP_W + 1):
                    if w < UP_W:
                        experts = picked(0, 8 * w, 8)
                        out = ring.wait_free(pe, ("W", w), t)
                        for m in range(8):
                            last = pe.matmul(out[0:D1, m * F1:(m + 1) * F1], X[:, 4 * w + m // 2, :],
                                             first_up[:, bass.ds(experts[m], 1), :].rearrange("p a f -> p (a f)"),
                                             start=True, stop=True)
                        last.then_inc(ring.full(("W", w)), 1)
                    if w >= 1:
                        u = w - 1
                        experts = picked(0, 8 * u, 8)
                        out = ring.wait_free(pe, ("h", u // 2), t) if u % 2 == 0 else ring.bank(("h", u // 2))
                        ring.wait_read(pe, ("W", u), t)
                        for m in range(8):
                            at = (u % 2) * 4 + m // 2
                            last = pe.matmul(out[0:F1, at * F1:(at + 1) * F1], W[u % 4][:, m, :],
                                             second_up[:, bass.ds(experts[m], 1), :].rearrange("p a f -> p (a f)"),
                                             start=m % 2 == 0, stop=m % 2 == 1)
                        if u % 2 == 1:
                            last.then_inc(ring.full(("h", u // 2)), 1)
                out = ring.wait_free(pe, ("logits", 1), t)
                pe.wait_ge(s_h, t * UP_H + UP_H)
                for i in range(F1):
                    last = pe.matmul(out[0:N, 0:E], h[:, :, i], router_down[:, i, :],
                                     start=i == 0, stop=i == F1 - 1)
                last.then_inc(ring.full(("logits", 1)), 1)
                probs(1, t)
                for w in range(DN_W + 1):
                    if w < DN_W:
                        experts = picked(1, 16 * w, 16)
                        out = ring.wait_free(pe, ("W2", w), t)
                        for m in range(16):
                            last = pe.matmul(out[0:F1, m * D1:(m + 1) * D1], h[:, 8 * w + m // 2, :],
                                             first_down[:, bass.ds(experts[m], 1), :].rearrange("p a f -> p (a f)"),
                                             start=True, stop=True)
                        last.then_inc(ring.full(("W2", w)), 1)
                    if w >= 1:
                        u = w - 1
                        experts = picked(1, 16 * u, 16)
                        out = ring.wait_free(pe, ("y", u), t)
                        ring.wait_read(pe, ("W2", u), t)
                        for m in range(16):
                            at = m // 2
                            last = pe.matmul(out[0:D1, at * D1:(at + 1) * D1], W2[u % 4][:, m, :],
                                             second_down[:, bass.ds(experts[m], 1), :].rearrange("p a f -> p (a f)"),
                                             start=m % 2 == 0, stop=m % 2 == 1)
                        last.then_inc(ring.full(("y", u)), 1)
                pe.wait_ge(s_yT, t + 1)
                for par in range(2):
                    out = ring.wait_free(pe, ("back", par), t)
                    for k in range(KC):
                        last = pe.transpose(out[0:T, k * 128:(k + 1) * 128], yT[:, k, par * T:(par + 1) * T],
                                            env.ident[:])
                    last.then_inc(ring.full(("back", par)), 1)
        ring.close(PAIRS)


def phase_self_attention_scaled(nc, env, head_mask):
    ctx = ExitStack()
    with ctx:
        sb, sem = tools(nc, ctx, "scaled")
        DH, UNITS = 16, 8
        own = sb("own_features", [128, 8])
        scaled = sb("scaled_features", [128, KC, 8])
        stats = sb("stats", [T, B, 6])
        mv = sb("mean_var", [T, B, 4])
        xn = [sb(f"xn{i}", [T, D]) for i in range(2)]
        v = [sb(f"v{i}", [T, H, DH + 1]) for i in range(2)]
        xT = [sb(f"xT{i}", [128, KC, T]) for i in range(2)]
        km = [sb(f"km{i}", [128, H, T]) for i in range(2)]
        P = [sb(f"P{i}", [T, 4 * T]) for i in range(4)]
        PT = [sb(f"PT{i}", [T, 4 * T]) for i in range(2)]
        mx = sb("max", [T, UNITS, 4])
        rs = sb("recip", [T, UNITS, 4])
        o = [sb(f"o{i}", [T, D]) for i in range(2)]

        loaded, ones = sem("loaded"), sem("ones")
        s_stats, s_var, s_rstd, s_xn, s_own = sem("stats"), sem("var"), sem("rstd"), sem("xn"), sem("own")
        s_v, s_km, s_max, s_exp, s_sum, s_res = sem("v"), sem("km"), sem("max"), sem("exp"), sem("sum"), sem("res")

        units = [(g, par) for g in range(4) for par in range(2)]
        names = [("xT", par) for par in range(2)]
        for u in range(UNITS + 3):
            names += [("S", u)] * (u < UNITS) + [("PT", u - 2)] * (0 <= u - 2 < UNITS) + [("O", u - 3)] * (u >= 3)
        ring = Ring(env, names)
        block = ctx.enter_context(nc.Block())

        @block.sync
        def _(sp):
            sp.dma_start(own[:], head_mask).then_inc(loaded, 16)
            sp.wait_ge(loaded, 16)

        @block.gpsimd
        def _(pool):
            for i in range(2):
                pool.memset(v[i][:], 1.0).then_inc(ones, 1)
            pool.wait_ge(s_var, 1)
            pool.tensor_tensor(mv[:, :, 3], mv[:, :, 2], env.minus_half[0:T, 0:B], ALU.pow).then_inc(s_rstd, 1)

        @block.scalar
        def _(act):
            act.wait_ge(ones, 2)
            with act.Fori(0, PAIRS) as t:
                for par in range(2):
                    src = ring.wait_full(act, ("xT", par), t)
                    act.copy(xT[par][:].rearrange("p k n -> p (k n)"), src[:, 0:KC * T])\
                        .then_inc(ring.free(("xT", par)), 1)
                    act.wait_ge(s_xn, t * 2 + (par + 1))
                    act.copy(v[par][:, :, 0:DH], heads(xn[par][:], H, DH)).then_inc(s_v, 1)
                for u in range(UNITS + 2):
                    if u < UNITS:
                        ring.wait_read(act, ("S", u), t)
                        act.activation(P[u % 4][:], P[u % 4][:], ACT.Exp).then_inc(s_exp, 1)
                    if u >= 2:
                        src = ring.wait_full(act, ("PT", u - 2), t)
                        act.copy(PT[u % 2][:], src[0:T, 0:4 * T]).then_inc(ring.free(("PT", u - 2)), 1)

        @block.vector
        def _(dve):
            dve.wait_ge(loaded, 16)
            for k in range(KC):
                dve.tensor_scalar(scaled[:, k, :], own[:], env.col("rotation", k), env.col("entangle", k),
                                  ALU.mult, ALU.mult).then_inc(s_own, 1)
            norm_columns(dve, mv, stats, lambda k: env.x[:, k, :], B, T, s_stats, s_var, 1.0, EPS)
            dve.wait_ge(s_rstd, 1)
            dve.wait_ge(s_own, 2)
            with dve.Fori(0, PAIRS) as t:
                for par in range(2):
                    b = t * 2 + par
                    xb = env.x[:, bass.ds(b, 1), :].rearrange("p a d -> p (a d)")
                    dve.tensor_scalar(xn[par][:], xb, mv[:, bass.ds(b, 1), 0:1].rearrange("p a o -> p (a o)"),
                                      mv[:, bass.ds(b, 1), 3:4].rearrange("p a o -> p (a o)"),
                                      ALU.subtract, ALU.mult).then_inc(s_xn, 1)
                for par in range(2):
                    ring.wait_read(dve, ("xT", par), t)
                    for k in range(KC):
                        dve.tensor_tensor(km[par][:, 8 * k:8 * k + 8, :],
                                          xT[par][:, k, :].rearrange("p (a n) -> p a n", a=1)
                                          .to_broadcast([128, 8, T]), spread(scaled[:, k, :], T), ALU.mult)\
                            .then_inc(s_km, 1)
                for u in range(UNITS + 3):
                    if u < UNITS:
                        src = ring.wait_full(dve, ("S", u), t)
                        s4 = heads(src[0:T, 0:4 * T], 4, T)
                        dve.tensor_reduce(mx[:, u, :], s4, AX.X, ALU.max).then_inc(s_max, 1)
                        dve.wait_ge(s_max, t * UNITS + (u + 1))
                        dve.tensor_tensor(heads(P[u % 4][:], 4, T), s4, spread(mx[:, u, :], T),
                                          ALU.subtract).then_inc(ring.free(("S", u)), 1)
                    if u >= 3:
                        w = u - 3
                        g, par = units[w]
                        src = ring.wait_full(dve, ("O", w), t)
                        o4 = heads(src[0:T, 0:4 * (DH + 1)], 4, DH + 1)
                        dve.reciprocal(rs[:, w, :], o4[:, :, DH]).then_inc(s_sum, 1)
                        dve.wait_ge(s_sum, t * UNITS + (w + 1))
                        dve.tensor_tensor(heads(o[par][:, g * 4 * DH:(g + 1) * 4 * DH], 4, DH), o4[:, :, 0:DH],
                                          spread(rs[:, w, :], DH), ALU.mult).then_inc(ring.free(("O", w)), 1)
                for par in range(2):
                    b = t * 2 + par
                    xb = env.x[:, bass.ds(b, 1), :].rearrange("p a d -> p (a d)")
                    ring.wait_read(dve, ("O", UNITS - 2 + par), t)
                    dve.tensor_tensor(xb, xb, o[par][:], ALU.add).then_inc(s_res, 1)

        @block.tensor
        def _(pe):
            with pe.Fori(0, PAIRS) as t:
                for par in range(2):
                    out = ring.wait_free(pe, ("xT", par), t)
                    pe.wait_ge(s_xn, t * 2 + (par + 1))
                    transposes(pe, env, out, xn[par], T, 128, KC).then_inc(ring.full(("xT", par)), 1)
                for u in range(UNITS + 3):
                    if u < UNITS:
                        g, par = units[u]
                        out = ring.wait_free(pe, ("S", u), t)
                        pe.wait_ge(s_km, t * 4 + (2 * par + g // 2 + 1))
                        pe.matmul(out[0:T, 0:4 * T], xT[par][:, g // 2, :],
                                  km[par][:, 4 * g:4 * g + 4, :].rearrange("p a b -> p (a b)"),
                                  start=True, stop=True).then_inc(ring.full(("S", u)), 1)
                    if 0 <= u - 2 < UNITS:
                        w = u - 2
                        out = ring.wait_free(pe, ("PT", w), t)
                        pe.wait_ge(s_exp, t * UNITS + (w + 1))
                        transposes(pe, env, out, P[w % 4], T, T, 4).then_inc(ring.full(("PT", w)), 1)
                    if u >= 3:
                        w = u - 3
                        g, par = units[w]
                        out = ring.wait_free(pe, ("O", w), t)
                        ring.wait_read(pe, ("PT", w), t)
                        pe.wait_ge(s_v, t * 2 + (par + 1))
                        for i in range(4):
                            last = pe.matmul(out[0:T, i * (DH + 1):(i + 1) * (DH + 1)],
                                             PT[w % 2][:, i * T:(i + 1) * T], v[par][:, 4 * g + i, :],
                                             start=True, stop=True)
                        last.then_inc(ring.full(("O", w)), 1)
        ring.close(PAIRS)


def phase_cross_attention_queries(nc, env, ctx_rows, head_mask, w_q, w_k, w_v, w_o, b_v, b_o):
    ctx = ExitStack()
    with ctx:
        sb, sem = tools(nc, ctx, "over")
        DH, UNITS, NT = 16, 8, C // CT
        wq, wk, wv, wo = (sb(n, [128, KC, D]) for n in ("w_q", "w_k", "w_v", "w_o"))
        bv = sb("b_v", [CT, D])
        bo = sb("b_o", [T, D])
        own = sb("own_features", [128, 8])
        rows_in = sb("ctx", [CT, B * NT, D])
        rows_now = [sb(f"ctx_now{i}", [CT, NT, D]) for i in range(2)]
        stats = sb("stats", [T, B, 6])
        mv = sb("mean_var", [T, B, 4])
        xn = [sb(f"xn{i}", [T, D]) for i in range(2)]
        xT = [sb(f"xT{i}", [128, KC, T]) for i in range(2)]
        qT = [sb(f"qT{i}", [128, KC, T]) for i in range(2)]
        qm = [sb(f"qm{i}", [128, H, T]) for i in range(2)]
        cT = [sb(f"cT{i}", [128, KC, C]) for i in range(2)]
        kT = [sb(f"kT{i}", [128, KC, C]) for i in range(2)]
        v = [sb(f"v{i}", [CT, NT, D]) for i in range(2)]
        P = [sb(f"P{i}", [CT, 4 * T]) for i in range(6)]
        V = [sb(f"V{i}", [CT, 4 * DH]) for i in range(6)]
        SUB = UNITS * NT
        mx = sb("max", [CT, SUB, 4])
        rs = sb("recip", [CT, SUB, 8])
        o = [sb(f"o{i}", [T, D]) for i in range(2)]
        oT = [sb(f"oT{i}", [128, KC, T]) for i in range(2)]
        res = [sb(f"res{i}", [T, D]) for i in range(2)]

        loaded = sem("loaded")
        s_stats, s_var, s_rstd, s_xn = sem("stats"), sem("var"), sem("rstd"), sem("xn")
        s_rows = sem("rows")
        s_qm, s_max, s_exp, s_den, s_rec, s_V, s_res = (sem(n) for n in ("qm", "max", "exp", "den", "rec", "V", "res"))

        units = [(g, par) for g in range(4) for par in range(2)]
        names = [("xT", 0), ("xT", 1)]
        names += [("cT", par, c) for par in range(2) for c in range(NT)]
        names += [("qT", 0), ("qT", 1)]
        names += [("kT", par, m) for par in range(2) for m in range(KC)]
        names += [("v", par, c) for par in range(2) for c in range(NT)]
        for u in range(SUB + 3):
            names += [("S", u)] * (u < SUB) + [("O", u // 3 - 1)] * (u >= 3 and u % 3 == 2)
        names += [("oT", 0), ("oT", 1), ("out", 0), ("out", 1)]
        ring = Ring(env, names)
        block = ctx.enter_context(nc.Block())

        @block.sync
        def _(sp):
            sp.dma_start(own[:], head_mask).then_inc(loaded, 16)
            for w, src in ((wq, w_q), (wk, w_k), (wv, w_v), (wo, w_o)):
                sp.dma_start(w[:], src.rearrange("(k p) n -> p k n", p=128)).then_inc(loaded, 16)
            sp.dma_start(bv[:], b_v.rearrange("(o d) -> o d", o=1).to_broadcast([CT, D])).then_inc(loaded, 16)
            sp.dma_start(bo[:], b_o.rearrange("(o d) -> o d", o=1).to_broadcast([T, D])).then_inc(loaded, 16)
            sp.dma_start(rows_in[:], ctx_rows.rearrange("b (c p) d -> p (b c) d", p=CT)).then_inc(loaded, 16)
            sp.wait_ge(loaded, 128)

        @block.gpsimd
        def _(pool):
            pool.wait_ge(s_var, 1)
            pool.tensor_tensor(mv[:, :, 3], mv[:, :, 2], env.minus_half[0:T, 0:B], ALU.pow).then_inc(s_rstd, 1)

        @block.scalar
        def _(act):
            with act.Fori(0, PAIRS) as t:
                for par in range(2):
                    src = ring.wait_full(act, ("xT", par), t)
                    act.copy(xT[par][:].rearrange("p k n -> p (k n)"), src[:, 0:KC * T])\
                        .then_inc(ring.free(("xT", par)), 1)
                for par in range(2):
                    for c in range(NT):
                        src = ring.wait_full(act, ("cT", par, c), t)
                        act.copy(cT[par][:, :, c * CT:(c + 1) * CT],
                                 src[:, 0:KC * CT].rearrange("p (k n) -> p k n", k=KC))\
                            .then_inc(ring.free(("cT", par, c)), 1)
                for par in range(2):
                    src = ring.wait_full(act, ("qT", par), t)
                    for m in range(KC):
                        last = act.activation(qT[par][:, m, :], src[:, m * T:(m + 1) * T], ACT.Identity,
                                              bias=env.col("bq", m))
                    last.then_inc(ring.free(("qT", par)), 1)
                for par in range(2):
                    for m in range(KC):
                        src = ring.wait_full(act, ("kT", par, m), t)
                        act.activation(kT[par][:, m, :], src[:, 0:C], ACT.Identity, bias=env.col("bk", m))\
                            .then_inc(ring.free(("kT", par, m)), 1)
                for u in range(SUB + 4):
                    if u < SUB:
                        ring.wait_read(act, ("S", u), t)
                        act.activation(P[u % 6][:], P[u % 6][:], ACT.Exp, scale=DH ** -0.5).then_inc(s_exp, 1)
                    if u >= 5 and u % 3 == 2:
                        w = u // 3 - 1
                        g, par = units[w]
                        src = ring.wait_full(act, ("O", w), t)
                        act.copy(o[par][:, g * 4 * DH:(g + 1) * 4 * DH], src[0:T, 0:4 * DH])\
                            .then_inc(ring.free(("O", w)), 1)
                for par in range(2):
                    src = ring.wait_full(act, ("oT", par), t)
                    act.copy(oT[par][:].rearrange("p k n -> p (k n)"), src[:, 0:KC * T])\
                        .then_inc(ring.free(("oT", par)), 1)

        @block.vector
        def _(dve):
            norm_columns(dve, mv, stats, lambda k: env.x[:, k, :], B, T, s_stats, s_var, 1.0, EPS)
            dve.wait_ge(s_rstd, 1)
            dve.wait_ge(loaded, 128)
            with dve.Fori(0, PAIRS) as t:
                for par in range(2):
                    b = t * 2 + par
                    xb = env.x[:, bass.ds(b, 1), :].rearrange("p a d -> p (a d)")
                    dve.tensor_scalar(xn[par][:], xb, mv[:, bass.ds(b, 1), 0:1].rearrange("p a o -> p (a o)"),
                                      mv[:, bass.ds(b, 1), 3:4].rearrange("p a o -> p (a o)"),
                                      ALU.subtract, ALU.mult).then_inc(s_xn, 1)
                for par in range(2):
                    for c in range(NT):
                        row = rows_in[:, bass.ds((t * 2 + par) * NT + c, 1), :].rearrange("p a d -> p (a d)")
                        dve.tensor_copy(rows_now[par][:, c, :], row).then_inc(s_rows, 1)
                for par in range(2):
                    ring.wait_read(dve, ("qT", par), t)
                    for k in range(KC):
                        dve.tensor_tensor(qm[par][:, 8 * k:8 * k + 8, :],
                                          qT[par][:, k, :].rearrange("p (a n) -> p a n", a=1)
                                          .to_broadcast([128, 8, T]), spread(own[:], T), ALU.mult)\
                            .then_inc(s_qm, 1)
                for par in range(2):
                    for c in range(NT):
                        src = ring.wait_full(dve, ("v", par, c), t)
                        dve.tensor_tensor(v[par][:, c, :], src[0:CT, 0:D], bv[:], ALU.add)\
                            .then_inc(ring.free(("v", par, c)), 1)
                for u in range(SUB + 1):
                    if u < SUB:
                        if u >= 6:
                            ring.wait_full(dve, ("O", u // 3 - 2), t)
                        src = ring.wait_full(dve, ("S", u), t)
                        s4 = heads(src[0:CT, 0:4 * T], 4, T)
                        dve.tensor_reduce(mx[:, u, :], s4, AX.X, ALU.max).then_inc(s_max, 1)
                        dve.wait_ge(s_max, t * SUB + (u + 1))
                        dve.tensor_tensor(heads(P[u % 6][:], 4, T), s4, spread(mx[:, u, :], T),
                                          ALU.subtract).then_inc(ring.free(("S", u)), 1)
                    if u >= 1:
                        w = u - 1
                        g, par = units[w // 3]
                        n = t * SUB + (w + 1)
                        dve.wait_ge(s_exp, n)
                        dve.tensor_reduce(rs[:, w, 0:4], heads(P[w % 6][:], 4, T), AX.X, ALU.add).then_inc(s_den, 1)
                        dve.wait_ge(s_den, n)
                        dve.reciprocal(rs[:, w, 4:8], rs[:, w, 0:4]).then_inc(s_rec, 1)
                        dve.wait_ge(s_rec, n)
                        if w == 0:
                            ring.wait_read(dve, ("v", 1, NT - 1), t)
                        dve.tensor_tensor(heads(V[w % 6][:], 4, DH),
                                          heads(v[par][:, w % 3, g * 4 * DH:(g + 1) * 4 * DH], 4, DH),
                                          spread(rs[:, w, 4:8], DH), ALU.mult).then_inc(s_V, 1)
                for par in range(2):
                    b = t * 2 + par
                    xb = env.x[:, bass.ds(b, 1), :].rearrange("p a d -> p (a d)")
                    src = ring.wait_full(dve, ("out", par), t)
                    dve.tensor_tensor(res[par][:], bo[:], src[0:T, 0:D], ALU.add).then_inc(ring.free(("out", par)), 1)
                    ring.wait_read(dve, ("out", par), t)
                    dve.tensor_tensor(xb, xb, res[par][:], ALU.add).then_inc(s_res, 1)

        @block.tensor
        def _(pe):
            pe.wait_ge(loaded, 128)
            with pe.Fori(0, PAIRS) as t:
                for par in range(2):
                    out = ring.wait_free(pe, ("xT", par), t)
                    pe.wait_ge(s_xn, t * 2 + (par + 1))
                    transposes(pe, env, out, xn[par], T, 128, KC).then_inc(ring.full(("xT", par)), 1)
                for par in range(2):
                    for c in range(NT):
                        out = ring.wait_free(pe, ("cT", par, c), t)
                        pe.wait_ge(s_rows, t * 2 * NT + (par * NT + c + 1))
                        transposes(pe, env, out, rows_now[par][:, c, :], CT, 128, KC)\
                            .then_inc(ring.full(("cT", par, c)), 1)
                for par in range(2):
                    out = ring.wait_free(pe, ("qT", par), t)
                    ring.wait_read(pe, ("xT", par), t)
                    for m in range(KC):
                        for k in range(KC):
                            last = pe.matmul(out[:, m * T:(m + 1) * T], wq[:, k, m * 128:(m + 1) * 128],
                                             xT[par][:, k, :], start=k == 0, stop=k == KC - 1)
                    last.then_inc(ring.full(("qT", par)), 1)
                for par in range(2):
                    for m in range(KC):
                        out = ring.wait_free(pe, ("kT", par, m), t)
                        ring.wait_read(pe, ("cT", par, NT - 1), t)
                        for k in range(KC):
                            last = pe.matmul(out[:, 0:C], wk[:, k, m * 128:(m + 1) * 128], cT[par][:, k, :],
                                             start=k == 0, stop=k == KC - 1)
                        last.then_inc(ring.full(("kT", par, m)), 1)
                for par in range(2):
                    for c in range(NT):
                        out = ring.wait_free(pe, ("v", par, c), t)
                        for k in range(KC):
                            last = pe.matmul(out[0:CT, 0:D], cT[par][:, k, c * CT:(c + 1) * CT], wv[:, k, :],
                                             start=k == 0, stop=k == KC - 1)
                        last.then_inc(ring.full(("v", par, c)), 1)
                for u in range(SUB + 3):
                    if u < SUB:
                        g, par = units[u // 3]
                        c = u % 3
                        out = ring.wait_free(pe, ("S", u), t)
                        if c == 0:
                            pe.wait_ge(s_qm, t * 4 + (2 * par + g // 2 + 1))
                            ring.wait_read(pe, ("kT", par, g // 2), t)
                        pe.matmul(out[0:CT, 0:4 * T], kT[par][:, g // 2, c * CT:(c + 1) * CT],
                                  qm[par][:, 4 * g:4 * g + 4, :].rearrange("p a b -> p (a b)"),
                                  start=True, stop=True).then_inc(ring.full(("S", u)), 1)
                    if u >= 3 and u % 3 == 2:
                        w = u // 3 - 1
                        out = ring.wait_free(pe, ("O", w), t)
                        pe.wait_ge(s_V, t * SUB + (3 * w + 3))
                        for i in range(4):
                            for c in range(NT):
                                n = (3 * w + c) % 6
                                last = pe.matmul(out[0:T, i * DH:(i + 1) * DH], P[n][:, i * T:(i + 1) * T],
                                                 V[n][:, i * DH:(i + 1) * DH], start=c == 0, stop=c == NT - 1)
                        last.then_inc(ring.full(("O", w)), 1)
                for par in range(2):
                    out = ring.wait_free(pe, ("oT", par), t)
                    ring.wait_read(pe, ("O", UNITS - 2 + par), t)
                    transposes(pe, env, out, o[par], T, 128, KC).then_inc(ring.full(("oT", par)), 1)
                for par in range(2):
                    out = ring.wait_free(pe, ("out", par), t)
                    ring.wait_read(pe, ("oT", par), t)
                    for k in range(KC):
                        last = pe.matmul(out[0:T, 0:D], oT[par][:, k, :], wo[:, k, :], start=k == 0, stop=k == KC - 1)
                    last.then_inc(ring.full(("out", par)), 1)
        ring.close(PAIRS)


def phase_attention_over_sequences(nc, env, w_in, w_out, b_v, b_out, ln_g, ln_b, block_bias):
    ctx = ExitStack()
    with ctx:
        sb, sem = tools(nc, ctx, "mha")
        NH, DH, BL = 4, 64, T * B // 128
        win = sb("w_in", [128, KC, 3 * D])
        wo = sb("w_out", [128, KC, D])
        bv = sb("b_v", [128, D])
        bo = sb("b_out", [T, D])
        g1 = sb("ln_gamma", [T, D])
        b1 = sb("ln_beta", [T, D])
        own = sb("block_bias", [128, 128])
        xT = sb("xT", [128, KC, T, B])
        qkT = sb("qkT", [128, 4, T * B])
        v = sb("v", [128, BL, NH, DH + 1])
        P = [sb(f"P{i}", [128, NH * 128]) for i in range(4)]
        PT = [sb(f"PT{i}", [128, NH * 128]) for i in range(2)]
        mx = sb("max", [128, BL, NH])
        rs = sb("recip", [128, BL, NH])
        o = [sb(f"o{i}", [128, D]) for i in range(2)]
        oT = sb("oT", [128, KC, B, T])
        res = [sb(f"res{i}", [T, D]) for i in range(2)]
        stats = sb("stats", [T, B, 6])
        mv = sb("mean_var", [T, B, 4])
        stats0 = sb("stats_in", [T, B, 6])
        mv0 = sb("mean_var_in", [T, B, 4])
        z = [sb(f"z{i}", [T, D]) for i in range(2)]

        loaded, ones = sem("loaded"), sem("ones")
        s_add, s_max, s_sub, s_exp, s_sum = (sem(n) for n in ("add", "max", "sub", "exp", "sum"))
        s_stats0, s_var0, s_rstd0, s_in = (sem(n) for n in ("stats_in", "var_in", "rstd_in", "normed_in"))
        s_res, s_stats, s_var, s_rstd, s_z, s_g, s_y = (sem(n) for n in ("res", "stats", "var", "rstd", "z", "g", "y"))

        names = [("xT", b) for b in range(B)]
        names += [("qkT", m, n) for n in range(2) for m in range(4)]
        names += [("v", u) for u in range(BL)]
        for u in range(BL + 4):
            names += [("S", u, 0), ("S", u, 1)] * (u < BL) + [("PT", u - 2)] * (0 <= u - 2 < BL)
            names += [("O", u - 3)] * (0 <= u - 3 < BL) + [("oT", u - 4)] * (u >= 4)
        names += [("out", b) for b in range(B)]
        ring = Ring(env, names)
        block = ctx.enter_context(nc.Block())

        def rows(ap, n):
            return ap.rearrange("(o d) -> o d", o=1).to_broadcast([n, D])

        @block.sync
        def _(sp):
            sp.dma_start(win[:], w_in.rearrange("(k p) n -> p k n", p=128)).then_inc(loaded, 16)
            sp.dma_start(wo[:], w_out.rearrange("(k p) n -> p k n", p=128)).then_inc(loaded, 16)
            sp.dma_start(own[:], block_bias).then_inc(loaded, 16)
            sp.dma_start(bv[:], rows(b_v, 128)).then_inc(loaded, 16)
            for dst, src in ((bo, b_out), (g1, ln_g), (b1, ln_b)):
                sp.dma_start(dst[:], rows(src, T)).then_inc(loaded, 16)
            sp.wait_ge(loaded, 112)

        @block.gpsimd
        def _(pool):
            pool.memset(v[:], 1.0).then_inc(ones, 1)
            pool.wait_ge(s_var0, 1)
            pool.tensor_tensor(mv0[:, :, 3], mv0[:, :, 2], env.minus_half[0:T, 0:B], ALU.pow).then_inc(s_rstd0, 1)
            pool.wait_ge(s_var, 1)
            pool.tensor_tensor(mv[:, :, 3], mv[:, :, 2], env.minus_half[0:T, 0:B], ALU.pow).then_inc(s_rstd, 1)

        @block.scalar
        def _(act):
            for b in range(B):
                src = ring.wait_full(act, ("xT", b), 0)
                act.copy(xT[:, :, :, b], src[:, 0:KC * T].rearrange("p (k n) -> p k n", k=KC))\
                    .then_inc(ring.free(("xT", b)), 1)
            for n in range(2):
                for m in range(4):
                    src = ring.wait_full(act, ("qkT", m, n), 0)
                    act.activation(qkT[:, m, n * 448:(n + 1) * 448], src[:, 0:448], ACT.Identity,
                                   bias=env.col("in_proj_b", m)).then_inc(ring.free(("qkT", m, n)), 1)
            for u in range(BL + 4):
                if u < BL:
                    act.wait_ge(s_sub, u + 1)
                    act.activation(P[u % 4][:], P[u % 4][:], ACT.Exp, scale=DH ** -0.5).then_inc(s_exp, 1)
                if 0 <= u - 2 < BL:
                    src = ring.wait_full(act, ("PT", u - 2), 0)
                    act.copy(PT[u % 2][:], src[:, :]).then_inc(ring.free(("PT", u - 2)), 1)
                if u >= 4:
                    w = u - 4
                    src = ring.wait_full(act, ("oT", w), 0)
                    for k in range(KC):
                        last = act.copy(oT[:, k, :, 16 * w:16 * w + 16].rearrange("p l n -> p n l"),
                                        src[:, k * 128:(k + 1) * 128].rearrange("p (n l) -> p n l", l=B))
                    last.then_inc(ring.free(("oT", w)), 1)

        @block.vector
        def _(dve):
            norm_columns(dve, mv0, stats0, lambda k: env.x[:, k, :], B, T, s_stats0, s_var0, 1.0, EPS)
            dve.wait_ge(s_rstd0, 1)
            for b in range(B):
                dve.tensor_scalar(env.y[:, b, :], env.x[:, b, :], mv0[:, b, 0:1], mv0[:, b, 3:4],
                                  ALU.subtract, ALU.mult).then_inc(s_in, 1)
            dve.wait_ge(loaded, 112)
            dve.wait_ge(ones, 1)
            for u in range(BL):
                src = ring.wait_full(dve, ("v", u), 0)
                dve.tensor_tensor(v[:, u, :, 0:DH], heads(src[:, 0:D], NH, DH), heads(bv[:], NH, DH), ALU.add)\
                    .then_inc(ring.free(("v", u)), 1)
            for u in range(BL + 3):
                if u < BL:
                    p4 = heads(P[u % 4][:], NH, 128)
                    for a in range(2):
                        src = ring.wait_full(dve, ("S", u, a), 0)
                        dve.tensor_tensor(p4[:, 2 * a:2 * a + 2, :], heads(src[:, 0:256], 2, 128),
                                          own[:].rearrange("p (a n) -> p a n", a=1).to_broadcast([128, 2, 128]),
                                          ALU.add).then_inc(ring.free(("S", u, a)), 1)
                        ring.wait_read(dve, ("S", u, a), 0)
                    dve.tensor_reduce(mx[:, u, :], p4, AX.X, ALU.max).then_inc(s_max, 1)
                    dve.wait_ge(s_max, u + 1)
                    dve.tensor_tensor(p4, p4, spread(mx[:, u, :], 128), ALU.subtract).then_inc(s_sub, 1)
                if u >= 3:
                    w = u - 3
                    src = ring.wait_full(dve, ("O", w), 0)
                    o4 = heads(src[:, 0:NH * (DH + 1)], NH, DH + 1)
                    dve.reciprocal(rs[:, w, :], o4[:, :, DH]).then_inc(s_sum, 1)
                    dve.wait_ge(s_sum, w + 1)
                    dve.tensor_tensor(heads(o[w % 2][:], NH, DH), o4[:, :, 0:DH], spread(rs[:, w, :], DH),
                                      ALU.mult).then_inc(ring.free(("O", w)), 1)
            for b in range(B):
                src = ring.wait_full(dve, ("out", b), 0)
                if b >= 2:
                    dve.wait_ge(s_res, b - 1)
                dve.tensor_tensor(res[b % 2][:], bo[:], src[0:T, 0:D], ALU.add).then_inc(ring.free(("out", b)), 1)
                ring.wait_read(dve, ("out", b), 0)
                dve.tensor_tensor(env.y[:, b, :], env.y[:, b, :], res[b % 2][:], ALU.add).then_inc(s_res, 1)
            dve.wait_ge(s_res, B)
            norm_columns(dve, mv, stats, lambda k: env.y[:, k, :], B, T, s_stats, s_var, 1.0, EPS)
            dve.wait_ge(s_rstd, 1)
            normalise_rows(dve, env, mv, z, g1, b1, s_z, s_g, s_y)

        @block.tensor
        def _(pe):
            pe.wait_ge(loaded, 112)
            for b in range(B):
                out = ring.wait_free(pe, ("xT", b), 0)
                pe.wait_ge(s_in, b + 1)
                transposes(pe, env, out, env.y[:, b, :], T, 128, KC).then_inc(ring.full(("xT", b)), 1)
            for b in range(B):
                ring.wait_read(pe, ("xT", b), 0)
            cols = xT[:].rearrange("p k n l -> p k (n l)")
            for n in range(2):
                for m in range(4):
                    out = ring.wait_free(pe, ("qkT", m, n), 0)
                    for k in range(KC):
                        last = pe.matmul(out[:, 0:448], win[:, k, m * 128:(m + 1) * 128],
                                         cols[:, k, n * 448:(n + 1) * 448], start=k == 0, stop=k == KC - 1)
                    last.then_inc(ring.full(("qkT", m, n)), 1)
            for u in range(BL):
                out = ring.wait_free(pe, ("v", u), 0)
                for k in range(KC):
                    last = pe.matmul(out[:, 0:D], cols[:, k, u * 128:(u + 1) * 128], win[:, k, 2 * D:3 * D],
                                     start=k == 0, stop=k == KC - 1)
                last.then_inc(ring.full(("v", u)), 1)
            for n in range(2):
                for m in range(4):
                    ring.wait_read(pe, ("qkT", m, n), 0)
            for u in range(BL + 4):
                if u < BL:
                    for a in range(2):
                        out = ring.wait_free(pe, ("S", u, a), 0)
                        rows_a = slice(64 * a, 64 * a + 64)
                        for j in range(2):
                            last = pe.matmul(out[:, j * 128:(j + 1) * 128],
                                             qkT[rows_a, j, u * 128:(u + 1) * 128],
                                             qkT[rows_a, 2 + j, u * 128:(u + 1) * 128], start=True, stop=True)
                        last.then_inc(ring.full(("S", u, a)), 1)
                if 0 <= u - 2 < BL:
                    w = u - 2
                    out = ring.wait_free(pe, ("PT", w), 0)
                    pe.wait_ge(s_exp, w + 1)
                    transposes(pe, env, out, P[w % 4], 128, 128, NH).then_inc(ring.full(("PT", w)), 1)
                if 0 <= u - 3 < BL:
                    w = u - 3
                    out = ring.wait_free(pe, ("O", w), 0)
                    ring.wait_read(pe, ("PT", w), 0)
                    ring.wait_read(pe, ("v", w), 0)
                    for h in range(NH):
                        i = (h % 2) * 2 + h // 2
                        last = pe.matmul(out[:, h * (DH + 1):(h + 1) * (DH + 1)],
                                         PT[w % 2][:, i * 128:(i + 1) * 128], v[:, w, h, :], start=True, stop=True)
                    last.then_inc(ring.full(("O", w)), 1)
                if u >= 4:
                    w = u - 4
                    out = ring.wait_free(pe, ("oT", w), 0)
                    ring.wait_read(pe, ("O", w), 0)
                    transposes(pe, env, out, o[w % 2], 128, 128, KC).then_inc(ring.full(("oT", w)), 1)
            ring.wait_read(pe, ("oT", BL - 1), 0)
            for b in range(B):
                out = ring.wait_free(pe, ("out", b), 0)
                for k in range(KC):
                    last = pe.matmul(out[0:T, 0:D], oT[:, k, b, :], wo[:, k, :], start=k == 0, stop=k == KC - 1)
                last.then_inc(ring.full(("out", b)), 1)
        ring.close(1)


def normalise_rows(dve, env, mv, z, gamma, beta, s_z, s_g, s_y):
    for b in range(B):
        if b >= 2:
            dve.wait_ge(s_y, b - 1)
        dve.tensor_scalar(z[b % 2][:], env.y[:, b, :], mv[:, b, 0:1], mv[:, b, 3:4],
                          ALU.subtract, ALU.mult).then_inc(s_z, 1)
        dve.wait_ge(s_z, b + 1)
        dve.tensor_tensor(z[b % 2][:], z[b % 2][:], gamma[:], ALU.mult).then_inc(s_g, 1)
        dve.wait_ge(s_g, b + 1)
        dve.tensor_tensor(env.y[:, b, :], z[b % 2][:], beta[:], ALU.add).then_inc(s_y, 1)


def phase_capacity_experts(nc, env, out, w_gate, w1, w2, b2, ln_g, ln_b, slots, slot_ids, iota8, before):
    ctx = ExitStack()
    with ctx:
        sb, sem = tools(nc, ctx, "moe")
        E, CAP, FF, WB = 8, B * T // 8, 1024, 4
        FC = FF // 128
        wg = sb("w_gate", [128, KC, E])
        w1_sb = [sb(f"w1_{i}", [128, KC, FF]) for i in range(WB)]
        w2_sb = [sb(f"w2_{i}", [128, FC, D]) for i in range(WB)]
        b2_sb = sb("b2", [CAP, E, D])
        g2 = sb("ln_gamma", [T, D])
        be2 = sb("ln_beta", [T, D])
        slot_row = sb("slot_row", [T, E * CAP])
        slot_id = sb("slot_id", [CAP, E])
        io = sb("iota8", [T, E])
        earlier = sb("earlier", [T, T])
        ones = sb("ones", [T, T])
        yT = sb("yT", [128, KC, B, T])
        logits = sb("logits", [T, B, E])
        mx = sb("max", [T, B])
        eq = sb("eq", [T, B, E])
        cand = sb("cand", [T, B, E])
        best = sb("best", [T, B])
        hot = sb("one_hot", [T, B, E])
        ex = sb("exp", [T, B, E])
        gate = sb("gate", [T, B, 2])
        loc = sb("loc", [T, B])
        lochot = sb("lochot", [T, B, E])
        over = sb("over", [T, B])
        slot = sb("slot", [T, B])
        Pm = sb("into_slots", [T, B, E * CAP])
        diag = [sb(f"diag{i}", [T, T]) for i in range(B)]
        srow = sb("slot_of_token", [CAP, B * T])
        R = sb("from_slots", [CAP, E, B * T])
        dT = sb("dispatched", [128, KC, E * CAP])
        hT = [sb(f"hT{i}", [128, FC, CAP]) for i in range(2)]
        ys = sb("expert_out", [CAP, E, D])
        stats = sb("stats", [T, B, 6])
        mv = sb("mean_var", [T, B, 4])
        z = [sb(f"z{i}", [T, D]) for i in range(2)]

        loaded, s_ones, stored, s_end = sem("loaded"), sem("ones"), sem("stored"), sem("end")
        w_in = [sem(f"w_in{i}") for i in range(WB)]
        chain = sem("routing_step")
        s_sub, s_exp, s_hot, s_slot, s_P, s_diag, s_R = (sem(n) for n in ("sub", "exp", "hot", "slot", "P", "diag", "R"))
        s_res, s_stats, s_var, s_rstd, s_z, s_g, s_y = (sem(n) for n in ("res", "stats", "var", "rstd", "z", "g", "y"))
        HALF = E * CAP // 2

        names = [("yT", b) for b in range(B)] + [("logits", 0), ("loc", 0), ("row", 0), ("row", 1)]
        names += [("d", n, k) for n in range(2) for k in range(KC)]
        ring = Ring(env, names)
        ring.close(1)
        TURNS = E // WB
        names = [("h", 0, 0), ("h", 0, 1)]
        for i in range(WB):
            names += [("h", i + 1, 0), ("h", i + 1, 1)] * (i + 1 < WB) + [("y", i)]
        work = Ring(env, names)
        work.close(TURNS)
        back = Ring(env, [("x", b) for b in range(B)])
        back.close(1)
        block = ctx.enter_context(nc.Block())

        @block.sync
        def _(sp):
            for dst, src in ((wg, w_gate.rearrange("(k p) n -> p k n", p=128)),
                             (b2_sb, b2.rearrange("(o e) d -> o e d", o=1).to_broadcast([CAP, E, D])),
                             (g2, ln_g.rearrange("(o d) -> o d", o=1).to_broadcast([T, D])),
                             (be2, ln_b.rearrange("(o d) -> o d", o=1).to_broadcast([T, D])),
                             (slot_row, slots.rearrange("(o d) -> o d", o=1).to_broadcast([T, E * CAP])),
                             (slot_id, slot_ids),
                             (io, iota8.rearrange("(o d) -> o d", o=1).to_broadcast([T, E])),
                             (earlier, before)):
                sp.dma_start(dst[:], src).then_inc(loaded, 16)
            for e in range(WB):
                sp.dma_start(w1_sb[e][:], w1[e].rearrange("(k p) n -> p k n", p=128)).then_inc(w_in[e], 16)
                sp.dma_start(w2_sb[e][:], w2[e].rearrange("(k p) n -> p k n", p=128)).then_inc(w_in[e], 16)
            for e in range(WB, E):
                work.wait_full(sp, ("y", e - WB), 0)
                sp.dma_start(w1_sb[e - WB][:], w1[e].rearrange("(k p) n -> p k n", p=128)).then_inc(w_in[e - WB], 16)
                sp.dma_start(w2_sb[e - WB][:], w2[e].rearrange("(k p) n -> p k n", p=128)).then_inc(w_in[e - WB], 16)
            for b in range(B):
                sp.wait_ge(s_end, b + 1)
                sp.dma_start(out[b], env.x[:, b, :]).then_inc(stored, 16)
            sp.wait_ge(stored, 16 * B)

        @block.gpsimd
        def _(pool):
            pool.memset(ones[:], 1.0).then_inc(s_ones, 1)
            pool.wait_ge(s_var, 1)
            pool.tensor_tensor(mv[:, :, 3], mv[:, :, 2], env.minus_half[0:T, 0:B], ALU.pow).then_inc(s_rstd, 1)

        @block.scalar
        def _(act):
            for b in range(B):
                src = ring.wait_full(act, ("yT", b), 0)
                act.copy(yT[:, :, b, :], src[:, 0:KC * T].rearrange("p (k n) -> p k n", k=KC))\
                    .then_inc(ring.free(("yT", b)), 1)
            act.wait_ge(s_sub, 1)
            act.activation(ex[:], ex[:], ACT.Exp).then_inc(s_exp, 1)
            for n in range(2):
                src = ring.wait_full(act, ("row", n), 0)
                act.copy(srow[:, n * HALF:(n + 1) * HALF], src[0:CAP, 0:HALF]).then_inc(ring.free(("row", n)), 1)
            for n in range(2):
                for k in range(KC):
                    src = ring.wait_full(act, ("d", n, k), 0)
                    act.copy(dT[:, k, n * HALF:(n + 1) * HALF], src[:, 0:HALF]).then_inc(ring.free(("d", n, k)), 1)

        @block.vector
        def _(dve):
            steps = [0]

            def step(op):
                steps[0] += 1
                op.then_inc(chain, 1)
                dve.wait_ge(chain, steps[0])

            dve.wait_ge(loaded, 128)
            per_expert = io[:].rearrange("p (b e) -> p b e", b=1).to_broadcast([T, B, E])
            src = ring.wait_full(dve, ("logits", 0), 0)
            dve.tensor_copy(logits[:], src[0:T, 0:B * E].rearrange("p (b e) -> p b e", b=B))\
                .then_inc(ring.free(("logits", 0)), 1)
            ring.wait_read(dve, ("logits", 0), 0)
            step(dve.tensor_reduce(mx[:], logits[:], AX.X, ALU.max))
            dve.tensor_tensor(ex[:], logits[:], spread(mx[:], E), ALU.subtract).then_inc(s_sub, 1)
            step(dve.tensor_tensor(eq[:], logits[:], spread(mx[:], E), ALU.is_equal))
            step(dve.scalar_tensor_tensor(cand[:], eq[:], -float(E), per_expert, ALU.mult, ALU.add))
            step(dve.tensor_reduce(best[:], cand[:], AX.X, ALU.min))
            step(dve.tensor_scalar(best[:], best[:], float(E), None, ALU.add))
            dve.tensor_tensor(hot[:], per_expert, spread(best[:], E), ALU.is_equal).then_inc(s_hot, 1)
            dve.wait_ge(s_hot, 1)
            dve.wait_ge(s_exp, 1)
            step(dve.tensor_reduce(gate[:, :, 0], ex[:], AX.X, ALU.add))
            step(dve.reciprocal(gate[:, :, 1], gate[:, :, 0]))
            src = ring.wait_full(dve, ("loc", 0), 0)
            dve.tensor_tensor(lochot[:], src[0:T, 0:B * E].rearrange("p (b e) -> p b e", b=B), hot[:], ALU.mult)\
                .then_inc(ring.free(("loc", 0)), 1)
            ring.wait_read(dve, ("loc", 0), 0)
            step(dve.tensor_reduce(loc[:], lochot[:], AX.X, ALU.add))
            step(dve.tensor_scalar(over[:], loc[:], float(CAP), float(4 * E * CAP), ALU.is_ge, ALU.mult))
            step(dve.scalar_tensor_tensor(slot[:], best[:], float(CAP), loc[:], ALU.mult, ALU.add))
            step(dve.tensor_tensor(slot[:], slot[:], over[:], ALU.add))
            for b in range(B):
                dve.tensor_scalar(diag[b][:], env.ident[0:T, 0:T], slot[:, b:b + 1], None, ALU.mult)\
                    .then_inc(s_diag, 1)
            for b in range(B):
                dve.tensor_scalar(Pm[:, b, :], slot_row[:], slot[:, b:b + 1], None, ALU.is_equal).then_inc(s_P, 1)
            ring.wait_read(dve, ("row", 0), 0)
            ring.wait_read(dve, ("row", 1), 0)
            for e in range(E):
                dve.tensor_scalar(R[:, e, :], srow[:], slot_id[:, e:e + 1], None, ALU.is_equal).then_inc(s_R, 1)

            b1_at = env.column_at("b1")
            with dve.Fori(0, TURNS) as t:
                for i in range(WB + 1):
                    if i < WB:
                        e = t * WB + i
                        for a in range(2):
                            src = work.wait_full(dve, ("h", i, a), t)
                            b1 = env.columns[:, bass.ds(e * FC + (b1_at + 4 * a), 4)]
                            dve.tensor_tensor(hT[i % 2][:, 4 * a:4 * a + 4, :], heads(src[:, 0:4 * CAP], 4, CAP),
                                              spread(b1, CAP), ALU.add).then_inc(work.free(("h", i, a)), 1)
                    if i >= 1:
                        e = t * WB + (i - 1)
                        src = work.wait_full(dve, ("y", i - 1), t)
                        dve.tensor_tensor(ys[:, bass.ds(e, 1), :].rearrange("p a d -> p (a d)"), src[0:CAP, 0:D],
                                          b2_sb[:, bass.ds(e, 1), :].rearrange("p a d -> p (a d)"), ALU.add)\
                            .then_inc(work.free(("y", i - 1)), 1)
            for b in range(B):
                src = back.wait_full(dve, ("x", b), 0)
                dve.scalar_tensor_tensor(env.y[:, b, :], src[0:T, 0:D], gate[:, b, 1:2], env.y[:, b, :],
                                         ALU.mult, ALU.add).then_inc(back.free(("x", b)), 1)
            back.wait_read(dve, ("x", B - 1), 0)
            norm_columns(dve, mv, stats, lambda k: env.y[:, k, :], B, T, s_stats, s_var, 1.0, EPS)
            dve.wait_ge(s_rstd, 1)
            normalise_rows(dve, env, mv, z, g2, be2, s_z, s_g, s_y)
            for b in range(B):
                dve.wait_ge(s_y, b + 1)
                dve.tensor_tensor(env.x[:, b, :], env.x[:, b, :], env.y[:, b, :], ALU.add).then_inc(s_end, 1)

        @block.tensor
        def _(pe):
            pe.wait_ge(loaded, 128)
            pe.wait_ge(s_ones, 1)
            for b in range(B):
                out_ = ring.wait_free(pe, ("yT", b), 0)
                transposes(pe, env, out_, env.y[:, b, :], T, 128, KC).then_inc(ring.full(("yT", b)), 1)
            acc = ring.wait_free(pe, ("logits", 0), 0)
            for b in range(B):
                ring.wait_read(pe, ("yT", b), 0)
                for k in range(KC):
                    last = pe.matmul(acc[0:T, b * E:(b + 1) * E], yT[:, k, b, :], wg[:, k, :],
                                     start=k == 0, stop=k == KC - 1)
            last.then_inc(ring.full(("logits", 0)), 1)
            acc = ring.wait_free(pe, ("loc", 0), 0)
            pe.wait_ge(s_hot, 1)
            pe.matmul(acc[0:T, 0:B * E], earlier[:], hot[:].rearrange("p b e -> p (b e)"), start=True, stop=False)
            for d in range(1, B):
                last = pe.matmul(acc[0:T, d * E:B * E], ones[:], hot[:, 0:B - d, :].rearrange("p b e -> p (b e)"),
                                 start=False, stop=d == B - 1)
            last.then_inc(ring.full(("loc", 0)), 1)
            for n in range(2):
                acc = ring.wait_free(pe, ("row", n), 0)
                for i in range(4):
                    b = 4 * n + i
                    pe.wait_ge(s_diag, b + 1)
                    last = pe.matmul(acc[0:CAP, i * T:(i + 1) * T], ones[:, 0:CAP], diag[b][:], start=True, stop=True)
                last.then_inc(ring.full(("row", n)), 1)
            for n in range(2):
                for k in range(KC):
                    acc = ring.wait_free(pe, ("d", n, k), 0)
                    for b in range(B):
                        if n + k == 0:
                            pe.wait_ge(s_P, b + 1)
                        last = pe.matmul(acc[:, 0:HALF], env.y[:, b, k * 128:(k + 1) * 128],
                                         Pm[:, b, n * HALF:(n + 1) * HALF], start=b == 0, stop=b == B - 1)
                    last.then_inc(ring.full(("d", n, k)), 1)
            for n in range(2):
                for k in range(KC):
                    ring.wait_read(pe, ("d", n, k), 0)

            def hidden(i, t):
                pe.wait_ge(w_in[i], t * 32 + 32)
                for a in range(2):
                    acc = work.wait_free(pe, ("h", i, a), t)
                    for f in range(4):
                        for k in range(KC):
                            last = pe.matmul(acc[:, f * CAP:(f + 1) * CAP],
                                             w1_sb[i][:, k, (4 * a + f) * 128:(4 * a + f + 1) * 128],
                                             dT[:, k, bass.ds((t * WB + i) * CAP, CAP)],
                                             start=k == 0, stop=k == KC - 1)
                    last.then_inc(work.full(("h", i, a)), 1)

            with pe.Fori(0, TURNS) as t:
                hidden(0, t)
                for i in range(WB):
                    if i + 1 < WB:
                        hidden(i + 1, t)
                    acc = work.wait_free(pe, ("y", i), t)
                    work.wait_read(pe, ("h", i, 0), t)
                    work.wait_read(pe, ("h", i, 1), t)
                    for f in range(FC):
                        last = pe.matmul(acc[0:CAP, 0:D], hT[i % 2][:, f, :], w2_sb[i][:, f, :],
                                         start=f == 0, stop=f == FC - 1)
                    last.then_inc(work.full(("y", i)), 1)
            work.wait_read(pe, ("y", WB - 1), TURNS - 1)
            pe.wait_ge(s_R, E)
            for b in range(B):
                acc = back.wait_free(pe, ("x", b), 0)
                for e in range(E):
                    last = pe.matmul(acc[0:T, 0:D], R[:, e, b * T:(b + 1) * T], ys[:, e, :],
                                     start=e == 0, stop=e == E - 1)
                last.then_inc(back.full(("x", b)), 1)


def program(nc, a, out):
    ctx = ExitStack()
    with ctx:
        env = Env(nc, ctx)
        phase_load(nc, env, a["x"], a["columns"])
        phase_self_attention_rope(nc, env, a["L0_attn_w_qkv"], a["L0_attn_w_out"],
                                  a["rope_cos"], a["rope_sin"])
        phase_cross_attention_normed(nc, env, a["ctx"], a["mask"], a["L0_xattn_Wq"], a["L0_xattn_Wkv"],
                                     a["L0_xattn_Wout"], a["L0_xattn_bout"])
        phase_kronecker_experts(nc, env, a["router_up"], a["A_up"], a["B_up"], a["router_down"], a["A_down"],
                                a["B_down"], a["bias_up"], a["bias_down"], a["kron_scales"])
        phase_self_attention_scaled(nc, env, a["head_mask_scaled"])
        phase_cross_attention_queries(nc, env, a["ctx"], a["head_mask"], a["L1_xattn_Wq"], a["L1_xattn_Wk"],
                                      a["L1_xattn_Wv"], a["L1_xattn_Wo"], a["L1_xattn_bv"], a["L1_xattn_bo"])
        phase_attention_over_sequences(nc, env, a["in_proj_w"], a["out_proj_w"], a["in_proj_b_v"],
                                       a["out_proj_b"], a["ln1_g"], a["ln1_b"], a["block_bias"])
        phase_capacity_experts(nc, env, out, a["wg"], a["w1"], a["w2"], a["b2"], a["ln2_g"], a["ln2_b"],
                               a["slots"], a["slot_ids"], a["iota8"], a["earlier"])


def rotary_tables():
    dim = 64
    inv = (1.0 / np.float32(10000.0) ** (np.arange(0, dim, 2, dtype=np.float32) / np.float32(dim))).astype(np.float32)
    f = np.arange(T - 1, dtype=np.float32)[:, None] * inv[None, :]
    cos = np.concatenate([np.ones((1, dim // 2), np.float32), np.cos(f)])
    sin = np.concatenate([np.zeros((1, dim // 2), np.float32), np.sin(f)])
    return np.concatenate([cos, cos], 1), np.concatenate([-sin, sin], 1)


def columns(inputs):
    def by_feature(name):
        return inputs[name].reshape(-1, 128).T

    def twice(name):
        return np.concatenate([inputs[name], inputs[name]]).reshape(128, 1)
    got = {"attn_gamma": by_feature("L0_attn_ln_gamma"), "attn_beta": by_feature("L0_attn_ln_beta"),
           "xattn_x_gamma": by_feature("L0_xattn_ln_x_g"), "xattn_x_beta": by_feature("L0_xattn_ln_x_b"),
           "xattn_l_gamma": by_feature("L0_xattn_ln_l_g"), "xattn_l_beta": by_feature("L0_xattn_ln_l_b"),
           "q_gamma": twice("L0_xattn_qn_g"), "k_gamma": twice("L0_xattn_kn_g"),
           "rotation": by_feature("L1_attn_rotation_params"), "entangle": by_feature("L1_attn_entangle_params"),
           "bq": by_feature("L1_xattn_bq"), "bk": by_feature("L1_xattn_bk"),
           "in_proj_b": by_feature("L1_ffn_in_proj_b"), "b1": by_feature("L1_ffn_b1")}
    return np.ascontiguousarray(np.concatenate([got[name] for name, _ in COLUMNS], axis=1))


def layout(inputs):
    a = {}
    c = np.ascontiguousarray
    a["x"] = c(inputs["x"])
    a["L0_attn_w_qkv"] = c(inputs["L0_attn_w_qkv"])
    a["L0_attn_w_out"] = c(inputs["L0_attn_w_out"])
    a["ctx"] = c(inputs["ctx_1024"])
    a["mask"] = c(inputs["mask_BxS2_bf1"]).view(np.uint8)
    for name in ("L0_xattn_Wq", "L0_xattn_Wkv", "L0_xattn_Wout", "L0_xattn_bout"):
        a[name] = c(inputs[name])
    E = 64
    a["router_up"] = c(inputs["L0_ffn_W_up"].T.reshape(8, 128, E).transpose(1, 0, 2))
    a["router_down"] = c(inputs["L0_ffn_W_down"].reshape(E, 64, 64).transpose(2, 1, 0))
    for name in ("A_up", "B_up", "A_down", "B_down"):
        a[name] = c(inputs[f"L0_ffn_{name}"].transpose(2, 0, 1))
    a["bias_up"] = c(inputs["L0_ffn_bias_up"].reshape(64, 64).T)
    a["bias_down"] = c(inputs["L0_ffn_bias_down"].reshape(32, 32).T)
    a["kron_scales"] = np.concatenate([inputs["L0_ffn_scale_up"], inputs["L0_ffn_scale_down"]])
    a["head_mask"] = (np.arange(128)[:, None] // 16 == np.arange(8)[None, :]).astype(np.float32)
    a["head_mask_scaled"] = np.where(np.arange(128)[:, None] // 16 == np.arange(8)[None, :], 0.25, 0.0)\
        .astype(np.float32)
    for name in ("Wq", "Wk", "Wv"):
        a[f"L1_xattn_{name}"] = c(inputs[f"L1_xattn_{name}"].reshape(D, D).T)
    a["L1_xattn_Wo"] = c(inputs["L1_xattn_Wo"].T)
    a["L1_xattn_bv"] = c(inputs["L1_xattn_bv"].reshape(D))
    a["L1_xattn_bo"] = c(inputs["L1_xattn_bo"])
    a["in_proj_w"] = c(inputs["L1_ffn_in_proj_w"].T)
    a["out_proj_w"] = c(inputs["L1_ffn_out_proj_w"].T)
    a["in_proj_b_v"] = c(inputs["L1_ffn_in_proj_b"][2 * D:])
    for name in ("out_proj_b", "ln1_g", "ln1_b", "ln2_g", "ln2_b", "wg", "w1", "w2", "b2"):
        a[name] = c(inputs[f"L1_ffn_{name}"])
    position = np.arange(128) // B
    a["block_bias"] = np.where(position[:, None] == position[None, :], 0.0, -1e30).astype(np.float32)
    a["slots"] = np.arange(B * T, dtype=np.float32)
    a["slot_ids"] = c(a["slots"].reshape(8, T).T)
    a["iota8"] = np.arange(8, dtype=np.float32)
    a["earlier"] = (np.arange(T)[:, None] < np.arange(T)[None, :]).astype(np.float32)
    a["columns"] = columns(inputs)
    a["rope_cos"], a["rope_sin"] = rotary_tables()
    return a


def kernel(**inputs):
    import concourse.bacc as bacc
    from concourse.bass_utils import run_bass_kernel_spmd

    nc = bacc.Bacc("TRN2", target_bir_lowering=False, num_devices=1)
    arrays = {f"in_{name}": array for name, array in layout(inputs).items()}
    aps = {name[3:]: nc.dram_tensor(name, array.shape, mybir.dt.from_np(array.dtype), kind="ExternalInput").ap()
           for name, array in arrays.items()}
    out = nc.dram_tensor("out_x", (B, T, D), F32, kind="ExternalOutput").ap()
    program(nc, aps, out)
    return run_bass_kernel_spmd(nc, [arrays], core_ids=[0]).results[0]["out_x"]
```

```python
import numpy as np
import concourse.bass as bass
from concourse import mybir
from contextlib import ExitStack

F32 = mybir.dt.float32
U32 = mybir.dt.uint32
U8 = mybir.dt.uint8
ALU = mybir.AluOpType
ACT = mybir.ActivationFunctionType
AX = mybir.AxisListType

B, T, D = 8, 112, 256
C = 375
CT = 125
H = 16
KC = D // 128
PAIRS = B // 2
EPS = 1e-5
BANKS = 8


class Ring:

    def __init__(self, env, names):
        self.env = env
        self.names = names
        self.at = {name: i for i, name in enumerate(names)}
        assert len(self.at) == len(names)
        self.uses = [len(range(k, len(names), BANKS)) for k in range(BANKS)]
        self.base = list(env.bank_uses)

    def close(self, turns):
        for k in range(BANKS):
            self.env.bank_uses[k] += turns * self.uses[k]

    def bank(self, name):
        return self.env.psum[:, self.at[name] % BANKS, :]

    def _count(self, name, turn):
        i = self.at[name]
        return i % BANKS, turn * self.uses[i % BANKS] + (self.base[i % BANKS] + i // BANKS + 1)

    def wait_free(self, pe, name, turn):
        k, n = self._count(name, turn)
        pe.wait_ge(self.env.bank_free[k], n)
        return self.bank(name)

    def wait_full(self, eng, name, turn):
        k, n = self._count(name, turn)
        eng.wait_ge(self.env.bank_full[k], n)
        return self.bank(name)

    def wait_read(self, eng, name, turn):
        k, n = self._count(name, turn)
        eng.wait_ge(self.env.bank_free[k], n + 1)

    def full(self, name):
        return self.env.bank_full[self.at[name] % BANKS]

    def free(self, name):
        return self.env.bank_free[self.at[name] % BANKS]


COLUMNS = [("attn_gamma", KC), ("attn_beta", KC), ("xattn_x_gamma", KC), ("xattn_x_beta", KC),
           ("xattn_l_gamma", KC), ("xattn_l_beta", KC), ("q_gamma", 1), ("k_gamma", 1),
           ("rotation", KC), ("entangle", KC), ("bq", KC), ("bk", KC), ("in_proj_b", 6), ("b1", 64)]


class Env:

    def __init__(self, nc, ctx):
        self.nc = nc
        self.psum = ctx.enter_context(nc.psum_tensor("psum", [128, BANKS, 512], F32))
        self.bank_full = [ctx.enter_context(nc.semaphore(f"bank_full{k}")) for k in range(BANKS)]
        self.bank_free = [ctx.enter_context(nc.semaphore(f"bank_free{k}")) for k in range(BANKS)]
        self.bank_uses = [0] * BANKS
        self.x = ctx.enter_context(nc.sbuf_tensor("x_stream", [T, B, D], F32))
        self.y = ctx.enter_context(nc.sbuf_tensor("last_block_stream", [T, B, D], F32))
        self.ident = ctx.enter_context(nc.sbuf_tensor("ident", [128, 128], F32))
        self.columns = ctx.enter_context(nc.sbuf_tensor("columns", [128, sum(n for _, n in COLUMNS)], F32))
        self.minus_half = ctx.enter_context(nc.sbuf_tensor("minus_half", [128, 32], F32))


    def column_at(self, name):
        names = [other for other, _ in COLUMNS]
        return sum(n for _, n in COLUMNS[:names.index(name)])

    def col(self, name, k=0):
        at = self.column_at(name) + k
        return self.columns[:, at:at + 1]


def tools(nc, ctx, phase):
    def sb(name, shape, dtype=F32):
        return ctx.enter_context(nc.sbuf_tensor(f"{phase}_{name}", shape, dtype))

    def sem(name):
        return ctx.enter_context(nc.semaphore(f"{phase}_{name}"))
    return sb, sem


class Ahead:

    def __init__(self, nc, ctx, phase, items):
        sb, sem = tools(nc, ctx, phase)
        self.items = items
        self.tiles = {name: sb(name, shape, dtype) for name, (shape, _, dtype) in items.items()}
        self.loaded = sem("ahead_loaded")
        self.all = 16 * len(items)

    def issue(self, sp):
        for name, (_, source, _) in self.items.items():
            sp.dma_start(self.tiles[name][:], source).then_inc(self.loaded, 16)

    def __getitem__(self, name):
        return self.tiles[name]


def all_rows(vector, n):
    return vector.rearrange("(o d) -> o d", o=1).to_broadcast([n, vector.shape[0]])


def heads(ap, h, d):
    return ap.rearrange("p (h d) -> p h d", h=h)


def spread(ap, n):
    p, h = ap.shape
    return ap.rearrange("p (h o) -> p h o", o=1).to_broadcast([p, h, n])


def transposes(pe, env, out, src, rows, cols, each=1):
    for k in range(each):
        last = pe.transpose(out[0:cols, k * rows:(k + 1) * rows], src[0:rows, k * cols:(k + 1) * cols],
                            env.ident[0:rows, 0:rows])
    return last


def phase_load(nc, env, x, columns):
    ctx = ExitStack()
    with ctx:
        sb, sem = tools(nc, ctx, "load")
        x_in, zeroed, ready = sem("x_in"), sem("zeroed"), sem("ready")
        block = ctx.enter_context(nc.Block())

        @block.sync
        def _(sp):
            sp.dma_start(env.x[:], x.rearrange("b s d -> s b d")).then_inc(x_in, 16)
            sp.dma_start(env.columns[:], columns).then_inc(x_in, 16)
            sp.wait_ge(x_in, 32)

        @block.tensor
        def _(pe):
            for k in range(BANKS):
                pe.sem_inc(env.bank_free[k], 1)

        @block.gpsimd
        def _(pool):
            pool.memset(env.minus_half[:], -0.5).then_inc(ready, 1)
            pool.memset(env.ident[:], 0.0).then_inc(zeroed, 1)
            pool.wait_ge(zeroed, 1)
            pool.affine_select(out=env.ident[:], in_=env.ident[:], compare_op=ALU.not_equal, fill=1.0,
                               base=0, pattern=[[-1, 128]], channel_multiplier=1).then_inc(ready, 1)
            pool.wait_ge(ready, 2)


def norm_columns(dve, mv, stats, src, n, rows, s_stats, s_var, scale, add):
    for k in range(n):
        dve.bn_stats(stats[0:rows, k, :], src(k)).then_inc(s_stats, 1)
    for k in range(n):
        dve.wait_ge(s_stats, k + 1)
        last = dve.bn_aggr(mv[0:rows, k, 0:2], stats[0:rows, k, :])
    last.then_inc(s_stats, 1)
    dve.wait_ge(s_stats, n + 1)
    dve.tensor_scalar(mv[0:rows, 0:n, 2], mv[0:rows, 0:n, 1], scale, add, ALU.mult, ALU.add).then_inc(s_var, 1)


def phase_self_attention_rope(nc, env, w_qkv, w_out, cos, sin, ahead):
    ctx = ExitStack()
    with ctx:
        sb, sem = tools(nc, ctx, "rope")
        DH, UNITS = 64, 8
        wq = sb("w_qkv", [128, KC, 3 * H * DH])
        wo = sb("w_out", [128, 8, D])
        cs = sb("cos", [T, DH])
        sn = sb("sin", [T, DH])
        stats = sb("stats", [T, B, 6])
        mv = sb("mean_var", [T, B, 4])
        xn = [sb(f"xn{i}", [T, D]) for i in range(2)]
        xT = [sb(f"xT{i}", [128, KC, T]) for i in range(2)]
        qk = [sb(f"qk{i}", [T, 2 * H * DH]) for i in range(2)]
        rot = [sb(f"rot{i}", [T, 512]) for i in range(2)]
        v = [sb(f"v{i}", [T, H, DH + 1]) for i in range(2)]
        qT = [sb(f"qT{i}", [128, 8, 2, T]) for i in range(2)]
        kT = [sb(f"kT{i}", [128, 8, T]) for i in range(2)]
        P = [sb(f"P{i}", [T, 4 * T]) for i in range(4)]
        PT = [sb(f"PT{i}", [T, 4 * T]) for i in range(2)]
        mx = sb("max", [T, UNITS, 4])
        rs = sb("recip", [T, UNITS, 4])
        o = [sb(f"o{i}", [T, H * DH]) for i in range(2)]
        oT = [sb(f"oT{i}", [128, 8, T]) for i in range(2)]

        loaded, wo_loaded, ones = sem("loaded"), sem("wo_loaded"), sem("ones")
        w_loaded = [sem(f"w_{part}_loaded") for part in "qkv"]
        s_stats, s_var, s_rstd, s_xn = sem("stats"), sem("var"), sem("rstd"), sem("xn")
        s_rot, s_max, s_exp, s_sum = sem("rotated"), sem("max"), sem("exp"), sem("sum")

        def head(g, i):
            return 8 * (g // 2) + g % 2 + 2 * i

        units = [(g, par) for g in range(4) for par in range(2)]
        names = [("xT", par) for par in range(2)]
        names += [("qkv", par, j) for par in range(2) for j in range(6)]
        names += [("qkT", par, j) for par in range(2) for j in range(4)]
        for u in range(UNITS + 3):
            names += [("S", u)] * (u < UNITS) + [("PT", u - 2)] * (0 <= u - 2 < UNITS) + [("O", u - 3)] * (u >= 3)
        names += [("oT", par, j) for par in range(2) for j in range(2)]
        names += [("out", par) for par in range(2)]
        ring = Ring(env, names)
        block = ctx.enter_context(nc.Block())

        @block.sync
        def _(sp):
            sp.dma_start(cs[:], cos).then_inc(loaded, 16)
            sp.dma_start(sn[:], sin).then_inc(loaded, 16)
            for i in range(3):
                columns = slice(i * H * DH, (i + 1) * H * DH)
                sp.dma_start(wq[:, :, columns], w_qkv.rearrange("(k p) n -> p k n", p=128)[:, :, columns])\
                    .then_inc(w_loaded[i], 16)
            sp.dma_start(wo[:], w_out.rearrange("(k p) n -> p k n", p=128)).then_inc(wo_loaded, 16)
            ahead.issue(sp)
            sp.wait_ge(wo_loaded, 16)

        @block.gpsimd
        def _(pool):
            for i in range(2):
                pool.memset(v[i][:], 1.0).then_inc(ones, 1)
                pool.memset(qT[i][:], 0.0).then_inc(ones, 1)
            pool.wait_ge(s_var, 1)
            pool.tensor_tensor(mv[:, :, 3], mv[:, :, 2], env.minus_half[0:T, 0:B], ALU.pow).then_inc(s_rstd, 1)
            with pool.Fori(0, PAIRS) as t:
                for par in range(2):
                    for j in range(4):
                        ring.wait_read(pool, ("qkv", par, j), t)
                        part = qk[par][:, j * 512:(j + 1) * 512]
                        pool.tensor_tensor(part, part, rot[j % 2][:], ALU.add).then_inc(s_rot, 1)

        @block.scalar
        def _(act):
            act.wait_ge(ones, 4)
            with act.Fori(0, PAIRS) as t:
                for par in range(2):
                    src = ring.wait_full(act, ("xT", par), t)
                    for k in range(KC):
                        last = act.activation(xT[par][:, k, :], src[:, k * T:(k + 1) * T], ACT.Identity,
                                              bias=env.col("attn_beta", k), scale=env.col("attn_gamma", k))
                    last.then_inc(ring.free(("xT", par)), 1)
                for par in range(2):
                    for j in range(4, 6):
                        src = ring.wait_full(act, ("qkv", par, j), t)
                        act.copy(v[par][:, (j - 4) * 8:(j - 3) * 8, 0:DH],
                                 heads(src[0:T, :], 8, DH)).then_inc(ring.free(("qkv", par, j)), 1)
                for par in range(2):
                    for j in range(2):
                        src = ring.wait_full(act, ("qkT", par, j), t)
                        for half in range(2):
                            rows = slice(64 * half, 64 * half + 64)
                            last = act.copy(qT[par][rows, 4 * j:4 * j + 4, half, :], heads(src[rows, 0:4 * T], 4, T))
                        last.then_inc(ring.free(("qkT", par, j)), 1)
                    for j in range(2):
                        src = ring.wait_full(act, ("qkT", par, 2 + j), t)
                        act.copy(kT[par][:, 4 * j:4 * j + 4, :].rearrange("p a b -> p (a b)"),
                                 src[:, 0:4 * T]).then_inc(ring.free(("qkT", par, 2 + j)), 1)
                for u in range(UNITS + 2):
                    if u < UNITS:
                        ring.wait_read(act, ("S", u), t)
                        act.activation(P[u % 4][:], P[u % 4][:], ACT.Exp, scale=DH ** -0.5).then_inc(s_exp, 1)
                    if u >= 2:
                        src = ring.wait_full(act, ("PT", u - 2), t)
                        act.copy(PT[u % 2][:], src[0:T, 0:4 * T]).then_inc(ring.free(("PT", u - 2)), 1)
                for par in range(2):
                    for j in range(2):
                        src = ring.wait_full(act, ("oT", par, j), t)
                        act.copy(oT[par][:, 4 * j:4 * j + 4, :].rearrange("p a b -> p (a b)"),
                                 src[:, 0:4 * T]).then_inc(ring.free(("oT", par, j)), 1)

        @block.vector
        def _(dve):
            dve.wait_ge(loaded, 32)
            norm_columns(dve, mv, stats, lambda k: env.x[:, k, :], B, T, s_stats, s_var, 1.0 + EPS, EPS * EPS)
            dve.wait_ge(s_rstd, 1)
            with dve.Fori(0, PAIRS) as t:
                for par in range(2):
                    b = t * 2 + par
                    xb = env.x[:, bass.ds(b, 1), :].rearrange("p a d -> p (a d)")
                    dve.tensor_scalar(xn[par][:], xb, mv[:, bass.ds(b, 1), 0:1].rearrange("p a o -> p (a o)"),
                                      mv[:, bass.ds(b, 1), 3:4].rearrange("p a o -> p (a o)"),
                                      ALU.subtract, ALU.mult).then_inc(s_xn, 1)
                for par in range(2):
                    for j in range(4):
                        src = ring.wait_full(dve, ("qkv", par, j), t)
                        if par * 4 + j >= 2:
                            dve.wait_ge(s_rot, t * 8 + (par * 4 + j - 1))
                        th = heads(src[0:T, :], 8, DH)
                        ch = cs[:, :].rearrange("p (o d) -> p o d", o=1).to_broadcast([T, 8, DH])
                        rh = heads(rot[j % 2][:], 8, DH)
                        HD = DH // 2
                        dve.tensor_tensor(heads(qk[par][:, j * 512:(j + 1) * 512], 8, DH), th, ch, ALU.mult)
                        for a in range(2):
                            sh = sn[:, a * HD:(a + 1) * HD].rearrange("p (o d) -> p o d", o=1)\
                                .to_broadcast([T, 8, HD])
                            last = dve.tensor_tensor(rh[:, :, a * HD:(a + 1) * HD],
                                                     th[:, :, (1 - a) * HD:(2 - a) * HD], sh, ALU.mult)
                        last.then_inc(ring.free(("qkv", par, j)), 1)
                for u in range(UNITS + 3):
                    if u < UNITS:
                        src = ring.wait_full(dve, ("S", u), t)
                        s4 = heads(src[0:T, 0:4 * T], 4, T)
                        dve.tensor_reduce(mx[:, u, :], s4, AX.X, ALU.max).then_inc(s_max, 1)
                        dve.wait_ge(s_max, t * UNITS + (u + 1))
                        dve.tensor_tensor(heads(P[u % 4][:], 4, T), s4, spread(mx[:, u, :], T),
                                          ALU.subtract).then_inc(ring.free(("S", u)), 1)
                    if u >= 3:
                        w = u - 3
                        g, par = units[w]
                        src = ring.wait_full(dve, ("O", w), t)
                        o4 = heads(src[0:T, 0:4 * (DH + 1)], 4, DH + 1)
                        dve.reciprocal(rs[:, w, :], o4[:, :, DH]).then_inc(s_sum, 1)
                        dve.wait_ge(s_sum, t * UNITS + (w + 1))
                        dve.tensor_tensor(heads(o[par][:], H, DH)[:, head(g, 0):head(g, 3) + 1:2, :], o4[:, :, 0:DH],
                                          spread(rs[:, w, :], DH), ALU.mult).then_inc(ring.free(("O", w)), 1)
                for par in range(2):
                    b = t * 2 + par
                    xb = env.x[:, bass.ds(b, 1), :].rearrange("p a d -> p (a d)")
                    src = ring.wait_full(dve, ("out", par), t)
                    dve.tensor_tensor(xb, xb, src[0:T, 0:D], ALU.add).then_inc(ring.free(("out", par)), 1)

        @block.tensor
        def _(pe):
            with pe.Fori(0, PAIRS) as t:
                for par in range(2):
                    out = ring.wait_free(pe, ("xT", par), t)
                    pe.wait_ge(s_xn, t * 2 + (par + 1))
                    transposes(pe, env, out, xn[par], T, 128, KC).then_inc(ring.full(("xT", par)), 1)
                for par in range(2):
                    ring.wait_read(pe, ("xT", par), t)
                    for j in range(6):
                        pe.wait_ge(w_loaded[j // 2], 16)
                        out = ring.wait_free(pe, ("qkv", par, j), t)
                        for k in range(KC):
                            last = pe.matmul(out[0:T, :], xT[par][:, k, :], wq[:, k, j * 512:(j + 1) * 512],
                                             start=k == 0, stop=k == KC - 1)
                        last.then_inc(ring.full(("qkv", par, j)), 1)
                for par in range(2):
                    for j in range(4):
                        pe.wait_ge(s_rot, t * 8 + (par * 4 + j + 1))
                        out = ring.wait_free(pe, ("qkT", par, j), t)
                        transposes(pe, env, out, qk[par][:, j * 512:(j + 1) * 512], T, 128, 4)\
                            .then_inc(ring.full(("qkT", par, j)), 1)
                for u in range(UNITS + 3):
                    if u < UNITS:
                        g, par = units[u]
                        out = ring.wait_free(pe, ("S", u), t)
                        ring.wait_read(pe, ("qkT", par, 2 + g // 2), t)
                        for i in range(4):
                            h = head(g, i)
                            last = pe.matmul(out[0:T, i * T:(i + 1) * T], qT[par][:, h // 2, h % 2, :],
                                             kT[par][:, h // 2, :], start=True, stop=True)
                        last.then_inc(ring.full(("S", u)), 1)
                    if 0 <= u - 2 < UNITS:
                        w = u - 2
                        out = ring.wait_free(pe, ("PT", w), t)
                        pe.wait_ge(s_exp, t * UNITS + (w + 1))
                        transposes(pe, env, out, P[w % 4], T, T, 4).then_inc(ring.full(("PT", w)), 1)
                    if u >= 3:
                        w = u - 3
                        g, par = units[w]
                        out = ring.wait_free(pe, ("O", w), t)
                        ring.wait_read(pe, ("PT", w), t)
                        ring.wait_read(pe, ("qkv", par, 4 + g // 2), t)
                        for i in range(4):
                            last = pe.matmul(out[0:T, i * (DH + 1):(i + 1) * (DH + 1)],
                                             PT[w % 2][:, i * T:(i + 1) * T], v[par][:, head(g, i), :],
                                             start=True, stop=True)
                        last.then_inc(ring.full(("O", w)), 1)
                for par in range(2):
                    ring.wait_read(pe, ("O", UNITS - 2 + par), t)
                    for j in range(2):
                        out = ring.wait_free(pe, ("oT", par, j), t)
                        transposes(pe, env, out, o[par][:, j * 512:(j + 1) * 512], T, 128, 4)\
                            .then_inc(ring.full(("oT", par, j)), 1)
                pe.wait_ge(wo_loaded, 16)
                for par in range(2):
                    out = ring.wait_free(pe, ("out", par), t)
                    ring.wait_read(pe, ("oT", par, 1), t)
                    for k in range(8):
                        last = pe.matmul(out[0:T, 0:D], oT[par][:, k, :], wo[:, k, :], start=k == 0, stop=k == 7)
                    last.then_inc(ring.full(("out", par)), 1)
        ring.close(PAIRS)


def cross_attention_normed_ahead(nc, ctx, ctx_rows, mask, w_q, w_kv, w_out, b_out):
    return Ahead(nc, ctx, "cross", {
        "ctx": ([CT, B * C // CT, D], ctx_rows.rearrange("b (c p) d -> p (b c) d", p=CT), F32),
        "w_kv": ([128, KC, 2 * H * 64], w_kv.rearrange("(k p) n -> p k n", p=128), F32),
        "w_q": ([128, KC, H * 64], w_q.rearrange("(k p) n -> p k n", p=128), F32),
        "mask": ([T, B, C], mask.rearrange("(o b) c -> o b c", o=1).to_broadcast([T, B, C]), U8),
        "w_out": ([128, 8, D], w_out.rearrange("(k p) n -> p k n", p=128), F32),
        "b_out": ([T, D], all_rows(b_out, T), F32)})


def phase_cross_attention_normed(nc, env, ahead):
    ctx = ExitStack()
    with ctx:
        sb, sem = tools(nc, ctx, "cross")
        DH, NT = 64, C // CT
        KEYS = C + T
        STEPS = H // 2
        BIG = float(np.finfo(np.float32).max)
        wq, wkv, wo, bo, rows_in, mask_in = (ahead[n] for n in ("w_q", "w_kv", "w_out", "b_out", "ctx", "mask"))
        qk_gamma = sb("qk_gamma", [128, 1])
        stats = sb("stats", [128, B * NT + B, 6])
        mv = sb("mean_var", [128, B * NT + B, 4])
        bias = [sb(f"mask_bias{i}", [T, KEYS]) for i in range(2)]
        xn = [sb(f"xn{i}", [CT, D]) for i in range(2)]
        xT = [sb(f"xT{i}", [128, KC, CT]) for i in range(2)]
        lT = [sb(f"lT{i}", [128, KC, T]) for i in range(2)]
        sq = [sb(f"squares{i}", [CT, H * DH]) for i in range(2)]
        ssq = sb("rms", [CT, 5, 2, H])
        kn = [sb(f"kn{i}", [CT, H * DH]) for i in range(2)]
        kT = [sb(f"kT{i}", [128, 8, KEYS]) for i in range(2)]
        qT = [sb(f"qT{i}", [128, 8, 2, T]) for i in range(2)]
        v = [sb(f"v{i}", [CT, NT + 1, H, DH + 1]) for i in range(2)]
        P = [sb(f"P{i}", [T, KEYS]) for i in range(4)]
        low = sb("row_min", [T, H])
        PT = [sb(f"PT{i}", [CT, 4 * T]) for i in range(4)]
        rs = sb("recip", [T, H // 4, 4])
        o = sb("o", [T, H * DH])
        oT = sb("oT", [128, 8, T])
        waited, whole = sb("waited", [1, STEPS]), sb("whole", [1, 1])
        res = sb("res", [T, D])

        set_up = sem("set_up")
        s_stats, s_var, s_lstats, s_lvar, s_rstd = sem("stats"), sem("var"), sem("lstats"), sem("lvar"), sem("rstd")
        s_xn, s_sq, s_ssum, s_mean, s_rms, s_kn = sem("xn"), sem("sq"), sem("ssum"), sem("mean"), sem("rms"), sem("kn")
        s_bias, s_exp, s_sum, s_res, s_gamma = sem("bias"), sem("exp"), sem("sum"), sem("res"), sem("gamma")
        s_divided, s_more = sem("divided"), sem("more_stats")
        MORE = (B - 1) * NT

        TILES = 5
        height = [T, T, CT, CT, CT]
        chunk = [NT, None, 0, 1, 2]
        TURNED = [0, 2, 3, 4]
        TURN = {0: [0], 2: [2], 3: [3], 6: [4]}
        BACK = {3: 0, 5: 1, 6: 2, 8: 3, 9: 4}
        KEY = {0: 0, 2: 1, 3: 2, 5: 3, 7: 4}
        VALUE = {1: 0, 4: 2, 6: 3, 8: 4}
        ALL = STEPS + 2

        def step_tiles(i, s, heads_too, build, tail):
            names = []
            if heads_too:
                names += [("S", i, 2 * s), ("S", i, 2 * s + 1)] * (s < STEPS)
            if build:
                names += [("xT", i, c) for c in TURN.get(s, [])]
            if tail:
                names += [("oT", i, 0), ("oT", i, 1)] * (s == 0) + [("out", i)] * (s == 1)
            back = [("kT", i, BACK[s], j) for j in range(2) if build and s in BACK]
            names += back * (s < ALL - 1)
            if heads_too:
                names += [("O", i, (s - 3) // 2)] * (s >= 3 and s % 2 == 1)
            names += back * (s == ALL - 1)
            if heads_too:
                names += [("PT", i, 2 * s - 2), ("PT", i, 2 * s - 1)] * (1 <= s <= STEPS)
            if build:
                names += [("mm", i, KEY[s], j) for j in range(2) if s in KEY]
                names += [("mm", i, VALUE[s], j) for j in range(2, 4) if s in VALUE]
            return names

        def ring_of(sections, turns):
            ring = Ring(env, [name for i, what in enumerate(sections) for s in range(ALL)
                              for name in step_tiles(i, s, *what)])
            ring.close(turns)
            return ring

        FIRST, SECTION_0, MIDDLE, SECTION_7 = (False, True, False), (True, True, False), (True, True, True), \
            (True, False, True)
        rings = [ring_of([FIRST], 1), ring_of([SECTION_0], 1), ring_of([MIDDLE, MIDDLE], PAIRS - 1),
                 ring_of([SECTION_7], 1), ring_of([(False, False, True)], 1)]

        def count(seq, each, k):
            t, offset = seq
            return t * (2 * each) + (offset * each + k + 1)

        def after(seq, k):
            return seq[0], seq[1] + k

        def program_of(eng, section):
            section(rings[0], 0, 0, (0, -1), *FIRST)
            section(rings[1], 0, 0, (0, 0), *SECTION_0)
            with eng.Fori(0, PAIRS - 1) as t:
                section(rings[2], t, 0, (t, 1), *MIDDLE)
                section(rings[2], t, 1, (t, 2), *MIDDLE)
            section(rings[3], 0, 0, (PAIRS - 1, 1), *SECTION_7)
            section(rings[4], 0, 0, (PAIRS, 0), False, False, True)

        block = ctx.enter_context(nc.Block())

        @block.gpsimd
        def _(pool):
            pool.wait_ge(s_lvar, 1)
            pool.tensor_tensor(mv[0:T, B * NT:, 3], mv[0:T, B * NT:, 2], env.minus_half[0:T, 0:B], ALU.pow)\
                .then_inc(s_rstd, 1)
            pool.wait_ge(s_var, 1)
            pool.tensor_tensor(mv[0:CT, 0:NT, 3], mv[0:CT, 0:NT, 2], env.minus_half[0:CT, 0:NT],
                               ALU.pow).then_inc(s_rstd, 1)
            pool.wait_ge(s_rstd, 2)
            for i in range(2):
                pool.memset(v[i][:], 1.0).then_inc(set_up, 1)
                pool.memset(bias[i][:, C:KEYS], 0.0).then_inc(set_up, 1)
                pool.memset(qT[i][:], 0.0).then_inc(set_up, 1)

            def section(ring, turn, i, seq, heads_too, build, tail):
                for m in range(TILES * build):
                    n = height[m]
                    pool.wait_ge(s_mean, count(after(seq, 1), TILES, m))
                    pool.tensor_tensor(ssq[0:n, m, 1, :], ssq[0:n, m, 0, :], env.minus_half[0:n, 0:H],
                                       ALU.pow).then_inc(s_rms, 1)
                if build and not heads_too:
                    pool.wait_ge(s_var, 2)
                    pool.tensor_tensor(mv[0:CT, NT:B * NT, 3], mv[0:CT, NT:B * NT, 2],
                                       env.minus_half[0:CT, 0:(B - 1) * NT], ALU.pow).then_inc(s_rstd, 1)

            program_of(pool, section)

        def turned(m, seq):
            return lT[seq[1] % 2] if m < 2 else xT[TURNED.index(m) % 2]

        @block.scalar
        def _(act):
            act.wait_ge(s_gamma, 2)

            def section(ring, turn, i, seq, heads_too, build, tail):
                par, nxt = seq[1] % 2, (seq[1] + 1) % 2
                for s in range(ALL):
                    for m in TURN.get(s, []) * build:
                        n = height[m]
                        src = ring.wait_full(act, ("xT", i, m), turn)
                        kind = "x" if m >= 2 else "l"
                        for k in range(KC):
                            last = act.activation(turned(m, after(seq, 1))[:, k, 0:n], src[:, k * n:(k + 1) * n],
                                                  ACT.Identity, bias=env.col(f"xattn_{kind}_beta", k),
                                                  scale=env.col(f"xattn_{kind}_gamma", k))
                        last.then_inc(ring.free(("xT", i, m)), 1)
                    if heads_too and s < STEPS:
                        for u in (2 * s, 2 * s + 1):
                            ring.wait_read(act, ("S", i, u), turn)
                            act.activation(P[u % 4][:], P[u % 4][:], ACT.Exp, bias=low[:, u:u + 1],
                                           scale=-1.0).then_inc(s_exp, 1)
                    for j in range(2 * (tail and s == 0)):
                        src = ring.wait_full(act, ("oT", i, j), turn)
                        act.copy(oT[:, 4 * j:4 * j + 4, :].rearrange("p a b -> p (a b)"),
                                 src[:, 0:4 * T]).then_inc(ring.free(("oT", i, j)), 1)
                    if build and s == 1:
                        act.wait_ge(set_up, 6)
                    if build and s in BACK:
                        m = BACK[s]
                        n = height[m]
                        for j in range(2):
                            src = ring.wait_full(act, ("kT", i, m, j), turn)
                            s4 = heads(src[:, 0:4 * n], 4, n)
                            if m != 1:
                                at = chunk[m] * CT
                                op = act.copy(kT[nxt][:, 4 * j:4 * j + 4, at:at + n], s4)
                            else:
                                for half in range(2):
                                    rows = slice(64 * half, 64 * half + 64)
                                    op = act.mul(qT[nxt][rows, 4 * j:4 * j + 4, half, :], s4[rows],
                                                 qk_gamma[rows, :])
                            op.then_inc(ring.free(("kT", i, m, j)), 1)
                    if heads_too and 1 <= s <= STEPS:
                        u = 2 * s - 2
                        src = ring.wait_full(act, ("PT", i, u), turn)
                        act.copy(PT[u % 4][:], src[0:CT, 0:4 * T]).then_inc(ring.free(("PT", i, u)), 1)
                    if build and s in KEY:
                        m = KEY[s]
                        n = height[m]
                        for j in range(2):
                            src = ring.wait_full(act, ("mm", i, m, j), turn)
                            act.activation(sq[m % 2][0:n, j * 512:(j + 1) * 512], src[0:n, :], ACT.Square)\
                                .then_inc(s_sq, 1)
                    if build and s in VALUE:
                        m = VALUE[s]
                        n = height[m]
                        for j in range(2):
                            src = ring.wait_full(act, ("mm", i, m, 2 + j), turn)
                            act.copy(v[nxt][0:n, chunk[m], 8 * j:8 * j + 8, 0:DH], heads(src[0:n, :], 8, DH))\
                                .then_inc(ring.free(("mm", i, m, 2 + j)), 1)

            program_of(act, section)

        @block.vector
        def _(dve):
            dve.tensor_scalar(qk_gamma[:], env.col("q_gamma"), env.col("k_gamma"), -(DH ** -0.5),
                              ALU.mult, ALU.mult).then_inc(s_gamma, 2)
            norm_columns(dve, mv[:, B * NT:, :], stats[:, B * NT:, :], lambda k: env.x[:, k, :], B, T,
                         s_lstats, s_lvar, 1.0 + EPS, EPS * EPS)
            def normalise(m, seq):
                b = seq[0] * 2 + seq[1]
                n = height[m]
                at, row = (b * NT + chunk[m], b * NT + chunk[m]) if m >= 2 else (b + B * NT, b)
                src = (rows_in if m >= 2 else env.x)[0:n, bass.ds(row, 1), :].rearrange("p a d -> p (a d)")
                dve.tensor_scalar(xn[TURNED.index(m) % 2][0:n, :], src,
                                  mv[0:n, bass.ds(at, 1), 0:1].rearrange("p a o -> p (a o)"),
                                  mv[0:n, bass.ds(at, 1), 3:4].rearrange("p a o -> p (a o)"),
                                  ALU.subtract, ALU.mult).then_inc(s_xn, 1)

            def divide(ring, turn, i, seq, w):
                src = ring.wait_full(dve, ("O", i, w), turn)
                o4 = heads(src[0:T, 0:4 * (DH + 1)], 4, DH + 1)
                dve.reciprocal(rs[:, w, :], o4[:, :, DH]).then_inc(s_sum, 1)
                dve.wait_ge(s_sum, count(seq, H // 4, w))
                op = dve.tensor_tensor(heads(o[:, w * 4 * DH:(w + 1) * 4 * DH], 4, DH), o4[:, :, 0:DH],
                                       spread(rs[:, w, :], DH), ALU.mult)
                if w < H // 4 - 1:
                    op.then_inc(ring.free(("O", i, w)), 1)
                else:
                    op.then_inc(s_divided, 1)
                    dve.wait_ge(s_divided, count(seq, 1, 0))
                    dve.tensor_copy(whole[:], o4[0:1, 0, 0:1]).then_inc(ring.free(("O", i, w)), 1)

            def section(ring, turn, i, seq, heads_too, build, tail):
                par, nxt = seq[1] % 2, (seq[1] + 1) % 2
                following = after(seq, 1)
                if build and heads_too:
                    normalise(0, following)
                for s in range(ALL):
                    if not heads_too and build and 1 <= s < B:
                        for k in range(NT * s, NT * s + NT):
                            dve.bn_stats(stats[0:CT, k, :], rows_in[:, k, :]).then_inc(s_more, 1)
                    if heads_too and s < STEPS:
                        if s == 0:
                            dve.wait_ge(s_bias, count(seq, 1, 0))
                        for u in (2 * s, 2 * s + 1):
                            src = ring.wait_full(dve, ("S", i, u), turn)
                        dve.tensor_copy(waited[:, s:s + 1], src[0:1, 0:1])
                        for u in (2 * s, 2 * s + 1):
                            src = ring.bank(("S", i, u))
                            dve.tensor_tensor_reduce(out=P[u % 4][:], in0=src[0:T, 0:KEYS], in1=bias[par][:],
                                                     scale=1.0, scalar=BIG, op0=ALU.add, op1=ALU.min,
                                                     accum_out=low[:, u:u + 1])\
                                .then_inc(ring.free(("S", i, u)), 1)
                    for m in TURN.get(s + 1, []) * build:
                        if m >= 3:
                            ring.wait_full(dve, ("xT", i, TURNED[TURNED.index(m) - 2]), turn)
                        normalise(m, following)
                    if build and s - 1 in KEY:
                        m = KEY[s - 1]
                        n = height[m]
                        dve.wait_ge(s_rms, count(following, TILES, m))
                        for j in range(2):
                            ring.wait_read(dve, ("mm", i, m, j), turn)
                            part = heads(kn[m % 2][0:n, j * 512:(j + 1) * 512], 8, DH)
                            dve.tensor_tensor(part, part, spread(ssq[0:n, m, 1, 8 * j:8 * j + 8], DH),
                                              ALU.mult).then_inc(s_kn, 1)
                    if build and s == 4:
                        b = following[0] * 2 + following[1]
                        dve.tensor_scalar(bias[nxt][:, 0:C],
                                          mask_in[:, bass.ds(b, 1), :].rearrange("p a c -> p (a c)"),
                                          -BIG, BIG, ALU.mult, ALU.add).then_inc(s_bias, 1)
                    if heads_too and 1 <= s <= STEPS:
                        u = 2 * s - 1
                        src = ring.wait_full(dve, ("PT", i, u), turn)
                        dve.tensor_copy(PT[u % 4][:], src[0:CT, 0:4 * T]).then_inc(ring.free(("PT", i, u)), 1)
                    if heads_too and s >= 3 and s % 2 == 1:
                        divide(ring, turn, i, seq, (s - 3) // 2)
                    if build and s in KEY:
                        m = KEY[s]
                        n = height[m]
                        for j in range(2):
                            dve.wait_ge(s_sq, count(following, 2 * TILES, 2 * m + j))
                            dve.tensor_copy(kn[m % 2][0:n, j * 512:(j + 1) * 512],
                                            ring.bank(("mm", i, m, j))[0:n, :])\
                                .then_inc(ring.free(("mm", i, m, j)), 1)
                        dve.tensor_reduce(ssq[0:n, m, 0, :], heads(sq[m % 2][0:n, :], H, DH), AX.X, ALU.add)\
                            .then_inc(s_ssum, 1)
                        dve.wait_ge(s_ssum, count(following, TILES, m))
                        dve.tensor_scalar(ssq[0:n, m, 0, :], ssq[0:n, m, 0, :], 1.0 / DH, 1e-16, ALU.mult, ALU.max)\
                            .then_inc(s_mean, 1)
                    if tail and s == 1:
                        b = seq[0] * 2 + (seq[1] - 1)
                        xb = env.x[:, bass.ds(b, 1), :].rearrange("p a d -> p (a d)")
                        src = ring.wait_full(dve, ("out", i), turn)
                        dve.tensor_tensor(res[:], bo[:], src[0:T, 0:D], ALU.add).then_inc(ring.free(("out", i)), 1)
                        ring.wait_read(dve, ("out", i), turn)
                        dve.tensor_tensor(xb, xb, res[:], ALU.add).then_inc(s_res, 1)
                if build and not heads_too:
                    dve.wait_ge(s_more, MORE)
                    for k in range(NT, B * NT):
                        last = dve.bn_aggr(mv[0:CT, k, 0:2], stats[0:CT, k, :])
                    last.then_inc(s_more, 1)
                    dve.wait_ge(s_more, MORE + 1)
                    dve.tensor_scalar(mv[0:CT, NT:B * NT, 2], mv[0:CT, NT:B * NT, 1], EPS, None, ALU.add)\
                        .then_inc(s_var, 1)
                    dve.wait_ge(s_rstd, 3)
                    dve.wait_ge(set_up, 6)

            dve.wait_ge(s_rstd, 1)
            normalise(0, (0, 0))
            dve.wait_ge(ahead.loaded, ahead.all)
            norm_columns(dve, mv, stats, lambda k: rows_in[:, k, :], NT, CT, s_stats, s_var, 1.0, EPS)
            dve.wait_ge(s_rstd, 2)
            program_of(dve, section)

        @block.tensor
        def _(pe):
            pe.wait_ge(ahead.loaded, ahead.all)

            def multiply(ring, turn, i, seq, m, columns):
                n = height[m]
                w = wq if m == 1 else wkv
                for j in columns:
                    out = ring.wait_free(pe, ("mm", i, m, j), turn)
                    for k in range(KC):
                        last = pe.matmul(out[0:n, :], turned(m, seq)[:, k, 0:n], w[:, k, j * 512:(j + 1) * 512],
                                         start=k == 0, stop=k == KC - 1)
                    last.then_inc(ring.full(("mm", i, m, j)), 1)

            def turn_back(ring, turn, i, seq, m):
                for j in range(2):
                    out = ring.wait_free(pe, ("kT", i, m, j), turn)
                    pe.wait_ge(s_kn, count(seq, 2 * TILES, 2 * m + j))
                    transposes(pe, env, out, kn[m % 2][:, j * 512:(j + 1) * 512], height[m], 128, 4)\
                        .then_inc(ring.full(("kT", i, m, j)), 1)

            def section(ring, turn, i, seq, heads_too, build, tail):
                par = seq[1] % 2
                following = after(seq, 1)
                for s in range(ALL):
                    if heads_too and s < STEPS:
                        for u in (2 * s, 2 * s + 1):
                            out = ring.wait_free(pe, ("S", i, u), turn)
                            pe.matmul(out[0:T, 0:KEYS], qT[par][:, u // 2, u % 2, :], kT[par][:, u // 2, :],
                                      start=True, stop=True).then_inc(ring.full(("S", i, u)), 1)
                    for m in TURN.get(s, []) * build:
                        out = ring.wait_free(pe, ("xT", i, m), turn)
                        pe.wait_ge(s_xn, count(following, len(TURNED), TURNED.index(m)))
                        transposes(pe, env, out, xn[TURNED.index(m) % 2], height[m], 128, KC)\
                            .then_inc(ring.full(("xT", i, m)), 1)
                    if tail and s == 0:
                        pe.wait_ge(s_divided, count(after(seq, -1), 1, 0))
                        for j in range(2):
                            out = ring.wait_free(pe, ("oT", i, j), turn)
                            transposes(pe, env, out, o[:, j * 512:(j + 1) * 512], T, 128, 4)\
                                .then_inc(ring.full(("oT", i, j)), 1)
                    if tail and s == 1:
                        out = ring.wait_free(pe, ("out", i), turn)
                        ring.wait_read(pe, ("oT", i, 1), turn)
                        for k in range(8):
                            last = pe.matmul(out[0:T, 0:D], oT[:, k, :], wo[:, k, :], start=k == 0, stop=k == 7)
                        last.then_inc(ring.full(("out", i)), 1)
                    if build and s in BACK and s < ALL - 1:
                        turn_back(ring, turn, i, following, BACK[s])
                    if heads_too and s >= 3 and s % 2 == 1:
                        w = (s - 3) // 2
                        out = ring.wait_free(pe, ("O", i, w), turn)
                        for u in range(4 * w, 4 * w + 4):
                            if build and s == ALL - 1 and u == H - 1:
                                turn_back(ring, turn, i, following, BACK[s])
                            ring.wait_read(pe, ("PT", i, u), turn)
                            for c in range(NT + 1):
                                n = CT if c < NT else T
                                last = pe.matmul(out[0:T, (u % 4) * (DH + 1):(u % 4 + 1) * (DH + 1)],
                                                 PT[u % 4][0:n, c * T:(c + 1) * T], v[par][0:n, c, u, :],
                                                 start=c == 0, stop=c == NT)
                        last.then_inc(ring.full(("O", i, w)), 1)
                    if heads_too and 1 <= s <= STEPS:
                        for u in (2 * s - 2, 2 * s - 1):
                            out = ring.wait_free(pe, ("PT", i, u), turn)
                            pe.wait_ge(s_exp, count(seq, H, u))
                            for c in range(NT + 1):
                                n = CT if c < NT else T
                                last = pe.transpose(out[0:n, c * T:(c + 1) * T], P[u % 4][:, c * CT:c * CT + n],
                                                    env.ident[0:T, 0:T])
                            last.then_inc(ring.full(("PT", i, u)), 1)
                    if build and s in KEY:
                        m = KEY[s]
                        if m != 1:
                            ring.wait_read(pe, ("xT", i, m), turn)
                        multiply(ring, turn, i, following, m, (0, 1))
                    if build and s in VALUE:
                        multiply(ring, turn, i, following, VALUE[s], (2, 3))
                if build and not heads_too:
                    turn_back(ring, turn, i, following, TILES - 1)
                if build:
                    ring.wait_read(pe, ("kT", i, TILES - 1, 1), turn)

            program_of(pe, section)


def phase_kronecker_experts(nc, env, w_up, a_up, b_up, w_down, a_down, b_down, bias_up, bias_down, scales):
    ctx = ExitStack()
    with ctx:
        sb, sem = tools(nc, ctx, "kron")
        E, D1, F1 = 64, 32, 64
        N = 2 * T // 4
        NB = T // 4
        router_up = sb("router_up", [128, 8, E])
        router_down = sb("router_down", [128, F1, E])
        first_up = sb("b_up", [128, E, F1])
        second_up = sb("a_up", [128, E, F1])
        first_down = sb("b_down", [128, E, D1])
        second_down = sb("a_down", [128, E, D1])
        bias_u = sb("bias_up", [F1, F1])
        bias_d = sb("bias_down", [D1, D1])
        scale = sb("scales", [F1, 2])
        ones = sb("ones", [N, 128])
        zero = sb("zero", [128, 1])
        stats = sb("stats", [T, B, 6])
        mv = sb("mean_var", [T, B, 4])
        xn = [sb(f"xn{i}", [T, D]) for i in range(2)]
        xT = sb("xT", [128, KC, 2 * T])
        X = sb("X", [128, N, D1])
        W = [sb(f"W{i}", [128, 8, F1]) for i in range(4)]
        pre = [sb(f"pre{i}", [F1, 512]) for i in range(2)]
        h = sb("h", [128, N, F1])
        W2 = [sb(f"W2_{i}", [128, 16, D1]) for i in range(4)]
        y = sb("y", [D1, N, D1])
        yT = sb("yT", [128, KC, 2 * T])
        logits = [sb(f"logits{i}", [N, E]) for i in range(2)]
        top = [sb(f"top{i}", [N, 8]) for i in range(2)]
        which = [sb(f"which{i}", [N, 8], U32) for i in range(2)]
        which8 = [sb(f"which8_{i}", [N, 2], U8) for i in range(2)]
        prob = [sb(f"prob{i}", [N, 8]) for i in range(2)]
        diag = [sb(f"diag{i}", [N, N, 2]) for i in range(2)]
        pb = [sb(f"prob_rows{i}", [F1, 2 * N]) for i in range(2)]
        row = [sb(f"index_row{i}", [1, 2 * N], U8) for i in range(2)]
        waited = sb("waited", [1, 8])

        loaded, tables, zeroed, oned = sem("loaded"), sem("tables"), sem("zeroed"), sem("oned")
        pool_zeroed, s_zero = sem("pool_zeroed"), sem("zero")
        s_stats, s_var, s_rstd, s_xn = sem("stats"), sem("var"), sem("rstd"), sem("xn")
        s_X, s_h, s_pre, s_yT = sem("X"), sem("h"), sem("pre"), sem("yT")
        s_top, s_which, s_which8, s_diff, s_exp = sem("top"), sem("which"), sem("which8"), sem("diff"), sem("exp")
        s_den, s_p0, s_p1, s_diag = sem("den"), sem("p0"), sem("p1"), sem("diag")
        s_index = [sem("index_up"), sem("index_down")]

        UP_W, UP_H, DN_W = N // 4, N // 8, N // 8
        names = [("xT", 0), ("xT", 1), ("logits", 0), ("probs", 0)]
        for w in range(UP_W + 1):
            names += [("W", w)] * (w < UP_W) + [("h", (w - 1) // 2)] * (w >= 1 and (w - 1) % 2 == 0)
        names += [("logits", 1), ("probs", 1)]
        for w in range(DN_W + 1):
            names += [("W2", w)] * (w < DN_W) + [("y", w - 1)] * (w >= 1)
        names += [("back", 0), ("back", 1)]
        ring = Ring(env, names)
        low, high, whole = slice(D1, F1), slice(F1, 128), slice(0, 128)
        zeros_vector = [(second_down, high)]
        zeros_scalar = [(first_up, low), (first_down, high)]
        zeros_pool = [(X, whole)] + [(tile, whole) for tile in W] + [(first_up, high), (second_up, low),
                                                                      (second_up, high), (h, whole),
                                                                      (router_down, high)]
        zeros_pool += [(tile, whole) for tile in W2]
        AFTER_X, AFTER_W, AFTER_FIRST_UP, AFTER_SECOND_UP, AFTER_H = 1, 5, 6, 8, 9

        block = ctx.enter_context(nc.Block())

        @block.sync
        def _(sp):
            sp.dma_start(router_up[:], w_up).then_inc(loaded, 16)
            sp.dma_start(bias_u[:], bias_up).then_inc(loaded, 16)
            sp.dma_start(bias_d[:], bias_down).then_inc(loaded, 16)
            sp.dma_start(scale[:], scales.rearrange("(o d) -> o d", o=1).to_broadcast([F1, 2])).then_inc(loaded, 16)
            sp.dma_start(router_down[0:F1], w_down).then_inc(tables, 16)
            sp.dma_start(first_up[0:D1], b_up).then_inc(tables, 16)
            sp.dma_start(second_up[0:D1], a_up).then_inc(tables, 16)
            sp.dma_start(first_down[0:F1], b_down).then_inc(tables, 16)
            sp.dma_start(second_down[0:F1], a_down).then_inc(tables, 16)
            with sp.Fori(0, PAIRS) as t:
                for layer in range(2):
                    sp.wait_ge(s_which8, t * 2 + (layer + 1))
                    sp.dma_start(row[layer][:].rearrange("o (n k) -> o n k", k=2),
                                 which8[layer][:]).then_inc(s_index[layer], 16)

        @block.gpsimd
        def _(pool):
            pool.memset(ones[:], 1.0).then_inc(oned, 1)
            pool.wait_ge(oned, 1)
            pool.memset(zero[:], 0.0).then_inc(s_zero, 1)
            pool.wait_ge(s_zero, 1)
            pool.wait_ge(s_var, 1)
            pool.tensor_tensor(mv[:, :, 3], mv[:, :, 2], env.minus_half[0:T, 0:B], ALU.pow).then_inc(s_rstd, 1)
            pool.wait_ge(s_rstd, 1)
            for k, (tile, rows) in enumerate(zeros_pool):
                pool.memset(tile[rows], 0.0).then_inc(pool_zeroed, 1)
                pool.wait_ge(pool_zeroed, k + 1)

        @block.scalar
        def _(act):
            act.wait_ge(s_zero, 1)
            for tile, rows in zeros_scalar:
                act.copy(tile[rows], zero[rows].rearrange("p (a o) -> p a o", a=1).to_broadcast(tile[rows].shape))\
                    .then_inc(zeroed, 1)
            act.wait_ge(loaded, 64)
            with act.Fori(0, PAIRS) as t:
                for par in range(2):
                    src = ring.wait_full(act, ("xT", par), t)
                    act.copy(xT[:, :, par * T:(par + 1) * T],
                             src[:, 0:KC * T].rearrange("p (k n) -> p k n", k=KC)).then_inc(ring.free(("xT", par)), 1)
                ring.wait_read(act, ("xT", 1), t)
                act.wait_ge(pool_zeroed, AFTER_X)
                for ci in range(8):
                    k, q = divmod(ci, 4)
                    last = act.copy(X[0:D1].rearrange("p n (r c) -> p (n r) c", c=8)[:, :, ci],
                                    xT[32 * q:32 * q + 32, k, :])
                last.then_inc(s_X, 1)
                for layer in range(2):
                    act.wait_ge(s_diff, t * 2 + (layer + 1))
                    act.activation(prob[layer][:, 1:2], prob[layer][:, 0:1], ACT.Exp).then_inc(s_exp, 1)
                    if layer == 0:
                        act.wait_ge(pool_zeroed, AFTER_H)
                        for w in range(UP_H):
                            ring.wait_read(act, ("h", w), t)
                            act.activation(h[0:F1, 8 * w:8 * w + 8, :].rearrange("p n o -> p (n o)"),
                                           pre[w % 2][:], ACT.Gelu).then_inc(s_h, 1)
                ring.wait_read(act, ("y", DN_W - 1), t)
                for ci in range(8):
                    k, q = divmod(ci, 4)
                    last = act.copy(yT[32 * q:32 * q + 32, k, :],
                                    y[:].rearrange("p n (r c) -> p (n r) c", c=8)[:, :, ci])
                last.then_inc(s_yT, 1)

        @block.vector
        def _(dve):
            norm_columns(dve, mv, stats, lambda k: env.x[:, k, :], B, T, s_stats, s_var, 1.0, EPS)
            for tile, rows in zeros_vector:
                dve.memset(tile[rows], 0.0).then_inc(zeroed, 1)
            dve.wait_ge(s_rstd, 1)
            dve.wait_ge(loaded, 64)

            def route(layer, t):
                n = t * 2 + (layer + 1)
                p = prob[layer]
                src = ring.wait_full(dve, ("logits", layer), t)
                dve.tensor_copy(logits[layer][:], src[0:N, 0:E]).then_inc(ring.free(("logits", layer)), 1)
                ring.wait_read(dve, ("logits", layer), t)
                dve.tensor_copy(waited[:, 4 * layer:4 * layer + 1], logits[layer][0:1, 0:1])
                dve.max(top[layer][:], logits[layer][:]).then_inc(s_top, 1)
                dve.wait_ge(s_top, n)
                dve.tensor_tensor(p[:, 0:1], top[layer][:, 1:2], top[layer][:, 0:1], ALU.subtract)\
                    .then_inc(s_diff, 1)
                dve.max_index(which[layer][:], top[layer][:], logits[layer][:]).then_inc(s_which, 1)
                dve.wait_ge(s_which, n)
                dve.tensor_copy(which8[layer][:], which[layer][:, 0:2]).then_inc(s_which8, 1)
                dve.wait_ge(s_exp, n)
                dve.tensor_scalar(p[:, 2:3], p[:, 1:2], 1.0, None, ALU.add).then_inc(s_den, 1)
                dve.wait_ge(s_den, n)
                dve.reciprocal(p[:, 3:4], p[:, 2:3]).then_inc(s_p0, 1)
                dve.wait_ge(s_p0, n)
                dve.tensor_tensor(p[:, 4:5], p[:, 1:2], p[:, 3:4], ALU.mult).then_inc(s_p1, 1)
                dve.wait_ge(s_p1, n)
                dve.tensor_tensor(diag[layer][:], spread(env.ident[0:N, 0:N], 2),
                                  p[:, 3:5].rearrange("p (o k) -> p o k", o=1).to_broadcast([N, N, 2]),
                                  ALU.mult).then_inc(s_diag, 1)
                src = ring.wait_full(dve, ("probs", layer), t)
                dve.tensor_copy(pb[layer][:], src[0:F1, 0:2 * N]).then_inc(ring.free(("probs", layer)), 1)
                ring.wait_read(dve, ("probs", layer), t)

            with dve.Fori(0, PAIRS) as t:
                for par in range(2):
                    b = t * 2 + par
                    xb = env.x[:, bass.ds(b, 1), :].rearrange("p a d -> p (a d)")
                    dve.tensor_scalar(xn[par][:], xb, mv[:, bass.ds(b, 1), 0:1].rearrange("p a o -> p (a o)"),
                                      mv[:, bass.ds(b, 1), 3:4].rearrange("p a o -> p (a o)"),
                                      ALU.subtract, ALU.mult).then_inc(s_xn, 1)
                route(0, t)
                dve.wait_ge(pool_zeroed, AFTER_W)
                for w in range(UP_W + 1):
                    if w < UP_W:
                        src = ring.wait_full(dve, ("W", w), t)
                        dve.tensor_tensor(W[w % 4][0:D1], src[0:D1, :].rearrange("p (n f) -> p n f", n=8),
                                          spread(pb[0][0:D1, 8 * w:8 * w + 8], F1), ALU.mult)\
                            .then_inc(ring.free(("W", w)), 1)
                    if w >= 2 and w % 2 == 0:
                        m = w // 2 - 1
                        if m >= 2:
                            dve.wait_ge(s_h, t * UP_H + (m - 1))
                        src = ring.wait_full(dve, ("h", m), t)
                        dve.scalar_tensor_tensor(pre[m % 2][:].rearrange("p (n o) -> p n o", n=8),
                                                 src[0:F1, :].rearrange("p (n o) -> p n o", n=8), scale[:, 0:1],
                                                 bias_u[:].rearrange("p (a o) -> p a o", a=1)
                                                 .to_broadcast([F1, 8, F1]), ALU.mult, ALU.add)\
                            .then_inc(ring.free(("h", m)), 1)
                route(1, t)
                dve.wait_ge(pool_zeroed, len(zeros_pool))
                for w in range(DN_W + 1):
                    if w < DN_W:
                        src = ring.wait_full(dve, ("W2", w), t)
                        dve.tensor_tensor(W2[w % 4][0:F1], src[0:F1, :].rearrange("p (n f) -> p n f", n=16),
                                          spread(pb[1][:, 16 * w:16 * w + 16], D1), ALU.mult)\
                            .then_inc(ring.free(("W2", w)), 1)
                    if w >= 1:
                        u = w - 1
                        src = ring.wait_full(dve, ("y", u), t)
                        dve.scalar_tensor_tensor(y[:, 8 * u:8 * u + 8, :],
                                                 src[0:D1, 0:8 * D1].rearrange("p (n o) -> p n o", n=8),
                                                 scale[0:D1, 1:2],
                                                 bias_d[:].rearrange("p (a o) -> p a o", a=1)
                                                 .to_broadcast([D1, 8, D1]), ALU.mult, ALU.add)\
                            .then_inc(ring.free(("y", u)), 1)
                for par in range(2):
                    b = t * 2 + par
                    xb = env.x[:, bass.ds(b, 1), :].rearrange("p a d -> p (a d)")
                    src = ring.wait_full(dve, ("back", par), t)
                    dve.tensor_tensor(xb, xb, src[0:T, 0:D], ALU.add).then_inc(ring.free(("back", par)), 1)

        @block.tensor
        def _(pe):
            pe.wait_ge(loaded, 64)

            def picked(layer, first, count):
                _, got = nc.values_load_multi_w_load_instructions(
                    row[layer][0:1, first:first + count], engines=[mybir.EngineType.PE],
                    min_val=0, max_val=E - 1,
                    skip_runtime_bounds_check_because="max_index over E logits yields 0 .. E - 1")
                return got

            def probs(layer, t):
                out = ring.wait_free(pe, ("probs", layer), t)
                pe.wait_ge(s_index[layer], t * 16 + 16)
                if layer == 0:
                    pe.wait_ge(s_X, t + 1)
                pe.wait_ge(s_diag, t * 2 + (layer + 1))
                pe.matmul(out[:, 0:2 * N], ones[:], diag[layer][:].rearrange("p n k -> p (n k)"),
                          start=True, stop=True).then_inc(ring.full(("probs", layer)), 1)

            with pe.Fori(0, PAIRS) as t:
                for par in range(2):
                    out = ring.wait_free(pe, ("xT", par), t)
                    pe.wait_ge(s_xn, t * 2 + (par + 1))
                    transposes(pe, env, out, xn[par], T, 128, KC).then_inc(ring.full(("xT", par)), 1)
                out = ring.wait_free(pe, ("logits", 0), t)
                ring.wait_read(pe, ("xT", 1), t)
                for r in range(4):
                    for k in range(KC):
                        last = pe.matmul(out[0:N, 0:E], xT[:, k, r::4], router_up[:, KC * r + k, :],
                                         start=r + k == 0, stop=r == 3 and k == KC - 1)
                last.then_inc(ring.full(("logits", 0)), 1)
                pe.wait_ge(tables, 80)
                pe.wait_ge(zeroed, len(zeros_vector) + len(zeros_scalar))
                pe.wait_ge(pool_zeroed, AFTER_FIRST_UP)
                pe.wait_ge(oned, 1)
                probs(0, t)
                experts = None
                for w in range(UP_W + 1):
                    if w < UP_W:
                        former, experts = experts, picked(0, 8 * w, 8)
                        out = ring.wait_free(pe, ("W", w), t)
                        for m in range(8):
                            last = pe.matmul(out[0:D1, m * F1:(m + 1) * F1], X[:, 4 * w + m // 2, :],
                                             first_up[:, bass.ds(experts[m], 1), :].rearrange("p a f -> p (a f)"),
                                             start=True, stop=True)
                        last.then_inc(ring.full(("W", w)), 1)
                    if w >= 1:
                        u = w - 1
                        former = former if w < UP_W else experts
                        if w == 1:
                            pe.wait_ge(pool_zeroed, AFTER_SECOND_UP)
                        out = ring.wait_free(pe, ("h", u // 2), t) if u % 2 == 0 else ring.bank(("h", u // 2))
                        ring.wait_read(pe, ("W", u), t)
                        for m in range(8):
                            at = (u % 2) * 4 + m // 2
                            last = pe.matmul(out[0:F1, at * F1:(at + 1) * F1], W[u % 4][:, m, :],
                                             second_up[:, bass.ds(former[m], 1), :].rearrange("p a f -> p (a f)"),
                                             start=m % 2 == 0, stop=m % 2 == 1)
                        if u % 2 == 1:
                            last.then_inc(ring.full(("h", u // 2)), 1)
                out = ring.wait_free(pe, ("logits", 1), t)
                pe.wait_ge(s_h, t * UP_H + UP_H)
                pe.wait_ge(pool_zeroed, len(zeros_pool))
                for i in range(F1):
                    last = pe.matmul(out[0:N, 0:E], h[:, :, i], router_down[:, i, :],
                                     start=i == 0, stop=i == F1 - 1)
                last.then_inc(ring.full(("logits", 1)), 1)
                probs(1, t)
                experts = None
                for w in range(DN_W + 1):
                    if w < DN_W:
                        former, experts = experts, picked(1, 16 * w, 16)
                        out = ring.wait_free(pe, ("W2", w), t)
                        for m in range(16):
                            last = pe.matmul(out[0:F1, m * D1:(m + 1) * D1], h[:, 8 * w + m // 2, :],
                                             first_down[:, bass.ds(experts[m], 1), :].rearrange("p a f -> p (a f)"),
                                             start=True, stop=True)
                        last.then_inc(ring.full(("W2", w)), 1)
                    if w >= 1:
                        u = w - 1
                        former = former if w < DN_W else experts
                        out = ring.wait_free(pe, ("y", u), t)
                        ring.wait_read(pe, ("W2", u), t)
                        for m in range(16):
                            at = m // 2
                            last = pe.matmul(out[0:D1, at * D1:(at + 1) * D1], W2[u % 4][:, m, :],
                                             second_down[:, bass.ds(former[m], 1), :].rearrange("p a f -> p (a f)"),
                                             start=m % 2 == 0, stop=m % 2 == 1)
                        last.then_inc(ring.full(("y", u)), 1)
                pe.wait_ge(s_yT, t + 1)
                for par in range(2):
                    out = ring.wait_free(pe, ("back", par), t)
                    for k in range(KC):
                        last = pe.transpose(out[0:T, k * 128:(k + 1) * 128], yT[:, k, par * T:(par + 1) * T],
                                            env.ident[:])
                    last.then_inc(ring.full(("back", par)), 1)
        ring.close(PAIRS)


def phase_self_attention_scaled(nc, env, head_mask, ahead):
    ctx = ExitStack()
    with ctx:
        sb, sem = tools(nc, ctx, "scaled")
        DH, UNITS = 16, 8
        own = sb("own_features", [128, 8])
        scaled = sb("scaled_features", [128, KC, 8])
        stats = sb("stats", [T, B, 6])
        mv = sb("mean_var", [T, B, 4])
        xn = [sb(f"xn{i}", [T, D]) for i in range(2)]
        v = [sb(f"v{i}", [T, H, DH + 1]) for i in range(2)]
        xT = [sb(f"xT{i}", [128, KC, T]) for i in range(2)]
        km = [sb(f"km{i}", [128, H, T]) for i in range(2)]
        P = [sb(f"P{i}", [T, 4 * T]) for i in range(4)]
        PT = [sb(f"PT{i}", [T, 4 * T]) for i in range(2)]
        mx = sb("max", [T, UNITS, 4])
        rs = sb("recip", [T, UNITS, 4])
        o = [sb(f"o{i}", [T, D]) for i in range(2)]

        loaded, ones = sem("loaded"), sem("ones")
        s_stats, s_var, s_rstd, s_xn, s_own = sem("stats"), sem("var"), sem("rstd"), sem("xn"), sem("own")
        s_v, s_km, s_max, s_exp, s_sum, s_res = sem("v"), sem("km"), sem("max"), sem("exp"), sem("sum"), sem("res")

        units = [(g, par) for g in range(4) for par in range(2)]
        names = [("xT", par) for par in range(2)]
        for u in range(UNITS + 3):
            names += [("S", u)] * (u < UNITS) + [("PT", u - 2)] * (0 <= u - 2 < UNITS) + [("O", u - 3)] * (u >= 3)
        ring = Ring(env, names)
        block = ctx.enter_context(nc.Block())

        @block.sync
        def _(sp):
            sp.dma_start(own[:], head_mask).then_inc(loaded, 16)
            ahead.issue(sp)
            sp.wait_ge(loaded, 16)

        @block.gpsimd
        def _(pool):
            for i in range(2):
                pool.memset(v[i][:], 1.0).then_inc(ones, 1)
            pool.wait_ge(s_var, 1)
            pool.tensor_tensor(mv[:, :, 3], mv[:, :, 2], env.minus_half[0:T, 0:B], ALU.pow).then_inc(s_rstd, 1)

        @block.scalar
        def _(act):
            act.wait_ge(ones, 2)
            with act.Fori(0, PAIRS) as t:
                for par in range(2):
                    src = ring.wait_full(act, ("xT", par), t)
                    act.copy(xT[par][:].rearrange("p k n -> p (k n)"), src[:, 0:KC * T])\
                        .then_inc(ring.free(("xT", par)), 1)
                    act.wait_ge(s_xn, t * 2 + (par + 1))
                    act.copy(v[par][:, :, 0:DH], heads(xn[par][:], H, DH)).then_inc(s_v, 1)
                for u in range(UNITS + 2):
                    if u < UNITS:
                        ring.wait_read(act, ("S", u), t)
                        act.activation(P[u % 4][:], P[u % 4][:], ACT.Exp).then_inc(s_exp, 1)
                    if u >= 2:
                        src = ring.wait_full(act, ("PT", u - 2), t)
                        act.copy(PT[u % 2][:], src[0:T, 0:4 * T]).then_inc(ring.free(("PT", u - 2)), 1)

        @block.vector
        def _(dve):
            dve.wait_ge(loaded, 16)
            for k in range(KC):
                dve.tensor_scalar(scaled[:, k, :], own[:], env.col("rotation", k), env.col("entangle", k),
                                  ALU.mult, ALU.mult).then_inc(s_own, 1)
            norm_columns(dve, mv, stats, lambda k: env.x[:, k, :], B, T, s_stats, s_var, 1.0, EPS)
            dve.wait_ge(s_rstd, 1)
            dve.wait_ge(s_own, 2)
            with dve.Fori(0, PAIRS) as t:
                for par in range(2):
                    b = t * 2 + par
                    xb = env.x[:, bass.ds(b, 1), :].rearrange("p a d -> p (a d)")
                    dve.tensor_scalar(xn[par][:], xb, mv[:, bass.ds(b, 1), 0:1].rearrange("p a o -> p (a o)"),
                                      mv[:, bass.ds(b, 1), 3:4].rearrange("p a o -> p (a o)"),
                                      ALU.subtract, ALU.mult).then_inc(s_xn, 1)
                for par in range(2):
                    ring.wait_read(dve, ("xT", par), t)
                    for k in range(KC):
                        dve.tensor_tensor(km[par][:, 8 * k:8 * k + 8, :],
                                          xT[par][:, k, :].rearrange("p (a n) -> p a n", a=1)
                                          .to_broadcast([128, 8, T]), spread(scaled[:, k, :], T), ALU.mult)\
                            .then_inc(s_km, 1)
                for u in range(UNITS + 3):
                    if u < UNITS:
                        src = ring.wait_full(dve, ("S", u), t)
                        s4 = heads(src[0:T, 0:4 * T], 4, T)
                        dve.tensor_reduce(mx[:, u, :], s4, AX.X, ALU.max).then_inc(s_max, 1)
                        dve.wait_ge(s_max, t * UNITS + (u + 1))
                        dve.tensor_tensor(heads(P[u % 4][:], 4, T), s4, spread(mx[:, u, :], T),
                                          ALU.subtract).then_inc(ring.free(("S", u)), 1)
                    if u >= 3:
                        w = u - 3
                        g, par = units[w]
                        src = ring.wait_full(dve, ("O", w), t)
                        o4 = heads(src[0:T, 0:4 * (DH + 1)], 4, DH + 1)
                        dve.reciprocal(rs[:, w, :], o4[:, :, DH]).then_inc(s_sum, 1)
                        dve.wait_ge(s_sum, t * UNITS + (w + 1))
                        dve.tensor_tensor(heads(o[par][:, g * 4 * DH:(g + 1) * 4 * DH], 4, DH), o4[:, :, 0:DH],
                                          spread(rs[:, w, :], DH), ALU.mult).then_inc(ring.free(("O", w)), 1)
                for par in range(2):
                    b = t * 2 + par
                    xb = env.x[:, bass.ds(b, 1), :].rearrange("p a d -> p (a d)")
                    ring.wait_read(dve, ("O", UNITS - 2 + par), t)
                    dve.tensor_tensor(xb, xb, o[par][:], ALU.add).then_inc(s_res, 1)

        @block.tensor
        def _(pe):
            with pe.Fori(0, PAIRS) as t:
                for par in range(2):
                    out = ring.wait_free(pe, ("xT", par), t)
                    pe.wait_ge(s_xn, t * 2 + (par + 1))
                    transposes(pe, env, out, xn[par], T, 128, KC).then_inc(ring.full(("xT", par)), 1)
                for u in range(UNITS + 3):
                    if u < UNITS:
                        g, par = units[u]
                        out = ring.wait_free(pe, ("S", u), t)
                        pe.wait_ge(s_km, t * 4 + (2 * par + g // 2 + 1))
                        pe.matmul(out[0:T, 0:4 * T], xT[par][:, g // 2, :],
                                  km[par][:, 4 * g:4 * g + 4, :].rearrange("p a b -> p (a b)"),
                                  start=True, stop=True).then_inc(ring.full(("S", u)), 1)
                    if 0 <= u - 2 < UNITS:
                        w = u - 2
                        out = ring.wait_free(pe, ("PT", w), t)
                        pe.wait_ge(s_exp, t * UNITS + (w + 1))
                        transposes(pe, env, out, P[w % 4], T, T, 4).then_inc(ring.full(("PT", w)), 1)
                    if u >= 3:
                        w = u - 3
                        g, par = units[w]
                        out = ring.wait_free(pe, ("O", w), t)
                        ring.wait_read(pe, ("PT", w), t)
                        pe.wait_ge(s_v, t * 2 + (par + 1))
                        for i in range(4):
                            last = pe.matmul(out[0:T, i * (DH + 1):(i + 1) * (DH + 1)],
                                             PT[w % 2][:, i * T:(i + 1) * T], v[par][:, 4 * g + i, :],
                                             start=True, stop=True)
                        last.then_inc(ring.full(("O", w)), 1)
        ring.close(PAIRS)


def cross_attention_queries_ahead(nc, ctx, ctx_rows, head_mask, w_q, w_k, w_v, w_o, b_v, b_o):
    items = {name: ([128, KC, D], w.rearrange("(k p) n -> p k n", p=128), F32)
             for name, w in (("w_q", w_q), ("w_k", w_k), ("w_v", w_v), ("w_o", w_o))}
    items["ctx"] = ([CT, B * C // CT, D], ctx_rows.rearrange("b (c p) d -> p (b c) d", p=CT), F32)
    items["own_features"] = ([128, 8], head_mask, F32)
    items["b_v"] = ([CT, D], all_rows(b_v, CT), F32)
    items["b_o"] = ([T, D], all_rows(b_o, T), F32)
    return Ahead(nc, ctx, "over", items)


def phase_cross_attention_queries(nc, env, ahead, ahead_next):
    ctx = ExitStack()
    with ctx:
        sb, sem = tools(nc, ctx, "over")
        DH, UNITS, NT = 16, 8, C // CT
        SUB = UNITS * NT
        AHEAD = 9
        wq, wk, wv, wo = (ahead[n] for n in ("w_q", "w_k", "w_v", "w_o"))
        bv, bo, own, rows_in = (ahead[n] for n in ("b_v", "b_o", "own_features", "ctx"))
        rows_now = [sb(f"ctx_now{i}", [CT, NT, D]) for i in range(2)]
        stats = sb("stats", [T, B, 6])
        mv = sb("mean_var", [T, B, 4])
        xn = [env.y[:, i, :] for i in range(2)]
        xT = [sb(f"xT{i}", [128, KC, T]) for i in range(2)]
        qT = [sb(f"qT{i}", [128, KC, T]) for i in range(2)]
        qm = [sb(f"qm{i}", [128, H, T]) for i in range(2)]
        cT = [sb(f"cT{i}", [128, KC, C]) for i in range(2)]
        kT = [sb(f"kT{i}", [128, KC, C]) for i in range(2)]
        v = [sb(f"v{i}", [CT, NT, D]) for i in range(2)]
        P = [sb(f"P{i}", [CT, 4 * T]) for i in range(AHEAD)]
        V = [sb(f"V{i}", [CT, 4 * DH]) for i in range(AHEAD)]
        mx = sb("max", [CT, SUB, 4])
        low = sb("minus_max", [CT, SUB, 4])
        rs = sb("sums", [CT, SUB, 4])
        recip = sb("recip", [CT, SUB, 4])
        o = [env.y[:, 2 + i, :] for i in range(2)]
        oT = [sb(f"oT{i}", [128, KC, T]) for i in range(2)]
        res = [env.y[:, 4 + i, :] for i in range(2)]

        s_stats, s_var, s_rstd, s_xn = sem("stats"), sem("var"), sem("rstd"), sem("xn")
        s_rows = sem("rows")
        s_qm, s_max, s_low, s_exp = sem("qm"), sem("max"), sem("low"), sem("exp")
        s_den, s_rec, s_V, s_res = sem("den"), sem("rec"), sem("V"), sem("res")

        units = [(g, par) for par in range(2) for g in range(4)]

        def build(par):
            return [("xT", par), *(("cT", par, c) for c in range(NT)), ("qT", par),
                    *(("kT", par, m) for m in range(KC)), *(("v", par, c) for c in range(NT))]

        BETWEEN = {1 + i: [name] for i, name in enumerate(build(1))}
        names = build(0)
        for u in range(SUB + 6):
            names += [("S", u)] * (u < SUB) + [("O", u // 3 - 2)] * (u >= 8 and u % 3 == 2) + BETWEEN.get(u, [])
        names += [("oT", 0), ("oT", 1), ("out", 0), ("out", 1)]
        ring = Ring(env, names)
        block = ctx.enter_context(nc.Block())

        @block.sync
        def _(sp):
            ahead_next.issue(sp)

        @block.gpsimd
        def _(pool):
            pool.wait_ge(s_var, 1)
            pool.tensor_tensor(mv[:, :, 3], mv[:, :, 2], env.minus_half[0:T, 0:B], ALU.pow).then_inc(s_rstd, 1)
            with pool.Fori(0, PAIRS) as t:
                for w in range(SUB):
                    if w % (SUB // 2) == 0:
                        ring.wait_read(pool, ("v", w // (SUB // 2), NT - 1), t)
                    pool.wait_ge(s_rec, t * (SUB // 2) + (w // 2 + 1))
                    g, par = units[w // 3]
                    pool.tensor_tensor(heads(V[w % AHEAD][:], 4, DH),
                                       heads(v[par][:, w % 3, g * 4 * DH:(g + 1) * 4 * DH], 4, DH),
                                       spread(recip[:, w, :], DH), ALU.mult).then_inc(s_V, 1)

        @block.scalar
        def _(act):
            def evacuate(name, t):
                kind, par = name[:2]
                src = ring.wait_full(act, name, t)
                if kind == "xT":
                    last = act.copy(xT[par][:].rearrange("p k n -> p (k n)"), src[:, 0:KC * T])
                elif kind == "cT":
                    c = name[2]
                    last = act.copy(cT[par][:, :, c * CT:(c + 1) * CT],
                                    src[:, 0:KC * CT].rearrange("p (k n) -> p k n", k=KC))
                elif kind == "qT":
                    for m in range(KC):
                        last = act.activation(qT[par][:, m, :], src[:, m * T:(m + 1) * T], ACT.Identity,
                                              bias=env.col("bq", m))
                else:
                    m = name[2]
                    last = act.activation(kT[par][:, m, :], src[:, 0:C], ACT.Identity, bias=env.col("bk", m))
                last.then_inc(ring.free(name), 1)

            with act.Fori(0, PAIRS) as t:
                for name in build(0):
                    if name[0] != "v":
                        evacuate(name, t)
                for u in range(SUB + 6):
                    if u < SUB and u % 2 == 0:
                        ring.wait_read(act, ("S", u), t)
                        act.activation(P[u % AHEAD][:], P[u % AHEAD][:], ACT.Exp, scale=DH ** -0.5).then_inc(s_exp, 1)
                    elif u < SUB:
                        act.wait_ge(s_low, t * (SUB // 2) + (u // 2 + 1))
                        src = ring.bank(("S", u))
                        for i in range(4):
                            last = act.activation(P[u % AHEAD][:, i * T:(i + 1) * T], src[0:CT, i * T:(i + 1) * T],
                                                  ACT.Exp, bias=low[:, u, i:i + 1], scale=DH ** -0.5,
                                                  accum_out=rs[:, u, i:i + 1])
                        last.then_inc(ring.free(("S", u)), 1)
                    for name in BETWEEN.get(u, []):
                        if name[0] != "v":
                            evacuate(name, t)
                    if u >= 8 and u % 3 == 2:
                        w = u // 3 - 2
                        g, par = units[w]
                        src = ring.wait_full(act, ("O", w), t)
                        act.copy(o[par][:, g * 4 * DH:(g + 1) * 4 * DH], src[0:T, 0:4 * DH])\
                            .then_inc(ring.free(("O", w)), 1)
                for par in range(2):
                    src = ring.wait_full(act, ("oT", par), t)
                    act.copy(oT[par][:].rearrange("p k n -> p (k n)"), src[:, 0:KC * T])\
                        .then_inc(ring.free(("oT", par)), 1)

        @block.vector
        def _(dve):
            norm_columns(dve, mv, stats, lambda k: env.x[:, k, :], B, T, s_stats, s_var, 1.0, EPS)
            dve.wait_ge(s_rstd, 1)
            dve.wait_ge(ahead.loaded, ahead.all)
            def start(par, t):
                b = t * 2 + par
                xb = env.x[:, bass.ds(b, 1), :].rearrange("p a d -> p (a d)")
                dve.tensor_scalar(xn[par], xb, mv[:, bass.ds(b, 1), 0:1].rearrange("p a o -> p (a o)"),
                                  mv[:, bass.ds(b, 1), 3:4].rearrange("p a o -> p (a o)"),
                                  ALU.subtract, ALU.mult).then_inc(s_xn, 1)
                for c in range(NT):
                    row = rows_in[:, bass.ds((t * 2 + par) * NT + c, 1), :].rearrange("p a d -> p (a d)")
                    dve.tensor_copy(rows_now[par][:, c, :], row).then_inc(s_rows, 1)

            def mask_queries(par, t):
                for k in range(KC):
                    dve.tensor_tensor(qm[par][:, 8 * k:8 * k + 8, :],
                                      qT[par][:, k, :].rearrange("p (a n) -> p a n", a=1)
                                      .to_broadcast([128, 8, T]), spread(own[:], T), ALU.mult).then_inc(s_qm, 1)

            def add_bias(par, c, t):
                src = ring.wait_full(dve, ("v", par, c), t)
                dve.tensor_tensor(v[par][:, c, :], src[0:CT, 0:D], bv[:], ALU.add)\
                    .then_inc(ring.free(("v", par, c)), 1)

            with dve.Fori(0, PAIRS) as t:
                start(0, t)
                ring.wait_read(dve, ("qT", 0), t)
                mask_queries(0, t)
                for c in range(NT):
                    add_bias(0, c, t)
                for u in range(SUB + 1):
                    if u < SUB:
                        if u >= AHEAD:
                            ring.wait_full(dve, ("O", u // 3 - 3), t)
                        src = ring.wait_full(dve, ("S", u), t)
                        s4 = heads(src[0:CT, 0:4 * T], 4, T)
                        dve.tensor_reduce(mx[:, u, :], s4, AX.X, ALU.max).then_inc(s_max, 1)
                    if u >= 1 and u % 2 == 1:
                        w = u - 1
                        dve.wait_ge(s_exp, t * (SUB // 2) + (w // 2 + 1))
                        dve.tensor_reduce(rs[:, w, :], heads(P[w % AHEAD][:], 4, T), AX.X, ALU.add).then_inc(s_den, 1)
                    if u < SUB:
                        dve.wait_ge(s_max, t * SUB + (u + 1))
                        if u % 2 == 0:
                            dve.tensor_tensor(heads(P[u % AHEAD][:], 4, T), s4, spread(mx[:, u, :], T),
                                              ALU.subtract).then_inc(ring.free(("S", u)), 1)
                        else:
                            dve.tensor_scalar(low[:, u, :], mx[:, u, :], -(DH ** -0.5), None, ALU.mult)\
                                .then_inc(s_low, 1)
                    if u >= 2 and u % 2 == 0:
                        dve.wait_ge(s_den, t * (SUB // 2) + u // 2)
                        ring.wait_read(dve, ("S", u - 1), t)
                        dve.reciprocal(recip[:, u - 2:u, :], rs[:, u - 2:u, :]).then_inc(s_rec, 1)
                    if u == 0:
                        start(1, t)
                    for name in BETWEEN.get(u - 1, []):
                        if name[0] == "qT":
                            ring.wait_read(dve, name, t)
                            mask_queries(1, t)
                        if name[0] == "v":
                            add_bias(1, name[2], t)
                for par in range(2):
                    b = t * 2 + par
                    xb = env.x[:, bass.ds(b, 1), :].rearrange("p a d -> p (a d)")
                    src = ring.wait_full(dve, ("out", par), t)
                    dve.tensor_tensor(res[par], bo[:], src[0:T, 0:D], ALU.add).then_inc(ring.free(("out", par)), 1)
                    ring.wait_read(dve, ("out", par), t)
                    dve.tensor_tensor(xb, xb, res[par], ALU.add).then_inc(s_res, 1)

        @block.tensor
        def _(pe):
            pe.wait_ge(ahead.loaded, ahead.all)
            def produce(name, t):
                kind, par = name[:2]
                out = ring.wait_free(pe, name, t)
                if kind == "xT":
                    pe.wait_ge(s_xn, t * 2 + (par + 1))
                    last = transposes(pe, env, out, xn[par], T, 128, KC)
                elif kind == "cT":
                    c = name[2]
                    pe.wait_ge(s_rows, t * 2 * NT + (par * NT + c + 1))
                    last = transposes(pe, env, out, rows_now[par][:, c, :], CT, 128, KC)
                elif kind == "qT":
                    ring.wait_read(pe, ("xT", par), t)
                    for m in range(KC):
                        for k in range(KC):
                            last = pe.matmul(out[:, m * T:(m + 1) * T], wq[:, k, m * 128:(m + 1) * 128],
                                             xT[par][:, k, :], start=k == 0, stop=k == KC - 1)
                elif kind == "kT":
                    m = name[2]
                    ring.wait_read(pe, ("cT", par, NT - 1), t)
                    for k in range(KC):
                        last = pe.matmul(out[:, 0:C], wk[:, k, m * 128:(m + 1) * 128], cT[par][:, k, :],
                                         start=k == 0, stop=k == KC - 1)
                else:
                    c = name[2]
                    for k in range(KC):
                        last = pe.matmul(out[0:CT, 0:D], cT[par][:, k, c * CT:(c + 1) * CT], wv[:, k, :],
                                         start=k == 0, stop=k == KC - 1)
                last.then_inc(ring.full(name), 1)

            with pe.Fori(0, PAIRS) as t:
                for name in build(0):
                    produce(name, t)
                for u in range(SUB + 6):
                    if u < SUB:
                        g, par = units[u // 3]
                        c = u % 3
                        out = ring.wait_free(pe, ("S", u), t)
                        if c == 0:
                            pe.wait_ge(s_qm, t * 4 + (2 * par + g // 2 + 1))
                            ring.wait_read(pe, ("kT", par, g // 2), t)
                        pe.matmul(out[0:CT, 0:4 * T], kT[par][:, g // 2, c * CT:(c + 1) * CT],
                                  qm[par][:, 4 * g:4 * g + 4, :].rearrange("p a b -> p (a b)"),
                                  start=True, stop=True).then_inc(ring.full(("S", u)), 1)
                    if u >= 8 and u % 3 == 2:
                        w = u // 3 - 2
                        out = ring.wait_free(pe, ("O", w), t)
                        pe.wait_ge(s_V, t * SUB + (3 * w + 3))
                        for i in range(4):
                            for c in range(NT):
                                n = (3 * w + c) % AHEAD
                                last = pe.matmul(out[0:T, i * DH:(i + 1) * DH], P[n][:, i * T:(i + 1) * T],
                                                 V[n][:, i * DH:(i + 1) * DH], start=c == 0, stop=c == NT - 1)
                        last.then_inc(ring.full(("O", w)), 1)
                    for name in BETWEEN.get(u, []):
                        produce(name, t)
                for par in range(2):
                    out = ring.wait_free(pe, ("oT", par), t)
                    ring.wait_read(pe, ("O", 4 * par + 3), t)
                    transposes(pe, env, out, o[par], T, 128, KC).then_inc(ring.full(("oT", par)), 1)
                for par in range(2):
                    out = ring.wait_free(pe, ("out", par), t)
                    ring.wait_read(pe, ("oT", par), t)
                    for k in range(KC):
                        last = pe.matmul(out[0:T, 0:D], oT[par][:, k, :], wo[:, k, :], start=k == 0, stop=k == KC - 1)
                    last.then_inc(ring.full(("out", par)), 1)
        ring.close(PAIRS)


def attention_over_sequences_ahead(nc, ctx, w_in, w_out, b_v, b_out, ln_g, ln_b, block_bias):
    return Ahead(nc, ctx, "mha", {
        "w_in": ([128, KC, 3 * D], w_in.rearrange("(k p) n -> p k n", p=128), F32),
        "w_out": ([128, KC, D], w_out.rearrange("(k p) n -> p k n", p=128), F32),
        "block_bias": ([128, 128], block_bias, F32),
        "b_v": ([128, D], all_rows(b_v, 128), F32),
        "b_out": ([T, D], all_rows(b_out, T), F32),
        "ln_gamma": ([T, D], all_rows(ln_g, T), F32),
        "ln_beta": ([T, D], all_rows(ln_b, T), F32)})


def phase_attention_over_sequences(nc, env, ahead, ahead_next):
    ctx = ExitStack()
    with ctx:
        sb, sem = tools(nc, ctx, "mha")
        NH, DH, BL = 4, 64, T * B // 128
        win, wo, bv, bo, g1, b1, own = (ahead[n] for n in ("w_in", "w_out", "b_v", "b_out", "ln_gamma", "ln_beta",
                                                            "block_bias"))
        xT = sb("xT", [128, KC, T, B])
        qkT = sb("qkT", [128, 4, T * B])
        v = sb("v", [128, BL, NH, DH + 1])
        P = [sb(f"P{i}", [128, NH * 128]) for i in range(4)]
        PT = [sb(f"PT{i}", [128, NH * 128]) for i in range(2)]
        mx = sb("max", [128, BL, NH])
        rs = sb("recip", [128, BL, NH])
        o = [sb(f"o{i}", [128, D]) for i in range(2)]
        oT = sb("oT", [128, KC, B, T])
        res = [sb(f"res{i}", [T, D]) for i in range(2)]
        stats = sb("stats", [T, B, 6])
        mv = sb("mean_var", [T, B, 4])
        stats0 = sb("stats_in", [T, B, 6])
        mv0 = sb("mean_var_in", [T, B, 4])
        z = [sb(f"z{i}", [T, D]) for i in range(2)]

        ones = sem("ones")
        s_add, s_max, s_sub, s_exp, s_sum = (sem(n) for n in ("add", "max", "sub", "exp", "sum"))
        s_stats0, s_var0, s_rstd0, s_in = (sem(n) for n in ("stats_in", "var_in", "rstd_in", "normed_in"))
        s_res, s_stats, s_var, s_rstd, s_z, s_g, s_y = (sem(n) for n in ("res", "stats", "var", "rstd", "z", "g", "y"))

        names = [("xT", b) for b in range(B)]
        names += [("qkT", m, n) for n in range(2) for m in range(4)]
        names += [("v", u) for u in range(BL)]
        for u in range(BL + 4):
            names += [("S", u, 0), ("S", u, 1)] * (u < BL) + [("PT", u - 2)] * (0 <= u - 2 < BL)
            names += [("O", u - 3)] * (0 <= u - 3 < BL) + [("oT", u - 4)] * (u >= 4)
        names += [("out", b) for b in range(B)]
        ring = Ring(env, names)
        block = ctx.enter_context(nc.Block())

        @block.sync
        def _(sp):
            ahead_next.issue(sp)

        @block.gpsimd
        def _(pool):
            pool.memset(v[:], 1.0).then_inc(ones, 1)
            pool.wait_ge(s_var0, 1)
            pool.tensor_tensor(mv0[:, :, 3], mv0[:, :, 2], env.minus_half[0:T, 0:B], ALU.pow).then_inc(s_rstd0, 1)
            rstd_by_sequence(pool, env, mv, s_var, s_rstd)

        @block.scalar
        def _(act):
            for b in range(B):
                src = ring.wait_full(act, ("xT", b), 0)
                act.copy(xT[:, :, :, b], src[:, 0:KC * T].rearrange("p (k n) -> p k n", k=KC))\
                    .then_inc(ring.free(("xT", b)), 1)
            for n in range(2):
                for m in range(4):
                    src = ring.wait_full(act, ("qkT", m, n), 0)
                    act.activation(qkT[:, m, n * 448:(n + 1) * 448], src[:, 0:448], ACT.Identity,
                                   bias=env.col("in_proj_b", m)).then_inc(ring.free(("qkT", m, n)), 1)
            for u in range(BL + 4):
                if u < BL:
                    act.wait_ge(s_sub, u + 1)
                    act.activation(P[u % 4][:], P[u % 4][:], ACT.Exp, scale=DH ** -0.5).then_inc(s_exp, 1)
                if 0 <= u - 2 < BL:
                    src = ring.wait_full(act, ("PT", u - 2), 0)
                    act.copy(PT[u % 2][:], src[:, :]).then_inc(ring.free(("PT", u - 2)), 1)
                if u >= 4:
                    w = u - 4
                    src = ring.wait_full(act, ("oT", w), 0)
                    for k in range(KC):
                        last = act.copy(oT[:, k, :, 16 * w:16 * w + 16].rearrange("p l n -> p n l"),
                                        src[:, k * 128:(k + 1) * 128].rearrange("p (n l) -> p n l", l=B))
                    last.then_inc(ring.free(("oT", w)), 1)

        @block.vector
        def _(dve):
            norm_columns(dve, mv0, stats0, lambda k: env.x[:, k, :], B, T, s_stats0, s_var0, 1.0, EPS)
            dve.wait_ge(s_rstd0, 1)
            for b in range(B):
                dve.tensor_scalar(env.y[:, b, :], env.x[:, b, :], mv0[:, b, 0:1], mv0[:, b, 3:4],
                                  ALU.subtract, ALU.mult).then_inc(s_in, 1)
            dve.wait_ge(ahead.loaded, ahead.all)
            dve.wait_ge(ones, 1)
            for u in range(BL):
                src = ring.wait_full(dve, ("v", u), 0)
                dve.tensor_tensor(v[:, u, :, 0:DH], heads(src[:, 0:D], NH, DH), heads(bv[:], NH, DH), ALU.add)\
                    .then_inc(ring.free(("v", u)), 1)
            for u in range(BL + 3):
                if u < BL:
                    p4 = heads(P[u % 4][:], NH, 128)
                    for a in range(2):
                        src = ring.wait_full(dve, ("S", u, a), 0)
                        dve.tensor_tensor(p4[:, 2 * a:2 * a + 2, :], heads(src[:, 0:256], 2, 128),
                                          own[:].rearrange("p (a n) -> p a n", a=1).to_broadcast([128, 2, 128]),
                                          ALU.add).then_inc(ring.free(("S", u, a)), 1)
                        ring.wait_read(dve, ("S", u, a), 0)
                    dve.tensor_reduce(mx[:, u, :], p4, AX.X, ALU.max).then_inc(s_max, 1)
                    dve.wait_ge(s_max, u + 1)
                    dve.tensor_tensor(p4, p4, spread(mx[:, u, :], 128), ALU.subtract).then_inc(s_sub, 1)
                if u >= 3:
                    w = u - 3
                    src = ring.wait_full(dve, ("O", w), 0)
                    o4 = heads(src[:, 0:NH * (DH + 1)], NH, DH + 1)
                    dve.reciprocal(rs[:, w, :], o4[:, :, DH]).then_inc(s_sum, 1)
                    dve.wait_ge(s_sum, w + 1)
                    dve.tensor_tensor(heads(o[w % 2][:], NH, DH), o4[:, :, 0:DH], spread(rs[:, w, :], DH),
                                      ALU.mult).then_inc(ring.free(("O", w)), 1)

            def add_bias(b):
                src = ring.wait_full(dve, ("out", b), 0)
                dve.tensor_tensor(res[b % 2][:], bo[:], src[0:T, 0:D], ALU.add).then_inc(ring.free(("out", b)), 1)

            def add(b):
                ring.wait_read(dve, ("out", b), 0)
                dve.tensor_tensor(env.y[:, b, :], env.y[:, b, :], res[b % 2][:], ALU.add).then_inc(s_res, 1)

            def added(b):
                dve.wait_ge(s_res, b + 1)

            add_and_normalise(dve, env, (add_bias, add, added), stats, mv, z, g1, b1, s_stats, s_var, s_rstd,
                              s_z, s_g, s_y)

        @block.tensor
        def _(pe):
            pe.wait_ge(ahead.loaded, ahead.all)
            for b in range(B):
                out = ring.wait_free(pe, ("xT", b), 0)
                pe.wait_ge(s_in, b + 1)
                transposes(pe, env, out, env.y[:, b, :], T, 128, KC).then_inc(ring.full(("xT", b)), 1)
            for b in range(B):
                ring.wait_read(pe, ("xT", b), 0)
            cols = xT[:].rearrange("p k n l -> p k (n l)")
            for n in range(2):
                for m in range(4):
                    out = ring.wait_free(pe, ("qkT", m, n), 0)
                    for k in range(KC):
                        last = pe.matmul(out[:, 0:448], win[:, k, m * 128:(m + 1) * 128],
                                         cols[:, k, n * 448:(n + 1) * 448], start=k == 0, stop=k == KC - 1)
                    last.then_inc(ring.full(("qkT", m, n)), 1)
            for u in range(BL):
                out = ring.wait_free(pe, ("v", u), 0)
                for k in range(KC):
                    last = pe.matmul(out[:, 0:D], cols[:, k, u * 128:(u + 1) * 128], win[:, k, 2 * D:3 * D],
                                     start=k == 0, stop=k == KC - 1)
                last.then_inc(ring.full(("v", u)), 1)
            for n in range(2):
                for m in range(4):
                    ring.wait_read(pe, ("qkT", m, n), 0)
            for u in range(BL + 4):
                if u < BL:
                    for a in range(2):
                        out = ring.wait_free(pe, ("S", u, a), 0)
                        rows_a = slice(64 * a, 64 * a + 64)
                        for j in range(2):
                            last = pe.matmul(out[:, j * 128:(j + 1) * 128],
                                             qkT[rows_a, j, u * 128:(u + 1) * 128],
                                             qkT[rows_a, 2 + j, u * 128:(u + 1) * 128], start=True, stop=True)
                        last.then_inc(ring.full(("S", u, a)), 1)
                if 0 <= u - 2 < BL:
                    w = u - 2
                    out = ring.wait_free(pe, ("PT", w), 0)
                    pe.wait_ge(s_exp, w + 1)
                    transposes(pe, env, out, P[w % 4], 128, 128, NH).then_inc(ring.full(("PT", w)), 1)
                if 0 <= u - 3 < BL:
                    w = u - 3
                    out = ring.wait_free(pe, ("O", w), 0)
                    ring.wait_read(pe, ("PT", w), 0)
                    ring.wait_read(pe, ("v", w), 0)
                    for h in range(NH):
                        i = (h % 2) * 2 + h // 2
                        last = pe.matmul(out[:, h * (DH + 1):(h + 1) * (DH + 1)],
                                         PT[w % 2][:, i * 128:(i + 1) * 128], v[:, w, h, :], start=True, stop=True)
                    last.then_inc(ring.full(("O", w)), 1)
                if u >= 4:
                    w = u - 4
                    out = ring.wait_free(pe, ("oT", w), 0)
                    ring.wait_read(pe, ("O", w), 0)
                    transposes(pe, env, out, o[w % 2], 128, 128, KC).then_inc(ring.full(("oT", w)), 1)
            ring.wait_read(pe, ("oT", BL - 1), 0)
            for b in range(B):
                out = ring.wait_free(pe, ("out", b), 0)
                for k in range(KC):
                    last = pe.matmul(out[0:T, 0:D], oT[:, k, b, :], wo[:, k, :], start=k == 0, stop=k == KC - 1)
                last.then_inc(ring.full(("out", b)), 1)
        ring.close(1)


def add_and_normalise(dve, env, adding, stats, mv, z, gamma, beta, s_stats, s_var, s_rstd, s_z, s_g, s_y,
                      after=lambda b: None):
    first, second, added = adding
    for b in range(B + 1):
        c = b - 1
        if b < B:
            first(b)
        if c >= 0:
            dve.wait_ge(s_rstd, c + 1)
            dve.tensor_scalar(z[c % 2][:], env.y[:, c, :], mv[:, c, 0:1], mv[:, c, 3:4],
                              ALU.subtract, ALU.mult).then_inc(s_z, 1)
        if b < B:
            second(b)
        if c >= 0:
            dve.wait_ge(s_z, c + 1)
            dve.tensor_tensor(z[c % 2][:], z[c % 2][:], gamma[:], ALU.mult).then_inc(s_g, 1)
        if b < B:
            added(b)
            dve.bn_stats(stats[:, b, :], env.y[:, b, :]).then_inc(s_stats, 1)
        if c >= 0:
            dve.wait_ge(s_g, c + 1)
            dve.tensor_tensor(env.y[:, c, :], z[c % 2][:], beta[:], ALU.add).then_inc(s_y, 1)
        if b < B:
            dve.wait_ge(s_stats, 2 * b + 1)
            dve.bn_aggr(mv[:, b, 0:2], stats[:, b, :]).then_inc(s_stats, 1)
            dve.wait_ge(s_stats, 2 * b + 2)
            dve.tensor_scalar(mv[:, b, 2:3], mv[:, b, 1:2], EPS, None, ALU.add).then_inc(s_var, 1)
        if c >= 0:
            dve.wait_ge(s_y, c + 1)
            after(c)


def rstd_by_sequence(pool, env, mv, s_var, s_rstd):
    for b in range(B):
        pool.wait_ge(s_var, b + 1)
        pool.tensor_tensor(mv[:, b, 3:4], mv[:, b, 2:3], env.minus_half[0:T, 0:1], ALU.pow).then_inc(s_rstd, 1)


def capacity_experts_ahead(nc, ctx, w_gate, w1, w2, b2, ln_g, ln_b, slots, slot_ids, iota8, before):
    E, CAP, FF = 8, B * T // 8, 1024
    items = {
        "w_gate": ([128, KC, E], w_gate.rearrange("(k p) n -> p k n", p=128), F32),
        "slot_row": ([T, E * CAP], all_rows(slots, T), F32),
        "slot_id": ([CAP, E], slot_ids, F32),
        "iota8": ([T, E], all_rows(iota8, T), F32),
        "earlier": ([T, T], before, F32),
        "b2": ([CAP, E, D], b2.rearrange("(o e) d -> o e d", o=1).to_broadcast([CAP, E, D]), F32),
        "ln_gamma": ([T, D], all_rows(ln_g, T), F32),
        "ln_beta": ([T, D], all_rows(ln_b, T), F32)}
    for e in range(4):
        items[f"w1_{e}"] = ([128, KC, FF], w1[e].rearrange("(k p) n -> p k n", p=128), F32)
        items[f"w2_{e}"] = ([128, FF // 128, D], w2[e].rearrange("(k p) n -> p k n", p=128), F32)
    return Ahead(nc, ctx, "moe", items)


def phase_capacity_experts(nc, env, out, ahead, w1, w2):
    ctx = ExitStack()
    with ctx:
        sb, sem = tools(nc, ctx, "moe")
        E, CAP, FF, WB = 8, B * T // 8, 1024, 4
        FC = FF // 128
        w1_sb = [ahead[f"w1_{i}"] for i in range(WB)]
        w2_sb = [ahead[f"w2_{i}"] for i in range(WB)]
        wg, b2_sb, g2, be2 = (ahead[n] for n in ("w_gate", "b2", "ln_gamma", "ln_beta"))
        slot_row, slot_id, io, earlier = (ahead[n] for n in ("slot_row", "slot_id", "iota8", "earlier"))
        ones = sb("ones", [T, T])
        yT = sb("yT", [128, KC, B, T])
        logits = sb("logits", [T, B, E])
        mx = sb("max", [T, B])
        eq = sb("eq", [T, B, E])
        cand = sb("cand", [T, B, E])
        best = sb("best", [T, B])
        hot = sb("one_hot", [T, B, E])
        ex = sb("exp", [T, B, E])
        gate = sb("gate", [T, B, 2])
        loc = sb("loc", [T, B])
        lochot = sb("lochot", [T, B, E])
        over = sb("over", [T, B])
        slot = sb("slot", [T, B])
        Pm = sb("into_slots", [T, B, E * CAP])
        diag = [sb(f"diag{i}", [T, T]) for i in range(B)]
        srow = sb("slot_of_token", [CAP, B * T])
        R = sb("from_slots", [CAP, E, B * T])
        dT = sb("dispatched", [128, KC, E * CAP])
        hT = [sb(f"hT{i}", [128, FC, CAP]) for i in range(2)]
        ys = sb("expert_out", [CAP, E, D])
        stats = sb("stats", [T, B, 6])
        mv = sb("mean_var", [T, B, 4])
        z = [sb(f"z{i}", [T, D]) for i in range(2)]

        s_ones, stored, s_end = sem("ones"), sem("stored"), sem("end")
        w_in = [sem(f"w_in{i}") for i in range(WB)]
        chain = sem("routing_step")
        s_sub, s_exp, s_hot, s_slot, s_P, s_diag, s_R = (sem(n) for n in ("sub", "exp", "hot", "slot", "P", "diag", "R"))
        s_res, s_stats, s_var, s_rstd, s_z, s_g, s_y = (sem(n) for n in ("res", "stats", "var", "rstd", "z", "g", "y"))
        HALF = E * CAP // 2

        names = [("yT", b) for b in range(B)] + [("logits", 0), ("loc", 0), ("row", 0), ("row", 1)]
        names += [("d", n, k) for n in range(2) for k in range(KC)]
        ring = Ring(env, names)
        ring.close(1)
        TURNS = E // WB
        names = [("h", 0, 0), ("h", 0, 1)]
        for i in range(WB):
            names += [("h", i + 1, 0), ("h", i + 1, 1)] * (i + 1 < WB) + [("y", i)]
        work = Ring(env, names)
        work.close(TURNS)
        back = Ring(env, [("x", b) for b in range(B)])
        back.close(1)
        block = ctx.enter_context(nc.Block())

        @block.sync
        def _(sp):
            sp.wait_ge(ahead.loaded, ahead.all)
            for e in range(WB):
                sp.sem_inc(w_in[e], 32)
            for e in range(WB, E):
                work.wait_full(sp, ("y", e - WB), 0)
                sp.dma_start(w1_sb[e - WB][:], w1[e].rearrange("(k p) n -> p k n", p=128)).then_inc(w_in[e - WB], 16)
                sp.dma_start(w2_sb[e - WB][:], w2[e].rearrange("(k p) n -> p k n", p=128)).then_inc(w_in[e - WB], 16)
            for b in range(B):
                sp.wait_ge(s_end, b + 1)
                sp.dma_start(out[b], env.x[:, b, :]).then_inc(stored, 16)
            sp.wait_ge(stored, 16 * B)

        @block.gpsimd
        def _(pool):
            pool.memset(ones[:], 1.0).then_inc(s_ones, 1)
            pool.wait_ge(s_ones, 1)
            pool.wait_ge(ahead.loaded, ahead.all)
            for n in range(2):
                ring.wait_read(pool, ("row", n), 0)
            for e in range(E):
                pool.tensor_scalar(R[:, e, :], srow[:], slot_id[:, e:e + 1], None, ALU.is_equal).then_inc(s_R, 1)
            rstd_by_sequence(pool, env, mv, s_var, s_rstd)

        @block.scalar
        def _(act):
            for b in range(B):
                src = ring.wait_full(act, ("yT", b), 0)
                act.copy(yT[:, :, b, :], src[:, 0:KC * T].rearrange("p (k n) -> p k n", k=KC))\
                    .then_inc(ring.free(("yT", b)), 1)
            act.wait_ge(s_sub, 1)
            act.activation(ex[:], ex[:], ACT.Exp).then_inc(s_exp, 1)
            for n in range(2):
                src = ring.wait_full(act, ("row", n), 0)
                act.copy(srow[:, n * HALF:(n + 1) * HALF], src[0:CAP, 0:HALF]).then_inc(ring.free(("row", n)), 1)
            for n in range(2):
                for k in range(KC):
                    src = ring.wait_full(act, ("d", n, k), 0)
                    act.copy(dT[:, k, n * HALF:(n + 1) * HALF], src[:, 0:HALF]).then_inc(ring.free(("d", n, k)), 1)

        @block.vector
        def _(dve):
            steps = [0]

            def step(op):
                steps[0] += 1
                op.then_inc(chain, 1)
                dve.wait_ge(chain, steps[0])

            dve.wait_ge(ahead.loaded, ahead.all)
            per_expert = io[:].rearrange("p (b e) -> p b e", b=1).to_broadcast([T, B, E])
            src = ring.wait_full(dve, ("logits", 0), 0)
            dve.tensor_copy(logits[:], src[0:T, 0:B * E].rearrange("p (b e) -> p b e", b=B))\
                .then_inc(ring.free(("logits", 0)), 1)
            ring.wait_read(dve, ("logits", 0), 0)
            step(dve.tensor_reduce(mx[:], logits[:], AX.X, ALU.max))
            dve.tensor_tensor(ex[:], logits[:], spread(mx[:], E), ALU.subtract).then_inc(s_sub, 1)
            step(dve.tensor_tensor(eq[:], logits[:], spread(mx[:], E), ALU.is_equal))
            step(dve.scalar_tensor_tensor(cand[:], eq[:], -float(E), per_expert, ALU.mult, ALU.add))
            step(dve.tensor_reduce(best[:], cand[:], AX.X, ALU.min))
            step(dve.tensor_scalar(best[:], best[:], float(E), None, ALU.add))
            dve.tensor_tensor(hot[:], per_expert, spread(best[:], E), ALU.is_equal).then_inc(s_hot, 1)
            dve.wait_ge(s_hot, 1)
            dve.wait_ge(s_exp, 1)
            step(dve.tensor_reduce(gate[:, :, 0], ex[:], AX.X, ALU.add))
            step(dve.reciprocal(gate[:, :, 1], gate[:, :, 0]))
            src = ring.wait_full(dve, ("loc", 0), 0)
            dve.tensor_tensor(lochot[:], src[0:T, 0:B * E].rearrange("p (b e) -> p b e", b=B), hot[:], ALU.mult)\
                .then_inc(ring.free(("loc", 0)), 1)
            ring.wait_read(dve, ("loc", 0), 0)
            step(dve.tensor_reduce(loc[:], lochot[:], AX.X, ALU.add))
            step(dve.tensor_scalar(over[:], loc[:], float(CAP), float(4 * E * CAP), ALU.is_ge, ALU.mult))
            step(dve.scalar_tensor_tensor(slot[:], best[:], float(CAP), loc[:], ALU.mult, ALU.add))
            step(dve.tensor_tensor(slot[:], slot[:], over[:], ALU.add))
            for b in range(B):
                dve.tensor_scalar(diag[b][:], env.ident[0:T, 0:T], slot[:, b:b + 1], None, ALU.mult)\
                    .then_inc(s_diag, 1)
            for b in range(B):
                dve.tensor_scalar(Pm[:, b, :], slot_row[:], slot[:, b:b + 1], None, ALU.is_equal).then_inc(s_P, 1)

            b1_at = env.column_at("b1")
            with dve.Fori(0, TURNS) as t:
                for i in range(WB + 1):
                    if i < WB:
                        e = t * WB + i
                        for a in range(2):
                            src = work.wait_full(dve, ("h", i, a), t)
                            b1 = env.columns[:, bass.ds(e * FC + (b1_at + 4 * a), 4)]
                            dve.tensor_tensor(hT[i % 2][:, 4 * a:4 * a + 4, :], heads(src[:, 0:4 * CAP], 4, CAP),
                                              spread(b1, CAP), ALU.add).then_inc(work.free(("h", i, a)), 1)
                    if i >= 1:
                        e = t * WB + (i - 1)
                        src = work.wait_full(dve, ("y", i - 1), t)
                        dve.tensor_tensor(ys[:, bass.ds(e, 1), :].rearrange("p a d -> p (a d)"), src[0:CAP, 0:D],
                                          b2_sb[:, bass.ds(e, 1), :].rearrange("p a d -> p (a d)"), ALU.add)\
                            .then_inc(work.free(("y", i - 1)), 1)

            def add(b):
                src = back.wait_full(dve, ("x", b), 0)
                dve.scalar_tensor_tensor(env.y[:, b, :], src[0:T, 0:D], gate[:, b, 1:2], env.y[:, b, :],
                                         ALU.mult, ALU.add).then_inc(back.free(("x", b)), 1)

            def added(b):
                back.wait_read(dve, ("x", b), 0)

            def add_to_stream(b):
                dve.tensor_tensor(env.x[:, b, :], env.x[:, b, :], env.y[:, b, :], ALU.add).then_inc(s_end, 1)

            add_and_normalise(dve, env, (add, lambda b: None, added), stats, mv, z, g2, be2, s_stats, s_var, s_rstd,
                              s_z, s_g, s_y, add_to_stream)

        @block.tensor
        def _(pe):
            pe.wait_ge(ahead.loaded, ahead.all)
            pe.wait_ge(s_ones, 1)
            for b in range(B):
                out_ = ring.wait_free(pe, ("yT", b), 0)
                transposes(pe, env, out_, env.y[:, b, :], T, 128, KC).then_inc(ring.full(("yT", b)), 1)
            acc = ring.wait_free(pe, ("logits", 0), 0)
            for b in range(B):
                ring.wait_read(pe, ("yT", b), 0)
                for k in range(KC):
                    last = pe.matmul(acc[0:T, b * E:(b + 1) * E], yT[:, k, b, :], wg[:, k, :],
                                     start=k == 0, stop=k == KC - 1)
            last.then_inc(ring.full(("logits", 0)), 1)
            acc = ring.wait_free(pe, ("loc", 0), 0)
            pe.wait_ge(s_hot, 1)
            pe.matmul(acc[0:T, 0:B * E], earlier[:], hot[:].rearrange("p b e -> p (b e)"), start=True, stop=False)
            for d in range(1, B):
                last = pe.matmul(acc[0:T, d * E:B * E], ones[:], hot[:, 0:B - d, :].rearrange("p b e -> p (b e)"),
                                 start=False, stop=d == B - 1)
            last.then_inc(ring.full(("loc", 0)), 1)
            for n in range(2):
                acc = ring.wait_free(pe, ("row", n), 0)
                for i in range(4):
                    b = 4 * n + i
                    pe.wait_ge(s_diag, b + 1)
                    last = pe.matmul(acc[0:CAP, i * T:(i + 1) * T], ones[:, 0:CAP], diag[b][:], start=True, stop=True)
                last.then_inc(ring.full(("row", n)), 1)
            for n in range(2):
                for k in range(KC):
                    acc = ring.wait_free(pe, ("d", n, k), 0)
                    for b in range(B):
                        if n + k == 0:
                            pe.wait_ge(s_P, b + 1)
                        last = pe.matmul(acc[:, 0:HALF], env.y[:, b, k * 128:(k + 1) * 128],
                                         Pm[:, b, n * HALF:(n + 1) * HALF], start=b == 0, stop=b == B - 1)
                    last.then_inc(ring.full(("d", n, k)), 1)
            for n in range(2):
                for k in range(KC):
                    ring.wait_read(pe, ("d", n, k), 0)

            def hidden(i, t):
                pe.wait_ge(w_in[i], t * 32 + 32)
                for a in range(2):
                    acc = work.wait_free(pe, ("h", i, a), t)
                    for f in range(4):
                        for k in range(KC):
                            last = pe.matmul(acc[:, f * CAP:(f + 1) * CAP],
                                             w1_sb[i][:, k, (4 * a + f) * 128:(4 * a + f + 1) * 128],
                                             dT[:, k, bass.ds((t * WB + i) * CAP, CAP)],
                                             start=k == 0, stop=k == KC - 1)
                    last.then_inc(work.full(("h", i, a)), 1)

            with pe.Fori(0, TURNS) as t:
                hidden(0, t)
                for i in range(WB):
                    if i + 1 < WB:
                        hidden(i + 1, t)
                    acc = work.wait_free(pe, ("y", i), t)
                    work.wait_read(pe, ("h", i, 0), t)
                    work.wait_read(pe, ("h", i, 1), t)
                    for f in range(FC):
                        last = pe.matmul(acc[0:CAP, 0:D], hT[i % 2][:, f, :], w2_sb[i][:, f, :],
                                         start=f == 0, stop=f == FC - 1)
                    last.then_inc(work.full(("y", i)), 1)
            work.wait_read(pe, ("y", WB - 1), TURNS - 1)
            pe.wait_ge(s_R, E)
            for b in range(B):
                acc = back.wait_free(pe, ("x", b), 0)
                for e in range(E):
                    last = pe.matmul(acc[0:T, 0:D], R[:, e, b * T:(b + 1) * T], ys[:, e, :],
                                     start=e == 0, stop=e == E - 1)
                last.then_inc(back.full(("x", b)), 1)


def program(nc, a, out):
    ctx = ExitStack()
    with ctx:
        env = Env(nc, ctx)
        phase_load(nc, env, a["x"], a["columns"])
        with ExitStack() as held:
            cross = cross_attention_normed_ahead(nc, held, a["ctx"], a["mask"], a["L0_xattn_Wq"], a["L0_xattn_Wkv"],
                                                 a["L0_xattn_Wout"], a["L0_xattn_bout"])
            phase_self_attention_rope(nc, env, a["L0_attn_w_qkv"], a["L0_attn_w_out"],
                                      a["rope_cos"], a["rope_sin"], cross)
            phase_cross_attention_normed(nc, env, cross)
        phase_kronecker_experts(nc, env, a["router_up"], a["A_up"], a["B_up"], a["router_down"], a["A_down"],
                                a["B_down"], a["bias_up"], a["bias_down"], a["kron_scales"])
        moe = capacity_experts_ahead(nc, ctx, a["wg"], a["w1"], a["w2"], a["b2"], a["ln2_g"], a["ln2_b"],
                                     a["slots"], a["slot_ids"], a["iota8"], a["earlier"])
        with ExitStack() as held:
            mha = attention_over_sequences_ahead(nc, held, a["in_proj_w"], a["out_proj_w"], a["in_proj_b_v"],
                                                 a["out_proj_b"], a["ln1_g"], a["ln1_b"], a["block_bias"])
            with ExitStack() as held_shorter:
                over = cross_attention_queries_ahead(nc, held_shorter, a["ctx"], a["head_mask"], a["L1_xattn_Wq"],
                                                     a["L1_xattn_Wk"], a["L1_xattn_Wv"], a["L1_xattn_Wo"],
                                                     a["L1_xattn_bv"], a["L1_xattn_bo"])
                phase_self_attention_scaled(nc, env, a["head_mask_scaled"], over)
                phase_cross_attention_queries(nc, env, over, mha)
            phase_attention_over_sequences(nc, env, mha, moe)
        phase_capacity_experts(nc, env, out, moe, a["w1"], a["w2"])


def rotary_tables():
    dim = 64
    inv = (1.0 / np.float32(10000.0) ** (np.arange(0, dim, 2, dtype=np.float32) / np.float32(dim))).astype(np.float32)
    f = np.arange(T - 1, dtype=np.float32)[:, None] * inv[None, :]
    cos = np.concatenate([np.ones((1, dim // 2), np.float32), np.cos(f)])
    sin = np.concatenate([np.zeros((1, dim // 2), np.float32), np.sin(f)])
    return np.concatenate([cos, cos], 1), np.concatenate([-sin, sin], 1)


def columns(inputs):
    def by_feature(name):
        return inputs[name].reshape(-1, 128).T

    def twice(name):
        return np.concatenate([inputs[name], inputs[name]]).reshape(128, 1)
    got = {"attn_gamma": by_feature("L0_attn_ln_gamma"), "attn_beta": by_feature("L0_attn_ln_beta"),
           "xattn_x_gamma": by_feature("L0_xattn_ln_x_g"), "xattn_x_beta": by_feature("L0_xattn_ln_x_b"),
           "xattn_l_gamma": by_feature("L0_xattn_ln_l_g"), "xattn_l_beta": by_feature("L0_xattn_ln_l_b"),
           "q_gamma": twice("L0_xattn_qn_g"), "k_gamma": twice("L0_xattn_kn_g"),
           "rotation": by_feature("L1_attn_rotation_params"), "entangle": by_feature("L1_attn_entangle_params"),
           "bq": by_feature("L1_xattn_bq"), "bk": by_feature("L1_xattn_bk"),
           "in_proj_b": by_feature("L1_ffn_in_proj_b"), "b1": by_feature("L1_ffn_b1")}
    return np.ascontiguousarray(np.concatenate([got[name] for name, _ in COLUMNS], axis=1))


def layout(inputs):
    a = {}
    c = np.ascontiguousarray
    a["x"] = c(inputs["x"])
    a["L0_attn_w_qkv"] = c(inputs["L0_attn_w_qkv"])
    a["L0_attn_w_out"] = c(inputs["L0_attn_w_out"])
    a["ctx"] = c(inputs["ctx_1024"])
    a["mask"] = c(inputs["mask_BxS2_bf1"]).view(np.uint8)
    for name in ("L0_xattn_Wq", "L0_xattn_Wkv", "L0_xattn_Wout", "L0_xattn_bout"):
        a[name] = c(inputs[name])
    E = 64
    a["router_up"] = c(inputs["L0_ffn_W_up"].T.reshape(8, 128, E).transpose(1, 0, 2))
    a["router_down"] = c(inputs["L0_ffn_W_down"].reshape(E, 64, 64).transpose(2, 1, 0))
    for name in ("A_up", "B_up", "A_down", "B_down"):
        a[name] = c(inputs[f"L0_ffn_{name}"].transpose(2, 0, 1))
    a["bias_up"] = c(inputs["L0_ffn_bias_up"].reshape(64, 64).T)
    a["bias_down"] = c(inputs["L0_ffn_bias_down"].reshape(32, 32).T)
    a["kron_scales"] = np.concatenate([inputs["L0_ffn_scale_up"], inputs["L0_ffn_scale_down"]])
    a["head_mask"] = (np.arange(128)[:, None] // 16 == np.arange(8)[None, :]).astype(np.float32)
    a["head_mask_scaled"] = np.where(np.arange(128)[:, None] // 16 == np.arange(8)[None, :], 0.25, 0.0)\
        .astype(np.float32)
    for name in ("Wq", "Wk", "Wv"):
        a[f"L1_xattn_{name}"] = c(inputs[f"L1_xattn_{name}"].reshape(D, D).T)
    a["L1_xattn_Wo"] = c(inputs["L1_xattn_Wo"].T)
    a["L1_xattn_bv"] = c(inputs["L1_xattn_bv"].reshape(D))
    a["L1_xattn_bo"] = c(inputs["L1_xattn_bo"])
    a["in_proj_w"] = c(inputs["L1_ffn_in_proj_w"].T)
    a["out_proj_w"] = c(inputs["L1_ffn_out_proj_w"].T)
    a["in_proj_b_v"] = c(inputs["L1_ffn_in_proj_b"][2 * D:])
    for name in ("out_proj_b", "ln1_g", "ln1_b", "ln2_g", "ln2_b", "wg", "w1", "w2", "b2"):
        a[name] = c(inputs[f"L1_ffn_{name}"])
    position = np.arange(128) // B
    a["block_bias"] = np.where(position[:, None] == position[None, :], 0.0, -1e30).astype(np.float32)
    a["slots"] = np.arange(B * T, dtype=np.float32)
    a["slot_ids"] = c(a["slots"].reshape(8, T).T)
    a["iota8"] = np.arange(8, dtype=np.float32)
    a["earlier"] = (np.arange(T)[:, None] < np.arange(T)[None, :]).astype(np.float32)
    a["columns"] = columns(inputs)
    a["rope_cos"], a["rope_sin"] = rotary_tables()
    return a


def kernel(**inputs):
    import concourse.bacc as bacc
    from concourse.bass_utils import run_bass_kernel_spmd

    nc = bacc.Bacc("TRN2", target_bir_lowering=False, num_devices=1)
    arrays = {f"in_{name}": array for name, array in layout(inputs).items()}
    aps = {name[3:]: nc.dram_tensor(name, array.shape, mybir.dt.from_np(array.dtype), kind="ExternalInput").ap()
           for name, array in arrays.items()}
    out = nc.dram_tensor("out_x", (B, T, D), F32, kind="ExternalOutput").ap()
    program(nc, aps, out)
    return run_bass_kernel_spmd(nc, [arrays], core_ids=[0]).results[0]["out_x"]
```
